# Optimizing a Trainium2 kernel written in Bass

```python
import numpy as np
import jax
import jax.numpy as jnp

def _softmax(x, axis=-1):
    return jax.nn.softmax(x, axis=axis)

def _gelu(x):
    return jax.nn.gelu(x, approximate=True)

def _silu(x):
    return jax.nn.silu(x)

def _sigmoid(x):
    return jax.nn.sigmoid(x)

def _layernorm(x, axis=-1, eps=1e-05):
    m = jnp.mean(x, axis=axis, keepdims=True)
    v = jnp.var(x, axis=axis, keepdims=True)
    return (x - m) / jnp.sqrt(v + eps)

def _scatter_add(tgt, idx, src, axis=0):
    return tgt.at[idx].add(src)

def _segment_sum(src, seg, n):
    return jax.ops.segment_sum(src, seg, n)
kernel_name = 'mk_flamingo_gated_d4_seqx_r8_1bf298'

def setup_inputs(seed: int=0):
    np.random.seed(seed)
    _w = jnp.asarray

    def _rec_inputs():
        import jax
        import jax.numpy as jnp
        _rk = jax.random.key(seed)
        x = -0.0002928 + 1 * jax.random.normal(jax.random.fold_in(_rk, 1), (1, 1024, 128), jnp.float32)
        _lenS = 1024 - jax.random.randint(jax.random.fold_in(_rk, 7), (1,), 0, max(1, 1024 // 4) + 1, jnp.int32)
        _lenS2 = 6404 - jax.random.randint(jax.random.fold_in(_rk, 8), (1,), 0, max(1, 6404 // 4) + 1, jnp.int32)
        _ctx_1024P = jax.random.normal(jax.random.fold_in(_rk, 11), (1, 16, 128), jnp.float32)
        _ctx_1024c = jax.random.dirichlet(jax.random.fold_in(_rk, 511), 0.3 * jnp.ones((16,), jnp.float32), (1, 6404))
        _ctx_1024t = jnp.einsum('bsk,bkd->bsd', _ctx_1024c, _ctx_1024P)
        _ctx_1024t = _ctx_1024t * jax.lax.rsqrt(jnp.mean(jnp.square(_ctx_1024t)) + 1e-12) * 0.953939
        ctx_1024 = -1.39393e-06 + 0.999914 * (_ctx_1024t + 0.3 * jax.random.normal(jax.random.fold_in(_rk, 611), (1, 6404, 128), jnp.float32))
        _validS = jnp.arange(1024)[None, :] < _lenS[:, None]
        _validS2 = jnp.arange(6404)[None, :] < _lenS2[:, None]
        _causal = jnp.tril(jnp.ones((1024, 1024), dtype=bool))
        mask_Bx1xS2_bf1 = jnp.ones((1, 1, 6404), dtype=bool)
        _g = jax.random.normal(jax.random.fold_in(_rk, 9001), (2, 4), jnp.float32)
        _g = jnp.sign(_g) * jnp.maximum(jnp.abs(_g), 1.0) + (_g == 0) * 1.0
        g_xattn = _g[0]
        g_ffn = _g[1]
        return (x, ctx_1024, mask_Bx1xS2_bf1, g_xattn, g_ffn)
    x, ctx_1024, mask_Bx1xS2_bf1, g_xattn, g_ffn = _rec_inputs()

    def _L0_xattn_setup():
        import jax, jax.numpy as jnp
        import numpy as np
        NDIM = 128
        NHEAD = 16
        HEAD_DIM = NDIM // NHEAD
        key = jax.random.key(seed)
        ks = jax.random.split(key, 12)
        B, L, C = (2, 256, NDIM)
        s = 0.02
        return {'q': jax.random.normal(ks[0], (B, L, C), jnp.float32), 'k': jax.random.normal(ks[1], (B, L, C), jnp.float32), 'v': jax.random.normal(ks[2], (B, L, C), jnp.float32), 'Wq': jax.random.normal(ks[3], (C, C), jnp.float32) * s, 'bq': jax.random.normal(ks[4], (C,), jnp.float32) * s, 'Wk': jax.random.normal(ks[5], (C, C), jnp.float32) * s, 'bk': jax.random.normal(ks[6], (C,), jnp.float32) * s, 'Wv': jax.random.normal(ks[7], (C, C), jnp.float32) * s, 'bv': jax.random.normal(ks[8], (C,), jnp.float32) * s, 'Wo': jax.random.normal(ks[9], (C, C), jnp.float32) * s, 'bo': jax.random.normal(ks[10], (C,), jnp.float32) * s}
    _L0_xattn_all = _L0_xattn_setup()
    _L0_xattn_in = {k: v for k, v in _L0_xattn_all.items() if k in ('Wq', 'bq', 'Wk', 'bk', 'Wv', 'bv', 'Wo', 'bo')}
    del _L0_xattn_all

    def _L0_ffn_setup():
        import jax, jax.numpy as jnp
        import numpy as np
        LATENT = 128
        LEAF_W = 64
        DEPTH = 4
        N_LEAVES = 2 ** DEPTH
        N_NODES = 2 ** DEPTH - 1
        B, S = (4, 256)

        def _fff_params(key, prefix):
            ks = jax.random.split(key, 4)
            d, h, l, n = (LATENT, LEAF_W, N_LEAVES, N_NODES)
            s_in = 1.0 / np.sqrt(d).astype(np.float32)
            s_h = 1.0 / np.sqrt(h).astype(np.float32)
            return {f'{prefix}_node_w': jax.random.normal(ks[0], (n, d), jnp.float32) * s_in, f'{prefix}_node_b': jax.random.normal(ks[1], (n,), jnp.float32) * s_in, f'{prefix}_w1': jax.random.normal(ks[2], (l, d, h), jnp.float32) * s_in, f'{prefix}_b1': jnp.zeros((l, h), jnp.float32), f'{prefix}_w2': jax.random.normal(ks[3], (l, h, d), jnp.float32) * s_h, f'{prefix}_b2': jnp.zeros((l, d), jnp.float32)}

        def _fff(x, node_w, node_b, w1, b1, w2, b2):
            Bx, Sx, D = x.shape
            xf = x.reshape(-1, D)
            N = xf.shape[0]
            cur = jnp.zeros((N,), jnp.int32)
            for _ in range(DEPTH):
                pw = node_w[cur]
                score = jnp.einsum('nd,nd->n', xf, pw) + node_b[cur]
                cur = 2 * cur + 1 + (score >= 0).astype(jnp.int32)
            leaf = cur - N_NODES
            sel = jax.nn.one_hot(leaf, N_LEAVES, dtype=xf.dtype)
            hidden_all = jax.nn.relu(jnp.einsum('nd,ldh->lnh', xf, w1) + b1[:, None, :])
            hidden = hidden_all * sel.T[:, :, None]
            out = jnp.einsum('lnh,lho->no', hidden, w2) + sel @ b2
            return out.reshape(Bx, Sx, D)
        key = jax.random.key(seed)
        kx, kq, kk, kv = jax.random.split(key, 4)
        inp = {'x': jax.random.normal(kx, (B, S, LATENT), jnp.float32)}
        inp.update(_fff_params(kq, 'q'))
        inp.update(_fff_params(kk, 'k'))
        inp.update(_fff_params(kv, 'v'))
        return inp
    _L0_ffn_all = _L0_ffn_setup()
    _L0_ffn_in = {k: v for k, v in _L0_ffn_all.items() if k in ('q_node_w', 'q_node_b', 'q_w1', 'q_b1', 'q_w2', 'q_b2', 'k_node_w', 'k_node_b', 'k_w1', 'k_b1', 'k_w2', 'k_b2', 'v_node_w', 'v_node_b', 'v_w1', 'v_b1', 'v_w2', 'v_b2')}
    del _L0_ffn_all

    def _L1_xattn_setup():
        import jax, jax.numpy as jnp
        import numpy as np
        HEADS = 16
        key = jax.random.key(seed)
        ks = jax.random.split(key, 6)
        b, n, m, dim = (2, 256, 64, 128)
        s = dim ** (-0.5)
        return {'x': jax.random.normal(ks[0], (b, n, dim), jnp.float32), 'mem': jax.random.normal(ks[1], (b, m, dim), jnp.float32), 'Wq': jax.random.normal(ks[2], (dim, dim), jnp.float32) * s, 'Wkv': jax.random.normal(ks[3], (dim, 2 * dim), jnp.float32) * s, 'Wout': jax.random.normal(ks[4], (dim, dim), jnp.float32) * s, 'bout': jnp.zeros((dim,), jnp.float32)}
    _L1_xattn_all = _L1_xattn_setup()
    _L1_xattn_in = {k: v for k, v in _L1_xattn_all.items() if k in ('Wq', 'Wkv', 'Wout', 'bout')}
    del _L1_xattn_all

    def _L1_ffn_setup():
        import jax, jax.numpy as jnp
        import numpy as np
        D_MODEL = 128
        HIDDEN = 256
        E_ROUTED = 14
        E_SHARED = 2
        TOP_K = 2
        EPS = 1e-09
        RMS_EPS = 1.1920929e-07

        def _ffn(xn, rw, W1, W2):
            ms = jnp.mean(xn * xn, axis=-1, keepdims=True)
            h = xn * jax.lax.rsqrt(ms + RMS_EPS) * rw
            return jax.nn.silu(h @ W1) @ W2
        key = jax.random.key(seed)
        ks = jax.random.split(key, 9)
        B, T = (2, 128)
        x = jax.random.normal(ks[0], (B, T, D_MODEL), dtype=jnp.float32)
        router_w = jax.random.normal(ks[1], (D_MODEL, E_ROUTED), dtype=jnp.float32) * 0.006
        rms_w = jnp.ones((E_ROUTED, D_MODEL), dtype=jnp.float32)
        w1 = jax.random.normal(ks[2], (E_ROUTED, D_MODEL, HIDDEN), dtype=jnp.float32) * 0.02
        w2 = jax.random.normal(ks[3], (E_ROUTED, HIDDEN, D_MODEL), dtype=jnp.float32) * 0.02
        rms_w_s = jnp.ones((E_SHARED, D_MODEL), dtype=jnp.float32)
        w1_s = jax.random.normal(ks[4], (E_SHARED, D_MODEL, HIDDEN), dtype=jnp.float32) * 0.02
        w2_s = jax.random.normal(ks[5], (E_SHARED, HIDDEN, D_MODEL), dtype=jnp.float32) * 0.02
        return {'x': x, 'router_w': router_w, 'rms_w': rms_w, 'w1': w1, 'w2': w2, 'rms_w_s': rms_w_s, 'w1_s': w1_s, 'w2_s': w2_s}
    _L1_ffn_all = _L1_ffn_setup()
    _L1_ffn_in = {k: v for k, v in _L1_ffn_all.items() if k in ('router_w', 'rms_w', 'w1', 'w2', 'rms_w_s', 'w1_s', 'w2_s')}
    del _L1_ffn_all

    def _L2_xattn_setup():
        import jax, jax.numpy as jnp
        import numpy as np
        D_MODEL = 128
        N_HEADS = 16
        D_HEAD = D_MODEL // N_HEADS
        LN_EPS = 1e-05

        def layer_norm(x, gamma, beta):
            mu = jnp.mean(x, axis=-1, keepdims=True)
            var = jnp.mean(jnp.square(x - mu), axis=-1, keepdims=True)
            return (x - mu) * jax.lax.rsqrt(var + LN_EPS) * gamma + beta
        key = jax.random.key(seed)
        ks = jax.random.split(key, 8)
        B, T = (4, 256)
        s = 1.0 / np.sqrt(D_MODEL)
        return {'encoder_seq': jax.random.normal(ks[0], (B, T, D_MODEL), jnp.float32), 'decoder_seq': jax.random.normal(ks[1], (B, T, D_MODEL), jnp.float32), 'Wq': jax.random.normal(ks[2], (D_MODEL, D_MODEL), jnp.float32) * s, 'bq': jnp.zeros((D_MODEL,), jnp.float32), 'Wk': jax.random.normal(ks[3], (D_MODEL, D_MODEL), jnp.float32) * s, 'bk': jnp.zeros((D_MODEL,), jnp.float32), 'Wv': jax.random.normal(ks[4], (D_MODEL, D_MODEL), jnp.float32) * s, 'bv': jnp.zeros((D_MODEL,), jnp.float32), 'ln_gamma': jnp.ones((D_MODEL,), jnp.float32), 'ln_beta': jnp.zeros((D_MODEL,), jnp.float32)}
    _L2_xattn_all = _L2_xattn_setup()
    _L2_xattn_in = {k: v for k, v in _L2_xattn_all.items() if k in ('Wq', 'bq', 'Wk', 'bk', 'Wv', 'bv', 'ln_gamma', 'ln_beta')}
    del _L2_xattn_all

    def _L2_ffn_setup():
        import jax, jax.numpy as jnp
        import numpy as np
        NUM_EXPERTS = 8
        HIDDEN = 128
        FFN = 512
        BATCH = 2
        SEQ = 256
        key = jax.random.key(seed)
        k_x, k_g, k_u, k_d = jax.random.split(key, 4)
        scale_in = 1.0 / np.sqrt(HIDDEN)
        scale_mid = 1.0 / np.sqrt(FFN)
        return {'hidden_states': jax.random.normal(k_x, (BATCH, SEQ, HIDDEN), dtype=jnp.float32), 'Wg': jax.random.normal(k_g, (NUM_EXPERTS, HIDDEN, FFN), dtype=jnp.float32) * scale_in, 'Wu': jax.random.normal(k_u, (NUM_EXPERTS, HIDDEN, FFN), dtype=jnp.float32) * scale_in, 'Wd': jax.random.normal(k_d, (NUM_EXPERTS, FFN, HIDDEN), dtype=jnp.float32) * scale_mid}
    _L2_ffn_all = _L2_ffn_setup()
    _L2_ffn_in = {k: v for k, v in _L2_ffn_all.items() if k in ('Wg', 'Wu', 'Wd')}
    del _L2_ffn_all

    def _L3_xattn_setup():
        import jax, jax.numpy as jnp
        import numpy as np
        B, S, D, H = (4, 256, 128, 16)
        HD = D // H
        key = jax.random.key(seed)
        ks = jax.random.split(key, 12)
        inp = {'k': jax.random.normal(ks[0], (B, S, D), jnp.float32), 'v': jax.random.normal(ks[1], (B, S, D), jnp.float32), 'q': jax.random.normal(ks[2], (B, S, D), jnp.float32), 'mask': jnp.ones((B, 1, S), dtype=bool), 'Wq': jax.random.normal(ks[3], (D, D), jnp.float32) / np.sqrt(D), 'bq': jax.random.normal(ks[4], (D,), jnp.float32) * 0.01, 'Wk': jax.random.normal(ks[5], (D, D), jnp.float32) / np.sqrt(D), 'bk': jax.random.normal(ks[6], (D,), jnp.float32) * 0.01, 'Wv': jax.random.normal(ks[7], (D, D), jnp.float32) / np.sqrt(D), 'bv': jax.random.normal(ks[8], (D,), jnp.float32) * 0.01, 'Wo': jax.random.normal(ks[9], (D, D), jnp.float32) / np.sqrt(D), 'bo': jax.random.normal(ks[10], (D,), jnp.float32) * 0.01}
        return inp
    _L3_xattn_all = _L3_xattn_setup()
    _L3_xattn_in = {k: v for k, v in _L3_xattn_all.items() if k in ('Wq', 'bq', 'Wk', 'bk', 'Wv', 'bv', 'Wo', 'bo')}
    del _L3_xattn_all

    def _L3_ffn_setup():
        import jax, jax.numpy as jnp
        import numpy as np
        NUM_EXPERTS = 8
        NUM_SELECTED = 2
        EXPERT_CAPACITY = 64
        NUM_GROUPS = 8

        def _routing(xg, w_router):
            G, T, H = xg.shape
            logits = jnp.einsum('gth,he->gte', xg, w_router)
            probs = jax.nn.softmax(logits, axis=-1)
            _gate, idx = jax.lax.top_k(probs, NUM_SELECTED)
            idx_kt = jnp.swapaxes(idx, 1, 2).reshape(G, -1)
            expert_mask = jax.nn.one_hot(idx_kt, NUM_EXPERTS, dtype=jnp.int32)
            priority = jnp.cumsum(expert_mask, axis=1) * expert_mask - 1
            priority = priority.reshape(G, NUM_SELECTED, T, NUM_EXPERTS)
            priority = jnp.swapaxes(priority, 1, 2).max(axis=2)
            dispatch = jax.nn.one_hot(priority, EXPERT_CAPACITY, dtype=xg.dtype)
            combine = probs[..., None] * dispatch
            return (dispatch, combine)
        key = jax.random.key(seed)
        k1, k2, k3, k4 = jax.random.split(key, 4)
        B, S, H, F = (8, 256, 128, 512)
        return {'x': jax.random.normal(k1, (B, S, H), jnp.float32), 'w_router': jax.random.normal(k2, (H, NUM_EXPERTS), jnp.float32) * 0.02, 'wi': jax.random.normal(k3, (NUM_EXPERTS, H, F), jnp.float32) * 0.02, 'wo': jax.random.normal(k4, (NUM_EXPERTS, F, H), jnp.float32) * 0.02}
    _L3_ffn_all = _L3_ffn_setup()
    _L3_ffn_in = {k: v for k, v in _L3_ffn_all.items() if k in ('w_router', 'wi', 'wo')}
    del _L3_ffn_all
    return {'x': x, 'ctx_1024': ctx_1024, 'mask_Bx1xS2_bf1': mask_Bx1xS2_bf1, 'g_xattn': g_xattn, 'g_ffn': g_ffn, 'L0_xattn_Wq': _L0_xattn_in['Wq'], 'L0_xattn_bq': _L0_xattn_in['bq'], 'L0_xattn_Wk': _L0_xattn_in['Wk'], 'L0_xattn_bk': _L0_xattn_in['bk'], 'L0_xattn_Wv': _L0_xattn_in['Wv'], 'L0_xattn_bv': _L0_xattn_in['bv'], 'L0_xattn_Wo': _L0_xattn_in['Wo'], 'L0_xattn_bo': _L0_xattn_in['bo'], 'L0_ffn_q_node_w': _L0_ffn_in['q_node_w'], 'L0_ffn_q_node_b': _L0_ffn_in['q_node_b'], 'L0_ffn_q_w1': _L0_ffn_in['q_w1'], 'L0_ffn_q_b1': _L0_ffn_in['q_b1'], 'L0_ffn_q_w2': _L0_ffn_in['q_w2'], 'L0_ffn_q_b2': _L0_ffn_in['q_b2'], 'L0_ffn_k_node_w': _L0_ffn_in['k_node_w'], 'L0_ffn_k_node_b': _L0_ffn_in['k_node_b'], 'L0_ffn_k_w1': _L0_ffn_in['k_w1'], 'L0_ffn_k_b1': _L0_ffn_in['k_b1'], 'L0_ffn_k_w2': _L0_ffn_in['k_w2'], 'L0_ffn_k_b2': _L0_ffn_in['k_b2'], 'L0_ffn_v_node_w': _L0_ffn_in['v_node_w'], 'L0_ffn_v_node_b': _L0_ffn_in['v_node_b'], 'L0_ffn_v_w1': _L0_ffn_in['v_w1'], 'L0_ffn_v_b1': _L0_ffn_in['v_b1'], 'L0_ffn_v_w2': _L0_ffn_in['v_w2'], 'L0_ffn_v_b2': _L0_ffn_in['v_b2'], 'L1_xattn_Wq': _L1_xattn_in['Wq'], 'L1_xattn_Wkv': _L1_xattn_in['Wkv'], 'L1_xattn_Wout': _L1_xattn_in['Wout'], 'L1_xattn_bout': _L1_xattn_in['bout'], 'L1_ffn_router_w': _L1_ffn_in['router_w'], 'L1_ffn_rms_w': _L1_ffn_in['rms_w'], 'L1_ffn_w1': _L1_ffn_in['w1'], 'L1_ffn_w2': _L1_ffn_in['w2'], 'L1_ffn_rms_w_s': _L1_ffn_in['rms_w_s'], 'L1_ffn_w1_s': _L1_ffn_in['w1_s'], 'L1_ffn_w2_s': _L1_ffn_in['w2_s'], 'L2_xattn_Wq': _L2_xattn_in['Wq'], 'L2_xattn_bq': _L2_xattn_in['bq'], 'L2_xattn_Wk': _L2_xattn_in['Wk'], 'L2_xattn_bk': _L2_xattn_in['bk'], 'L2_xattn_Wv': _L2_xattn_in['Wv'], 'L2_xattn_bv': _L2_xattn_in['bv'], 'L2_xattn_ln_gamma': _L2_xattn_in['ln_gamma'], 'L2_xattn_ln_beta': _L2_xattn_in['ln_beta'], 'L2_ffn_Wg': _L2_ffn_in['Wg'], 'L2_ffn_Wu': _L2_ffn_in['Wu'], 'L2_ffn_Wd': _L2_ffn_in['Wd'], 'L3_xattn_Wq': _L3_xattn_in['Wq'], 'L3_xattn_bq': _L3_xattn_in['bq'], 'L3_xattn_Wk': _L3_xattn_in['Wk'], 'L3_xattn_bk': _L3_xattn_in['bk'], 'L3_xattn_Wv': _L3_xattn_in['Wv'], 'L3_xattn_bv': _L3_xattn_in['bv'], 'L3_xattn_Wo': _L3_xattn_in['Wo'], 'L3_xattn_bo': _L3_xattn_in['bo'], 'L3_ffn_w_router': _L3_ffn_in['w_router'], 'L3_ffn_wi': _L3_ffn_in['wi'], 'L3_ffn_wo': _L3_ffn_in['wo']}

def reference(x, ctx_1024, mask_Bx1xS2_bf1, g_xattn, g_ffn, L0_xattn_Wq, L0_xattn_bq, L0_xattn_Wk, L0_xattn_bk, L0_xattn_Wv, L0_xattn_bv, L0_xattn_Wo, L0_xattn_bo, L0_ffn_q_node_w, L0_ffn_q_node_b, L0_ffn_q_w1, L0_ffn_q_b1, L0_ffn_q_w2, L0_ffn_q_b2, L0_ffn_k_node_w, L0_ffn_k_node_b, L0_ffn_k_w1, L0_ffn_k_b1, L0_ffn_k_w2, L0_ffn_k_b2, L0_ffn_v_node_w, L0_ffn_v_node_b, L0_ffn_v_w1, L0_ffn_v_b1, L0_ffn_v_w2, L0_ffn_v_b2, L1_xattn_Wq, L1_xattn_Wkv, L1_xattn_Wout, L1_xattn_bout, L1_ffn_router_w, L1_ffn_rms_w, L1_ffn_w1, L1_ffn_w2, L1_ffn_rms_w_s, L1_ffn_w1_s, L1_ffn_w2_s, L2_xattn_Wq, L2_xattn_bq, L2_xattn_Wk, L2_xattn_bk, L2_xattn_Wv, L2_xattn_bv, L2_xattn_ln_gamma, L2_xattn_ln_beta, L2_ffn_Wg, L2_ffn_Wu, L2_ffn_Wd, L3_xattn_Wq, L3_xattn_bq, L3_xattn_Wk, L3_xattn_bk, L3_xattn_Wv, L3_xattn_bv, L3_xattn_Wo, L3_xattn_bo, L3_ffn_w_router, L3_ffn_wi, L3_ffn_wo):
    import jax
    import jax.numpy as jnp

    def _L0_xattn_ref(q, k, v, Wq, bq, Wk, bk, Wv, bv, Wo, bo):
        import jax, jax.numpy as jnp
        import numpy as np
        NDIM = 128
        NHEAD = 16
        HEAD_DIM = NDIM // NHEAD
        B, Lq, C = q.shape
        H, D = (NHEAD, HEAD_DIM)
        qh = (q @ Wq + bq).reshape(B, Lq, H, D).transpose(0, 2, 1, 3)
        kh = (k @ Wk + bk).reshape(B, k.shape[1], H, D).transpose(0, 2, 1, 3)
        vh = (v @ Wv + bv).reshape(B, v.shape[1], H, D).transpose(0, 2, 1, 3)
        scale = 1.0 / jnp.sqrt(jnp.asarray(D, qh.dtype))
        att = jnp.einsum('bhqd,bhkd->bhqk', qh, kh) * scale
        att = jax.nn.softmax(att, axis=-1)
        y = jnp.einsum('bhqk,bhkd->bhqd', att, vh)
        y = y.transpose(0, 2, 1, 3).reshape(B, Lq, C)
        return y @ Wo + bo

    def _L0_ffn_ref(x, q_node_w, q_node_b, q_w1, q_b1, q_w2, q_b2, k_node_w, k_node_b, k_w1, k_b1, k_w2, k_b2, v_node_w, v_node_b, v_w1, v_b1, v_w2, v_b2):
        import jax, jax.numpy as jnp
        import numpy as np
        LATENT = 128
        LEAF_W = 64
        DEPTH = 4
        N_LEAVES = 2 ** DEPTH
        N_NODES = 2 ** DEPTH - 1
        B, S = (4, 256)

        def _fff_params(key, prefix):
            ks = jax.random.split(key, 4)
            d, h, l, n = (LATENT, LEAF_W, N_LEAVES, N_NODES)
            s_in = 1.0 / np.sqrt(d).astype(np.float32)
            s_h = 1.0 / np.sqrt(h).astype(np.float32)
            return {f'{prefix}_node_w': jax.random.normal(ks[0], (n, d), jnp.float32) * s_in, f'{prefix}_node_b': jax.random.normal(ks[1], (n,), jnp.float32) * s_in, f'{prefix}_w1': jax.random.normal(ks[2], (l, d, h), jnp.float32) * s_in, f'{prefix}_b1': jnp.zeros((l, h), jnp.float32), f'{prefix}_w2': jax.random.normal(ks[3], (l, h, d), jnp.float32) * s_h, f'{prefix}_b2': jnp.zeros((l, d), jnp.float32)}

        def _fff(x, node_w, node_b, w1, b1, w2, b2):
            Bx, Sx, D = x.shape
            xf = x.reshape(-1, D)
            N = xf.shape[0]
            cur = jnp.zeros((N,), jnp.int32)
            for _ in range(DEPTH):
                pw = node_w[cur]
                score = jnp.einsum('nd,nd->n', xf, pw) + node_b[cur]
                cur = 2 * cur + 1 + (score >= 0).astype(jnp.int32)
            leaf = cur - N_NODES
            sel = jax.nn.one_hot(leaf, N_LEAVES, dtype=xf.dtype)
            hidden_all = jax.nn.relu(jnp.einsum('nd,ldh->lnh', xf, w1) + b1[:, None, :])
            hidden = hidden_all * sel.T[:, :, None]
            out = jnp.einsum('lnh,lho->no', hidden, w2) + sel @ b2
            return out.reshape(Bx, Sx, D)
        q = _fff(x, q_node_w, q_node_b, q_w1, q_b1, q_w2, q_b2)
        k = _fff(x, k_node_w, k_node_b, k_w1, k_b1, k_w2, k_b2)
        v = _fff(x, v_node_w, v_node_b, v_w1, v_b1, v_w2, v_b2)
        scale = 1.0 / np.sqrt(LATENT).astype(np.float32)
        attn = jax.nn.softmax(jnp.einsum('bqd,bkd->bqk', q, k) * scale, axis=-1)
        return jnp.einsum('bqk,bkd->bqd', attn, v)

    def _L1_xattn_ref(x, mem, Wq, Wkv, Wout, bout):
        import jax, jax.numpy as jnp
        import numpy as np
        HEADS = 16
        b, n, dim = x.shape
        h = HEADS
        d = dim // h
        scale = d ** (-0.5)
        mem_len = mem.shape[1]
        q = x @ Wq
        xc = jnp.concatenate((mem, x), axis=1)
        kv = xc @ Wkv
        k, v = jnp.split(kv, 2, axis=-1)

        def to_heads(t):
            bb, nn, _ = t.shape
            return t.reshape(bb, nn, h, d).transpose(0, 2, 1, 3)
        q, k, v = (to_heads(q), to_heads(k), to_heads(v))
        dots = jnp.einsum('bhid,bhjd->bhij', q, k) * scale
        j = dots.shape[-1]
        i_idx = jnp.arange(n)[:, None]
        j_idx = jnp.arange(j)[None, :]
        mask = j_idx > i_idx + mem_len
        dots = jnp.where(mask[None, None], -jnp.inf, dots)
        attn = jax.nn.softmax(dots, axis=-1)
        out = jnp.einsum('bhij,bhjd->bhid', attn, v)
        out = out.transpose(0, 2, 1, 3).reshape(b, n, dim)
        return out @ Wout + bout

    def _L1_ffn_ref(x, router_w, rms_w, w1, w2, rms_w_s, w1_s, w2_s):
        import jax, jax.numpy as jnp
        import numpy as np
        D_MODEL = 128
        HIDDEN = 256
        E_ROUTED = 14
        E_SHARED = 2
        TOP_K = 2
        EPS = 1e-09
        RMS_EPS = 1.1920929e-07

        def _ffn(xn, rw, W1, W2):
            ms = jnp.mean(xn * xn, axis=-1, keepdims=True)
            h = xn * jax.lax.rsqrt(ms + RMS_EPS) * rw
            return jax.nn.silu(h @ W1) @ W2
        B, T, D = x.shape
        N = B * T
        xf = x.reshape(N, D)
        gates = jax.nn.softmax(xf @ router_w, axis=-1)
        top_v, top_i = jax.lax.top_k(gates, TOP_K)
        masked = jnp.zeros_like(gates).at[jnp.arange(N)[:, None], top_i].set(top_v)
        masked = masked / (masked.sum(axis=-1, keepdims=True) + EPS)
        routed = jax.vmap(lambda rw_, W1_, W2_: _ffn(xf, rw_, W1_, W2_))(rms_w, w1, w2)
        routed_out = jnp.einsum('end,ne->nd', routed, masked)
        shared = jax.vmap(lambda rw_, W1_, W2_: _ffn(xf, rw_, W1_, W2_))(rms_w_s, w1_s, w2_s).sum(0)
        return (routed_out + shared).reshape(B, T, D)

    def _L2_xattn_ref(encoder_seq, decoder_seq, Wq, bq, Wk, bk, Wv, bv, ln_gamma, ln_beta):
        import jax, jax.numpy as jnp
        import numpy as np
        D_MODEL = 128
        N_HEADS = 16
        D_HEAD = D_MODEL // N_HEADS
        LN_EPS = 1e-05

        def layer_norm(x, gamma, beta):
            mu = jnp.mean(x, axis=-1, keepdims=True)
            var = jnp.mean(jnp.square(x - mu), axis=-1, keepdims=True)
            return (x - mu) * jax.lax.rsqrt(var + LN_EPS) * gamma + beta
        B, T_dec, _ = decoder_seq.shape
        T_enc = encoder_seq.shape[1]
        q = (decoder_seq @ Wq.T + bq).reshape(B, T_dec, N_HEADS, D_HEAD)
        k = (encoder_seq @ Wk.T + bk).reshape(B, T_enc, N_HEADS, D_HEAD)
        v = (encoder_seq @ Wv.T + bv).reshape(B, T_enc, N_HEADS, D_HEAD)
        scale = 1.0 / np.sqrt(D_HEAD)
        kv = jnp.einsum('bthd,bthe->bhde', k, v)
        att = jnp.einsum('bqhd,bhde->bqhe', q, kv) * scale
        att = att.reshape(B, T_dec, D_MODEL)
        return layer_norm(att + decoder_seq, ln_gamma, ln_beta)

    def _L2_ffn_ref(hidden_states, Wg, Wu, Wd):
        import jax, jax.numpy as jnp
        import numpy as np
        NUM_EXPERTS = 8
        HIDDEN = 128
        FFN = 512
        BATCH = 2
        SEQ = 256
        B, S, H = hidden_states.shape
        x = hidden_states.reshape(-1, H)

        def expert_step(acc, w):
            wg, wu, wd = w
            h = jax.nn.silu(x @ wg) * (x @ wu)
            return (acc + h @ wd, None)
        acc, _ = jax.lax.scan(expert_step, jnp.zeros_like(x), (Wg, Wu, Wd))
        return acc.reshape(B, S, H)

    def _L3_xattn_ref(k, v, q, mask, Wq, bq, Wk, bk, Wv, bv, Wo, bo):
        import jax, jax.numpy as jnp
        import numpy as np
        B, S, D, H = (4, 256, 128, 16)
        HD = D // H
        b = q.shape[0]

        def split_heads(x):
            return x.reshape(b, -1, H, HD).transpose(0, 2, 1, 3)
        qh = split_heads(q @ Wq + bq) / jnp.sqrt(jnp.asarray(HD, q.dtype))
        kh = split_heads(k @ Wk + bk)
        vh = split_heads(v @ Wv + bv)
        scores = jnp.einsum('bhqd,bhkd->bhqk', qh, kh)
        if mask is not None:
            scores = jnp.where(mask[:, None, :, :], scores, jnp.asarray(-jnp.inf, scores.dtype))
        attn = jax.nn.softmax(scores, axis=-1)
        ctx = jnp.einsum('bhqk,bhkd->bhqd', attn, vh)
        ctx = ctx.transpose(0, 2, 1, 3).reshape(b, -1, H * HD)
        out = ctx @ Wo + bo
        return out

    def _L3_ffn_ref(x, w_router, wi, wo):
        import jax, jax.numpy as jnp
        import numpy as np
        NUM_EXPERTS = 8
        NUM_SELECTED = 2
        EXPERT_CAPACITY = 64
        NUM_GROUPS = 8

        def _routing(xg, w_router):
            G, T, H = xg.shape
            logits = jnp.einsum('gth,he->gte', xg, w_router)
            probs = jax.nn.softmax(logits, axis=-1)
            _gate, idx = jax.lax.top_k(probs, NUM_SELECTED)
            idx_kt = jnp.swapaxes(idx, 1, 2).reshape(G, -1)
            expert_mask = jax.nn.one_hot(idx_kt, NUM_EXPERTS, dtype=jnp.int32)
            priority = jnp.cumsum(expert_mask, axis=1) * expert_mask - 1
            priority = priority.reshape(G, NUM_SELECTED, T, NUM_EXPERTS)
            priority = jnp.swapaxes(priority, 1, 2).max(axis=2)
            dispatch = jax.nn.one_hot(priority, EXPERT_CAPACITY, dtype=xg.dtype)
            combine = probs[..., None] * dispatch
            return (dispatch, combine)
        B, S, H = x.shape
        T = B * S // NUM_GROUPS
        xg = x.reshape(NUM_GROUPS, T, H)
        dispatch, combine = _routing(xg, w_router)
        expert_in = jnp.einsum('gth,gtec->gech', xg, dispatch)
        h = jax.nn.gelu(jnp.einsum('gech,ehf->gecf', expert_in, wi))
        expert_out = jnp.einsum('gecf,efh->gech', h, wo)
        out = jnp.einsum('gech,gtec->gth', expert_out, combine)
        return out.reshape(B, S, H)
    x = x + jnp.tanh(g_xattn[0]) * _L0_xattn_ref(_layernorm(x, axis=-1), ctx_1024, ctx_1024, L0_xattn_Wq, L0_xattn_bq, L0_xattn_Wk, L0_xattn_bk, L0_xattn_Wv, L0_xattn_bv, L0_xattn_Wo, L0_xattn_bo)
    x = x + jnp.tanh(g_ffn[0]) * _L0_ffn_ref(_layernorm(x, axis=-1), L0_ffn_q_node_w, L0_ffn_q_node_b, L0_ffn_q_w1, L0_ffn_q_b1, L0_ffn_q_w2, L0_ffn_q_b2, L0_ffn_k_node_w, L0_ffn_k_node_b, L0_ffn_k_w1, L0_ffn_k_b1, L0_ffn_k_w2, L0_ffn_k_b2, L0_ffn_v_node_w, L0_ffn_v_node_b, L0_ffn_v_w1, L0_ffn_v_b1, L0_ffn_v_w2, L0_ffn_v_b2)
    x = x + jnp.tanh(g_xattn[1]) * _L1_xattn_ref(_layernorm(x, axis=-1), ctx_1024, L1_xattn_Wq, L1_xattn_Wkv, L1_xattn_Wout, L1_xattn_bout)
    x = x + jnp.tanh(g_ffn[1]) * _L1_ffn_ref(_layernorm(x, axis=-1), L1_ffn_router_w, L1_ffn_rms_w, L1_ffn_w1, L1_ffn_w2, L1_ffn_rms_w_s, L1_ffn_w1_s, L1_ffn_w2_s)
    x = x + jnp.tanh(g_xattn[2]) * _L2_xattn_ref(ctx_1024, _layernorm(x, axis=-1), L2_xattn_Wq, L2_xattn_bq, L2_xattn_Wk, L2_xattn_bk, L2_xattn_Wv, L2_xattn_bv, L2_xattn_ln_gamma, L2_xattn_ln_beta)
    x = x + jnp.tanh(g_ffn[2]) * _L2_ffn_ref(_layernorm(x, axis=-1), L2_ffn_Wg, L2_ffn_Wu, L2_ffn_Wd)
    x = x + jnp.tanh(g_xattn[3]) * _L3_xattn_ref(ctx_1024, ctx_1024, _layernorm(x, axis=-1), mask_Bx1xS2_bf1, L3_xattn_Wq, L3_xattn_bq, L3_xattn_Wk, L3_xattn_bk, L3_xattn_Wv, L3_xattn_bv, L3_xattn_Wo, L3_xattn_bo)
    x = x + jnp.tanh(g_ffn[3]) * _L3_ffn_ref(_layernorm(x, axis=-1), L3_ffn_w_router, L3_ffn_wi, L3_ffn_wo)
    return x

_drawn_inputs = setup_inputs


def setup_inputs(seed=0):
    import zlib

    import numpy as np

    out = dict(_drawn_inputs(seed))
    spreads = {'L0_ffn_q_b1': (0.0, 0.8),
     'L0_ffn_q_b2': (0.0, 0.8),
     'L0_ffn_k_b1': (0.0, 0.8),
     'L0_ffn_k_b2': (0.0, 0.8),
     'L0_ffn_v_b1': (0.0, 0.756),
     'L0_ffn_v_b2': (0.0, 0.365),
     'L1_xattn_bout': (0.0, 0.1),
     'L1_ffn_rms_w': (1.0, 0.6),
     'L1_ffn_rms_w_s': (1.0, 0.6),
     'L2_xattn_bq': (0.0, 0.1),
     'L2_xattn_bk': (0.0, 0.1),
     'L2_xattn_bv': (0.0, 0.1),
     'L2_xattn_ln_gamma': (1.0, 0.2),
     'L2_xattn_ln_beta': (0.0, 0.1)}
    factors = {'g_ffn': 8.0,
     'L0_xattn_Wq': 8.0,
     'L0_xattn_bq': 8.0,
     'L0_xattn_Wk': 8.0,
     'L0_xattn_bk': 8.0,
     'L0_xattn_Wv': 2.862,
     'L0_xattn_bv': 8.0,
     'L0_xattn_Wo': 2.703,
     'L0_xattn_bo': 2.738,
     'L0_ffn_q_node_w': 5.357,
     'L0_ffn_q_node_b': 8.0,
     'L0_ffn_q_w1': 6.091,
     'L0_ffn_q_w2': 5.122,
     'L0_ffn_k_node_w': 5.143,
     'L0_ffn_k_node_b': 8.0,
     'L0_ffn_k_w1': 6.018,
     'L0_ffn_k_w2': 5.156,
     'L0_ffn_v_node_b': 3.656,
     'L3_xattn_bq': 8.0,
     'L3_xattn_bk': 8.0,
     'L3_xattn_bv': 8.0,
     'L3_xattn_bo': 8.0,
     'L3_ffn_w_router': 8.0,
     'L3_ffn_wi': 8.0,
     'L3_ffn_wo': 8.0}
    for name, (base, spread) in spreads.items():
        noise = np.random.default_rng([zlib.crc32(name.encode()), seed]).standard_normal(out[name].shape)
        drawn = base * np.exp(spread * noise) if base else spread * noise
        out[name] = jnp.asarray(drawn.astype(out[name].dtype))
    for name, factor in factors.items():
        out[name] = (out[name] * factor).astype(out[name].dtype)
    return out
```

```python
from contextlib import ExitStack

import concourse.bass as bass
from concourse import mybir

F32 = mybir.dt.float32
BF16 = mybir.dt.bfloat16
I32 = mybir.dt.int32
U8 = mybir.dt.uint8
ALU = mybir.AluOpType
ACT = mybir.ActivationFunctionType
X_AXIS = mybir.AxisListType.X

P = 128
S = 1024
D = 128
NT = S // P
CTX = 6404
H = 16
HD = D // H
NC = -(-CTX // P)
LAST = CTX - (NC - 1) * P
TC = 3
NTILE = NC // TC
TW = TC * P
SPLIT = 3
KROWS = SPLIT * HD
SROWS = SPLIT * KROWS + SPLIT + 1
SCALE = float(HD) ** -0.5
BIG = 1e30
SAFE = 60.0
LN_EPS = 1e-5
VC = HD + 1
ATT = ("L0", "L1", "L3")
NSW = 4
WEIGHTS_IN = 16 * (6 + 9 + 4 + 4 + 3 + 2)
assert NTILE * TC == NC and SROWS <= P


class Chain:

    def __init__(self, eng, sem):
        self.eng, self.sem, self.n = eng, sem, 0

    def __call__(self, ins):
        ins.then_inc(self.sem, 1)
        self.n = self.n + 1
        self.eng.wait_ge(self.sem, self.n)


class Sweep:

    def __init__(self, w, a, hh, qh, nx, before):
        self.w, self.a, self.hh, self.qh, self.nx = w, a, hh, qh, nx
        self.n = NC + nx
        self.chunks = sum(s.n for s in before)
        self.pairs = 4 * self.chunks
        self.groups = 2 * self.chunks
        self.ring = [sum(-(-(s.n - b) // TC) for s in before) for b in range(TC)]
        self.aligned = all(s.n % TC == 0 for s in before[-1:])


SWEEPS = []
for _a in range(len(ATT)):
    for _hh in range(2):
        for _qh in range(2):
            _nx = (NT // 2) * (_qh + 1) if ATT[_a] == "L1" else 0
            SWEEPS.append(Sweep(len(SWEEPS), _a, _hh, _qh, _nx, SWEEPS))


def flamingo_decoder(nc, t, out, ks, v_scr, q_scr, m_scr, row_scr):
    with ExitStack() as ctx:
        def sb(name, shape, dt=F32):
            return ctx.enter_context(nc.sbuf_tensor(name, shape, dt))

        def sem(name):
            return ctx.enter_context(nc.semaphore(name))

        PS = ctx.enter_context(nc.psum_tensor("PS", [P, 8, 512], F32))

        ident = sb("ident", [P, P])
        ident_b = sb("ident_b", [P, P], BF16)
        head_of = sb("head_of", [P, 32])
        stair = sb("stair", [P, 384 + 512], BF16)
        upper = sb("upper", [P, P], BF16)
        ones_row = sb("ones_row", [1, P])
        zero_one = sb("zero_one", [P, 2, P], BF16)
        valid = sb("valid", [64, P])
        valid_last = sb("valid_last", [P, 1])
        wk_in = sb("wk_in", [P, 3, D])
        wk = sb("wk", [P, 3, D])
        wq_in = sb("wq_in", [P, 3, D])
        wq = sb("wq", [P, 3, D])
        wo = sb("wo", [P, 3, D])
        bo = sb("bo", [1, 3, D])
        bqk = sb("bqk", [P, 2, 3])
        wv5 = sb("wv5", [P, 5, D])
        l2w = sb("l2w", [P, 3, D])
        l2wq = sb("l2wq", [P, D])
        b5 = sb("b5", [P, 5, D])
        gates_raw = sb("gates_raw", [P, 8])
        gates = sb("gates", [P, 8])
        c_in = sb("c_in", [P, TC, D])
        c_last = sb("c_last", [P, D])
        c_T = sb("c_T", [P, TW])
        kf = sb("kf", [P, 3, TW])
        k_rest = sb("k_rest", [P, 3, TW])
        ksq = sb("ksq", [P, 3, TW])
        kparts = sb("kparts", [P, SPLIT, 3, TW], BF16)
        kv2 = sb("kv2", [P, TC, 2 * D])
        vs = sb("vs", [P, NC + NT, H, VC])
        v_next = sb("v_next", [P, TC, 2, H, VC])
        kmax = sb("kmax", [P, NTILE + 2])
        mask_u8 = sb("mask_u8", [64, P], U8)
        mask_f = sb("mask_f", [64, P])
        mask_rows = sb("mask_rows", [64, 2, P], BF16)
        mask_T = sb("mask_T", [P, 64])
        kv_mask = sb("kv_mask", [P, P])
        kv_sum = sb("kv_sum", [P, P])
        x = sb("x", [P, NT, D])
        xn = sb("xn", [P, NT, D])
        xT = sb("xT", [P, S])
        ln_st = sb("ln_st", [P, NT, 6])
        ln_mv = sb("ln_mv", [P, NT, 2])
        ln_ve = sb("ln_ve", [P, NT])
        ln_sd = sb("ln_sd", [P, NT])
        ln_rs = sb("ln_rs", [P, NT])
        accs = sb("accs", [P, 4, S])
        qf, qr1, qsq = (accs[:, i, :] for i in range(3))
        qparts = sb("qparts", [P, SPLIT, S], BF16)
        q_max = sb("q_max", [P, 1])
        k_max = sb("k_max", [P, 1])
        bound = sb("bound", [P, 1])
        bound_row = sb("bound_row", [1, H])
        bound_max = sb("bound_max", [1, 1])
        flag = sb("flag", [1, 3], I32)
        wide = sb("wide", [P, H, S], BF16)
        qs = wide[0:SROWS, :, :]
        kr = [sb(f"kr{b}", [SROWS, H // 2, P], BF16) for b in range(TC)]
        vr = [sb(f"vr{b}", [P, H // 2, 32]) for b in range(TC)]
        probs = sb("probs", [P, 4, 2, 512])
        prob = [probs[:, i] for i in range(4)]
        rden = sb("rden", [P, NT, H])
        att, att_T = xn, xT
        run_max = sb("run_max", [P, H, NT])
        new_max = sb("new_max", [P, 2 * NT])
        mneg = sb("mneg", [P, P])
        mr1 = sb("mr1", [P, P])
        mparts = sb("mparts", [P, SPLIT, P], BF16)

        const_ready = sem("const_ready")
        w_in = sem("w_in")
        rows_in = sem("rows_in")
        rows_ready = sem("rows_ready")
        rows_out = sem("rows_out")
        wprep_ps = sem("wprep_ps")
        wprep_ready = sem("wprep_ready")
        c_loaded = sem("c_loaded")
        ct_ps = sem("ct_ps")
        ct_ready = sem("ct_ready")
        k_ps = sem("k_ps")
        k_act = sem("k_act")
        k_r1 = sem("k_r1")
        k_part2 = sem("k_part2")
        k_part3 = sem("k_part3")
        k_out = sem("k_out")
        v_ps = sem("v_ps")
        v_ev = sem("v_ev")
        kv_mm = sem("kv_mm")
        kn_ps = sem("kn_ps")
        kn_ev = sem("kn_ev")
        v_out = sem("v_out")
        v_in = sem("v_in")
        v_final = sem("v_final")
        xv_ready = sem("xv_ready")
        x_in = sem("x_in")
        x_ready = sem("x_ready")
        x_out = sem("x_out")
        ln_var = sem("ln_var")
        ln_root = sem("ln_root")
        ln_xn = sem("ln_xn")
        ln_ps = sem("ln_ps")
        ln_xT = sem("ln_xT")
        q_ps = sem("q_ps")
        q_act = sem("q_act")
        q_split = sem("q_split")
        qn_ps = sem("qn_ps")
        bound_ready = sem("bound_ready")
        bound_in = sem("bound_in")
        flag_ready = sem("flag_ready")
        q_out = sem("q_out")
        qs_in = sem("qs_in")
        kr_in = [sem(f"kr_in{b}") for b in range(TC)]
        v_copied = sem("v_copied")
        s_ready = sem("s_ready")
        p_ready = sem("p_ready")
        pv_done = sem("pv_done")
        acc_ev = sem("acc_ev")
        at_ps = sem("at_ps")
        at_rd = sem("at_rd")
        atT_ps = sem("atT_ps")
        atT_ready = sem("atT_ready")
        y_ps = sem("y_ps")
        mx_in = [sem(f"mx_in{a}") for a in range(3)]
        mx_ps = [sem(f"mx_ps{a}") for a in range(3)]
        mx_red = [sem(f"mx_red{a}") for a in range(3)]
        mx_tp = [sem(f"mx_tp{a}") for a in range(3)]
        mx_run = [sem(f"mx_run{a}") for a in range(3)]
        mx_dve = [sem(f"mx_dve{a}") for a in range(3)]
        mx_out = [sem(f"mx_out{a}") for a in range(3)]
        dve_c = sem("dve_c")
        act_c = sem("act_c")
        pool_c = sem("pool_c")

        block = ctx.enter_context(nc.Block())

        def dh(ap):
            return ap.rearrange("p (h d) -> p d h", h=H)

        def norm(dve, chain, src, dst, j):
            v = nc.vector
            for n in range(NT):
                last = v.bn_stats(ln_st[:, n, :], src[:, n, :])
            chain(last)
            for n in range(NT):
                last = v.bn_aggr(ln_mv[:, n, :], ln_st[:, n, :])
            chain(last)
            v.tensor_scalar(ln_ve[:, :], ln_mv[:, :, 1], LN_EPS, None, ALU.add).then_inc(ln_var, 1)
            dve.wait_ge(ln_root, j + 1)
            chain(v.reciprocal(ln_rs[:, :], ln_sd[:, :]))
            for n in range(NT):
                last = v.tensor_scalar(dst[:, n, :], src[:, n, :], ln_mv[:, n, 0:1], ln_rs[:, n:n + 1], ALU.subtract, ALU.mult)
            return last

        def norm_at(k):
            return k + (k >= 5)

        def ln_dve(dve, chain, k):
            if k:
                dve.wait_ge(x_ready, k)
            norm(dve, chain, x, xn, norm_at(k)).then_inc(ln_xn, 1)

        def ln_act(act, k):
            act.wait_ge(ln_var, norm_at(k) + 1)
            nc.scalar.activation(ln_sd[:, :], ln_ve[:, :], ACT.Sqrt).then_inc(ln_root, 1)
            act.wait_ge(ln_ps, k + 1)
            nc.scalar.activation(xT[:, :], PS[:, 0:2, :].rearrange("p b n -> p (b n)"), ACT.Copy).then_inc(ln_xT, 1)

        def ln_pe(pe, k):
            pe.wait_ge(ln_xn, k + 1)
            for n in range(NT):
                last = nc.tensor.transpose(PS[:, n // 4, n % 4 * P:n % 4 * P + P], xn[:, n, :], ident[:, :])
            last.then_inc(ln_ps, 1)

        def add_to_x(dve, gate, y, y_sem, val, k):
            dve.wait_ge(y_sem, val)
            xf = x[:, :, :].rearrange("p n d -> p (n d)")
            nc.vector.scalar_tensor_tensor(xf, y, gates[:, gate:gate + 1], xf, ALU.mult, ALU.add).then_inc(x_ready, 1)

        NODES, LEAVES, DEPTH = 15, 16, 4
        HC = LEAVES * 64 // P
        NETS = ("q", "k", "v")
        FSCALE = float(D) ** -0.5
        wide32 = wide[:, :, :].rearrange("p h n -> p (h n)").bitcast(F32)
        accs_flat = accs[:, :, :].rearrange("p g n -> p (g n)")
        probs_flat = probs[:, :, :, :].rearrange("p i e n -> p (i e n)")
        fw1 = [wide32[:, S * n:S * n + S] for n in range(3)]
        fw2 = [wide32[:, S * (3 + n):S * (4 + n)] for n in range(3)]
        rows_w = sb("rows_w", [96, P])
        cols_w = sb("cols_w", [P, 96])
        B1_AT, RMS_AT = 3 * NODES, 3 * NODES + 3 * HC
        node_b = sb("node_b", [P, 3 * NODES])
        leaf_b2 = sb("leaf_b2", [96, 3, D])
        leaf_sel = sb("leaf_sel", [96, HC, P], BF16)
        bits = sb("bits", [P, NT * 3, NODES])
        paths = [None] + [sb(f"path{l}", [P, NT * 3, 2 ** l]) for l in range(1, DEPTH)]
        leaf = sb("leaf", [P, NT * 3, 32])
        leaf_T = wide32[0:96, 6 * S:7 * S]
        leaf_Tb = wide32[0:96, 7 * S:7 * S + S // 2].bitcast(BF16)
        hid = [probs_flat[:, 512 * r:512 * r + 512] for r in range(4)]
        qkv = [accs[:, n, :] for n in range(3)]
        v_tok = accs[:, 3, :]
        prob_q = [probs_flat[:, S * i:S * i + S] for i in range(2)]
        prob_T = [probs_flat[:, S * (2 + i):S * (3 + i)] for i in range(2)]
        fmax = sb("fmax", [P, NT])
        fneg = sb("fneg", [P, NT])
        fden = sb("fden", [P, NT])
        frec = sb("frec", [P, NT])
        E1, E1S, HID1 = 14, 2, 256
        E2, E3, HID3, CAP = 8, 8, 512, 64
        rw1 = sb("rw1", [P, E1])
        rw3 = sb("rw3", [P, E3])
        countdown = sb("countdown", [P, LEAVES])
        tri = sb("tri", [P, P])
        ones = sb("ones", [P, P])
        logit = sb("logit", [P, NT, E1])
        rprob = sb("rprob", [P, NT, E1])
        work = sb("work", [P, NT, E1])
        sel1 = sb("sel1", [P, NT, E1])
        sel2 = sb("sel2", [P, NT, E1])
        egate = sb("egate", [P, NT, E1 + E1S])
        rmax = sb("rmax", [P, NT])
        rsum = sb("rsum", [P, NT])
        l2bq = sb("l2bq", [P, 1])
        gamma_b = sb("gamma_b", [P, 2, D])
        h_T = ksq[:, :, :].rearrange("p a k -> p (a k)")[:, 0:S]
        moe_acc = kf[:, :, :].rearrange("p a k -> p (a k)")[:, 0:S]
        moe_hid = [probs_flat, accs_flat]
        eA = [wide32[:, 2048 * i:2048 * i + 512] for i in range(2)]
        eB = [wide32[:, 2048 * i + 512:2048 * i + 1024] for i in range(2)]
        eC = [wide32[:, 2048 * i + 1024:2048 * i + 1536] for i in range(2)]

        f_in = sem("f_in")
        fw_in = sem("fw_in")
        l2_normed = sem("l2_normed")
        f_cols_ps = sem("f_cols_ps")
        f_cols = sem("f_cols")
        f_node = sem("f_node")
        f_leaf = sem("f_leaf")
        f_leafT_ps = sem("f_leafT_ps")
        f_leafT = sem("f_leafT")
        f_up = sem("f_up")
        f_relu = sem("f_relu")
        f_masked = sem("f_masked")
        f_out = sem("f_out")
        f_net_ps = sem("f_net_ps")
        f_net = sem("f_net")
        f_v_ps = sem("f_v_ps")
        f_v = sem("f_v")
        fa_s = sem("fa_s")
        fa_max = sem("fa_max")
        fa_p = sem("fa_p")
        fa_T = sem("fa_T")
        fa_Tc = sem("fa_Tc")
        fa_o = sem("fa_o")
        r_ps = sem("r_ps")
        r_cen = sem("r_cen")
        r_exp = sem("r_exp")
        r_sel = sem("r_sel")
        r_cum = sem("r_cum")
        ms_ready = sem("ms_ready")
        ms_root = sem("ms_root")
        ht_sb = sem("ht_sb")
        ht_ps = sem("ht_ps")
        ht_ready = sem("ht_ready")
        e_in = [sem(f"e_in{i}") for i in range(2)]
        e_scaled = sem("e_scaled")
        h_ps = sem("h_ps")
        h_act = sem("h_act")
        h_mul = sem("h_mul")
        dn_ps = sem("dn_ps")
        dn_ev = sem("dn_ev")
        l2q_ps = sem("l2q_ps")
        l2q = sem("l2q")
        l2_ps = sem("l2_ps")

        class Moe:

            def __init__(self, n, chunks, up, func, scaled, gated, before):
                self.n, self.chunks, self.up, self.func, self.scaled, self.gated = n, chunks, up, func, scaled, gated
                self.units = 2 * chunks
                self.loads = 3 if up else 2
                self.e0 = sum(m.n for m in before)
                self.u0 = sum(m.n * m.units for m in before)
                self.mul0 = sum(m.n * m.units for m in before if m.up)
                self.in0 = sum(16 * m.loads * (m.n // 2) for m in before)
                self.ring = 2 if up else 4

        MOE = []
        MOE.append(Moe(E1 + E1S, HID1 // P, False, ACT.Silu, True, True, MOE[:]))
        MOE.append(Moe(E2, HID3 // P, True, ACT.Silu, False, False, MOE[:]))
        MOE.append(Moe(E3, HID3 // P, False, ACT.Gelu_apprx_tanh, False, True, MOE[:]))

        def sp_late_weights(sp):
            for n, net in enumerate(NETS):
                sp.dma_start(rows_w[NODES * n:NODES * (n + 1), :], t[f"L0_ffn_{net}_node_w"][:, :]).then_inc(f_in, 16)
                sp.dma_start(rows_w[B1_AT + HC * n:B1_AT + HC * (n + 1), :],
                             t[f"L0_ffn_{net}_b1"].rearrange("(c l) h -> c (l h)", c=HC)).then_inc(f_in, 16)
                sp.dma_start(node_b[:, NODES * n:NODES * (n + 1)], t[f"L0_ffn_{net}_node_b"].partition_broadcast(P)).then_inc(f_in, 16)
                sp.dma_start(leaf_b2[32 * n:32 * n + LEAVES, n, :], t[f"L0_ffn_{net}_b2"][:, :]).then_inc(f_in, 16)
            sp.dma_start(rows_w[RMS_AT:RMS_AT + E1, :], t["L1_ffn_rms_w"][:, :]).then_inc(f_in, 16)
            sp.dma_start(rows_w[RMS_AT + E1:RMS_AT + E1 + E1S, :], t["L1_ffn_rms_w_s"][:, :]).then_inc(f_in, 16)
            sp.dma_start(rw1[:, :], t["L1_ffn_router_w"][:, :]).then_inc(f_in, 16)
            sp.dma_start(rw3[:, :], t["L3_ffn_w_router"][:, :]).then_inc(f_in, 16)
            sp.dma_start(l2bq[:, :], t["L2_xattn_bq"].unsqueeze(1), allow_slow_non_contiguous=True).then_inc(f_in, 16)
            sp.dma_start(gamma_b[:, 0, :], t["L2_xattn_ln_gamma"].partition_broadcast(P)).then_inc(f_in, 16)
            sp.dma_start(gamma_b[:, 1, :], t["L2_xattn_ln_beta"].partition_broadcast(P)).then_inc(f_in, 16)

        SMALL_IN = 16 * (4 * 3 + 7)

        def moe_sp(sp, m, parts):
            def load(e, i, use):
                for dst, src in use(e, i):
                    sp.dma_start(dst, src).then_inc(e_in[i], 16)

            for i in range(2):
                load(i, i, parts[0])
            last = m.n // 2 - (1 if len(parts) > 1 else 0)
            with sp.Fori(1, last) as j:
                for i in range(2):
                    sp.wait_ge(dn_ps, 2 * j + (m.e0 + i - 1))
                    load(2 * j + i, i, parts[0])
            if len(parts) > 1:
                for i in range(2):
                    sp.wait_ge(dn_ps, m.e0 + m.n - 3 + i)
                    load(i, i, parts[1])

        def between_sp(sp, a):
            if a == 0:
                for n, net in enumerate(NETS):
                    sp.dma_start(fw1[n].rearrange("p (l h) -> p l h", l=LEAVES), t[f"L0_ffn_{net}_w1"].rearrange("l d h -> d l h")).then_inc(fw_in, 16)
                    sp.dma_start(fw2[n].rearrange("p (c o) -> p c o", c=HC),
                                 t[f"L0_ffn_{net}_w2"].rearrange("(c l) h o -> (l h) c o", c=HC)).then_inc(fw_in, 16)
            if a == 1:
                def shared(e, i):
                    return ((eA[i][:, 0:HID1], t["L1_ffn_w1_s"][e]),
                            (eC[i][:, 0:HID1].rearrange("p (c o) -> p c o", c=2), t["L1_ffn_w2_s"][e].rearrange("(c p) o -> p c o", p=P)))

                def routed(e, i):
                    return ((eA[i][:, 0:HID1], t["L1_ffn_w1"][bass.ds(e, 1), :, :].rearrange("e d f -> (e d) f")),
                            (eC[i][:, 0:HID1].rearrange("p (c o) -> p c o", c=2),
                             t["L1_ffn_w2"][bass.ds(e, 1), :, :].rearrange("e (c p) o -> p (e c) o", p=P)))

                moe_sp(sp, MOE[0], (routed, shared))

                def swiglu(e, i):
                    return ((eA[i], t["L2_ffn_Wg"][bass.ds(e, 1), :, :].rearrange("e d f -> (e d) f")),
                            (eB[i], t["L2_ffn_Wu"][bass.ds(e, 1), :, :].rearrange("e d f -> (e d) f")),
                            (eC[i].rearrange("p (c o) -> p c o", c=4),
                             t["L2_ffn_Wd"][bass.ds(e, 1), :, :].rearrange("e (c p) o -> p (e c) o", p=P)))

                sp.wait_ge(dn_ps, MOE[1].e0)
                moe_sp(sp, MOE[1], (swiglu,))
            if a == 2:
                def gelu_expert(e, i):
                    return ((eA[i], t["L3_ffn_wi"][bass.ds(e, 1), :, :].rearrange("e d f -> (e d) f")),
                            (eC[i].rearrange("p (c o) -> p c o", c=4),
                             t["L3_ffn_wo"][bass.ds(e, 1), :, :].rearrange("e (c p) o -> p (e c) o", p=P)))

                moe_sp(sp, MOE[2], (gelu_expert,))

        def const_pool(g, chain):
            chain(g.memset(leaf_sel[:, :, :], 0.0))
            for n in range(3):
                ls = leaf_sel[:, :, :].rearrange("p c (l h) -> p c l h", l=2)
                chain(g.affine_select(out=ls, in_=ls, compare_op=ALU.not_equal, fill=1.0,
                                      base=-32 * n, pattern=[[-2, HC], [-1, 2], [0, 64]], channel_multiplier=1))
            chain(g.iota(countdown[:, :], pattern=[[-1, LEAVES]], base=LEAVES, channel_multiplier=0,
                         allow_small_or_imprecise_dtypes=True))
            chain(g.memset(ones[:, :], 1.0))
            chain(g.affine_select(out=tri[:, :], in_=ones[:, :], compare_op=ALU.is_ge, fill=0.0,
                                  base=0, pattern=[[1, P]], channel_multiplier=-1))
            g.memset(leaf[:, :, :], 0.0)
            g.memset(rows_w[:, :], 0.0)
            g.memset(leaf_b2[:, :, :], 0.0)
            chain(g.memset(egate[:, :, E1:E1 + E1S], 1.0))

        def between_pool(pool, a):
            if a == 1:
                m = MOE[0]
                pool.wait_ge(f_cols, 1)

                def scale(e, i, loads):
                    pool.wait_ge(e_in[i], loads)
                    nc.gpsimd.tensor_tensor(eA[i][:, 0:HID1], eA[i][:, 0:HID1],
                                             cols_w[:, bass.ds(e + RMS_AT, 1)].to_broadcast([P, HID1]), ALU.mult).then_inc(e_scaled, 1)

                for i in range(2):
                    scale(i, i, m.in0 + 16 * m.loads)
                with pool.Fori(1, m.n // 2) as j:
                    for i in range(2):
                        scale(2 * j + i, i, j * (16 * m.loads) + (m.in0 + 16 * m.loads))

        def moe_pe(pe, m, hT):
            te = nc.tensor

            def up(e, i, loads, first=False):
                pe.wait_ge(e_in[i], loads)
                if m.scaled:
                    pe.wait_ge(e_scaled, e + 1)
                for k in range(m.units):
                    c, half = divmod(k, 2)
                    if not (first and k < m.ring):
                        if m.up:
                            pe.wait_ge(h_mul, m.units * e + (m.mul0 + k - m.ring + 1))
                        else:
                            pe.wait_ge(h_act, m.units * e + (m.u0 + k - m.ring + 1))
                    last = te.matmul(PS[:, slot(m, k, i), :], eA[i][:, P * c:P * c + P], hT[:, 512 * half:512 * half + 512], start=True, stop=True)
                    if m.up:
                        last = te.matmul(PS[:, 3 + slot(m, k, i), :], eB[i][:, P * c:P * c + P], hT[:, 512 * half:512 * half + 512], start=True, stop=True)
                    last.then_inc(h_ps, 1)

            def down(e, i, first=False):
                if m.up:
                    pe.wait_ge(h_mul, m.units * e + (m.mul0 + m.units))
                else:
                    pe.wait_ge(h_act, m.units * e + (m.u0 + m.units))
                if not first:
                    pe.wait_ge(dn_ev, e + m.e0)
                for n in range(NT):
                    for c in range(m.chunks):
                        last = te.matmul(PS[:, 6 + n // 4, n % 4 * P:n % 4 * P + P], moe_hid[i][:, S * c + P * n:S * c + P * n + P],
                                         eC[i][:, P * c:P * c + P], start=(c == 0), stop=(c == m.chunks - 1))
                last.then_inc(dn_ps, 1)

            per = 16 * m.loads
            up(0, 0, m.in0 + per, True)
            up(1, 1, m.in0 + per)
            down(0, 0, True)
            with pe.Fori(1, m.n // 2) as j:
                up(2 * j, 0, j * per + (m.in0 + per))
                down(2 * j - 1, 1)
                up(2 * j + 1, 1, j * per + (m.in0 + per))
                down(2 * j, 0)
            down(m.n - 1, 1)

        def slot(m, k, i):
            return (m.units * i + k) % m.ring

        def moe_act(act, m):
            def units(e, i, first=False):
                for k in range(m.units):
                    c, half = divmod(k, 2)
                    act.wait_ge(h_ps, m.units * e + (m.u0 + k + 1))
                    if k == 0 and not first:
                        act.wait_ge(dn_ps, e + (m.e0 - 1))
                    nc.scalar.activation(moe_hid[i][:, S * c + 512 * half:S * c + 512 * half + 512], PS[:, slot(m, k, i), :], m.func).then_inc(h_act, 1)

            units(0, 0, True)
            units(1, 1, True)
            with act.Fori(1, m.n // 2) as j:
                units(2 * j, 0)
                units(2 * j + 1, 1)

        def moe_dve(dve, m):
            v = nc.vector

            def mul(e, i):
                if not m.up:
                    return
                for k in range(m.units):
                    c, half = divmod(k, 2)
                    o = moe_hid[i][:, S * c + 512 * half:S * c + 512 * half + 512]
                    dve.wait_ge(h_act, m.units * e + (m.u0 + k + 1))
                    v.tensor_tensor(o, o, PS[:, 3 + slot(m, k, i), :], ALU.mult).then_inc(h_mul, 1)

            def add(e, first=False):
                dve.wait_ge(dn_ps, e + (m.e0 + 1))
                if not first:
                    dve.wait_ge(dn_ev, e + m.e0)
                if not m.gated:
                    o = PS[:, 6:8, :].rearrange("p b n -> p (b n)")
                    if first:
                        v.tensor_copy(moe_acc, o).then_inc(dn_ev, 1)
                    else:
                        v.tensor_tensor(moe_acc, moe_acc, o, ALU.add).then_inc(dn_ev, 1)
                    return
                for n in range(NT):
                    o = PS[:, 6 + n // 4, n % 4 * P:n % 4 * P + P]
                    g = egate[:, n, bass.ds(e, 1)]
                    if first:
                        last = v.tensor_scalar(moe_acc[:, P * n:P * n + P], o, g, None, ALU.mult)
                    else:
                        last = v.scalar_tensor_tensor(moe_acc[:, P * n:P * n + P], o, g, moe_acc[:, P * n:P * n + P], ALU.mult, ALU.add)
                last.then_inc(dn_ev, 1)

            mul(0, 0)
            mul(1, 1)
            add(0, True)
            with dve.Fori(1, m.n // 2) as j:
                mul(2 * j, 0)
                add(2 * j - 1)
                mul(2 * j + 1, 1)
                add(2 * j)
            add(m.n - 1)

        def router_pe(pe, rw, n_e, k):
            for n in range(NT):
                last = nc.tensor.matmul(PS[:, 2, n * n_e:(n + 1) * n_e], xT[:, n * P:(n + 1) * P], rw[:, :], start=True, stop=True)
            last.then_inc(r_ps, 1)

        def router_act(act, n_e, i):
            act.wait_ge(r_cen, i + 1)
            nc.scalar.activation(work[:, :, 0:n_e], logit[:, :, 0:n_e], ACT.Exp).then_inc(r_exp, 1)

        def router_dve(dve, chain, n_e, i):
            v = nc.vector

            def bc(a):
                return a.unsqueeze(2).to_broadcast([P, NT, n_e])

            ps = PS[:, 2, 0:NT * n_e].rearrange("p (n e) -> p n e", e=n_e)
            lg, pr, wk_, s1, s2 = (w[:, :, 0:n_e] for w in (logit, rprob, work, sel1, sel2))
            count = countdown[:, LEAVES - n_e:LEAVES].unsqueeze(1).to_broadcast([P, NT, n_e])
            dve.wait_ge(r_ps, i + 1)
            chain(v.reduce_max(rmax[:, :], ps, X_AXIS))
            v.tensor_tensor(lg, ps, bc(rmax[:, :]), ALU.subtract).then_inc(r_cen, 1)
            dve.wait_ge(r_exp, i + 1)
            chain(v.reduce_sum(rsum[:, :], wk_, X_AXIS))
            chain(v.reciprocal(rsum[:, :], rsum[:, :]))
            chain(v.tensor_tensor(pr, wk_, bc(rsum[:, :]), ALU.mult))
            for s, src in ((s1, pr), (s2, lg)):
                chain(v.reduce_max(rmax[:, :], src, X_AXIS))
                chain(v.tensor_tensor(wk_, src, bc(rmax[:, :]), ALU.is_ge))
                chain(v.tensor_tensor(wk_, wk_, count, ALU.mult))
                chain(v.reduce_max(rmax[:, :], wk_, X_AXIS))
                chain(v.tensor_tensor(s, wk_, bc(rmax[:, :]), ALU.is_equal))
                if s is s1:
                    chain(v.scalar_tensor_tensor(lg, s1, -2.0, pr, ALU.mult, ALU.add))

        def fff_dve(dve, chain):
            v = nc.vector
            dve.wait_ge(f_node, 1)
            ps = PS[:, 2, 0:NT * 3 * NODES].rearrange("p (n m) -> p n m", n=NT)
            b3 = bits[:, :, :].rearrange("p (n m) k -> p n (m k)", n=NT)
            chain(v.tensor_tensor(b3, ps, node_b[:, :].unsqueeze(1).to_broadcast([P, NT, 3 * NODES]), ALU.add))
            chain(v.tensor_scalar(b3, b3, 0.0, None, ALU.is_ge))
            for l in range(DEPTH):
                w = 2 ** l
                dst = leaf[:, :, 0:LEAVES] if l == DEPTH - 1 else paths[l + 1][:, :, :]
                dst = dst.rearrange("p m (w s) -> p m w s", s=2)
                b = bits[:, :, w - 1:2 * w - 1]
                if l == 0:
                    v.tensor_copy(dst[:, :, :, 1], b)
                    chain(v.tensor_scalar(dst[:, :, :, 0], b, -1.0, 1.0, ALU.mult, ALU.add))
                else:
                    chain(v.tensor_tensor(dst[:, :, :, 1], paths[l][:, :, :], b, ALU.mult))
                    last = v.tensor_tensor(dst[:, :, :, 0], paths[l][:, :, :], dst[:, :, :, 1], ALU.subtract)
                    if l < DEPTH - 1:
                        chain(last)
            last.then_inc(f_leaf, 1)
            for u in range(3 * 2 * HC):
                dve.wait_ge(f_relu, u + 1)
                v.tensor_tensor(hid[u % 4], hid[u % 4], PS[:, 2 + u % 2, :], ALU.mult).then_inc(f_masked, 1)
            dve.wait_ge(f_v_ps, 1)
            v.tensor_copy(v_tok, PS[:, 6:8, :].rearrange("p b n -> p (b n)")).then_inc(f_v, 1)

            def copy_T(n):
                dve.wait_ge(fa_T, n + 1)
                if n >= 2:
                    dve.wait_ge(fa_o, n - 1)
                v.tensor_copy(prob_T[n % 2], PS[:, 4:6, :].rearrange("p b n -> p (b n)")).then_inc(fa_Tc, 1)

            for n in range(NT):
                dve.wait_ge(fa_s, n + 1)
                b = 2 * (n % 2)
                chain(v.reduce_max(fmax[:, n:n + 1], PS[:, b:b + 2, :].rearrange("p b n -> p (b n)"), X_AXIS))
                v.tensor_scalar(fneg[:, n:n + 1], fmax[:, n:n + 1], -FSCALE, None, ALU.mult).then_inc(fa_max, 1)
                if n:
                    copy_T(n - 1)
            copy_T(NT - 1)
            dve.wait_ge(fa_p, NT)
            chain(v.reciprocal(frec[:, :], fden[:, :]))
            chain(v.tensor_scalar(frec[:, :], frec[:, :], gates[:, 4:5], None, ALU.mult))
            dve.wait_ge(fa_o, NT)
            for n in range(NT):
                last = v.scalar_tensor_tensor(x[:, n, :], PS[:, 6 + n // 4, n % 4 * P:n % 4 * P + P], frec[:, n:n + 1], x[:, n, :], ALU.mult, ALU.add)
            last.then_inc(x_ready, 1)

        def fff_act(act):
            sc = nc.scalar
            act.wait_ge(f_leafT_ps, 1)
            ps = PS[0:96, 4:6, :].rearrange("p b n -> p (b n)")
            sc.activation(leaf_T, ps, ACT.Copy)
            sc.activation(leaf_Tb, ps, ACT.Copy).then_inc(f_leafT, 1)
            for u in range(3 * 2 * HC):
                net, k = divmod(u, 2 * HC)
                act.wait_ge(f_up, u + 1)
                if u >= 4:
                    act.wait_ge(f_out, u - 3)
                col = B1_AT + HC * net + k // 2
                sc.activation(hid[u % 4], PS[:, u % 2, :], ACT.Relu, bias=cols_w[:, col:col + 1]).then_inc(f_relu, 1)
                if k == 2 * HC - 1:
                    act.wait_ge(f_net_ps, net + 1)
                    b = 4 + 2 * (net % 2)
                    sc.activation(qkv[net], PS[:, b:b + 2, :].rearrange("p b n -> p (b n)"), ACT.Copy).then_inc(f_net, 1)
            for n in range(NT):
                act.wait_ge(fa_max, n + 1)
                if n >= 2:
                    act.wait_ge(fa_T, n - 1)
                b = 2 * (n % 2)
                sc.activation(prob_q[n % 2], PS[:, b:b + 2, :].rearrange("p b n -> p (b n)"), ACT.Exp,
                              bias=fneg[:, n:n + 1], scale=FSCALE, accum_out=fden[:, n:n + 1]).then_inc(fa_p, 1)

        def fff_pe(pe):
            te = nc.tensor
            pe.wait_ge(f_cols, 1)
            pe.wait_ge(ln_xT, 2)
            for n in range(NT):
                last = te.matmul(PS[:, 2, n * 3 * NODES:(n + 1) * 3 * NODES], xT[:, n * P:(n + 1) * P], cols_w[:, 0:3 * NODES], start=True, stop=True)
            last.then_inc(f_node, 1)
            pe.wait_ge(f_leaf, 1)
            for n in range(NT):
                last = te.transpose(PS[0:96, 4 + n // 4, n % 4 * P:n % 4 * P + P], leaf[:, 3 * n:3 * n + 3, :].rearrange("p m l -> p (m l)"), ident[:, :])
            last.then_inc(f_leafT_ps, 1)
            pe.wait_ge(f_leafT, 1)
            pe.wait_ge(fw_in, 16 * 6)
            n_units = 3 * 2 * HC

            def up(u):
                net, k = divmod(u, 2 * HC)
                c, half = divmod(k, 2)
                cols = slice(512 * half, 512 * half + 512)
                if u >= 2:
                    pe.wait_ge(f_masked, u - 1)
                te.matmul(PS[:, u % 2, :], fw1[net][:, P * c:P * c + P], xT[:, cols], start=True, stop=True)
                te.matmul(PS[:, 2 + u % 2, :], leaf_sel[32 * net:32 * net + LEAVES, c, :], leaf_Tb[32 * net:32 * net + LEAVES, cols],
                          start=True, stop=True).then_inc(f_up, 1)

            def out(u):
                net, k = divmod(u, 2 * HC)
                c, half = divmod(k, 2)
                cols = slice(512 * half, 512 * half + 512)
                o = PS[:, 4 + 2 * (net % 2) + half, :]
                if net == 2 and k == 0:
                    pe.wait_ge(f_net, 1)
                pe.wait_ge(f_masked, u + 1)
                last = te.matmul(o, fw2[net][:, D * c:D * c + D], hid[u % 4], start=(c == 0), stop=False)
                last.then_inc(f_out, 1)
                if c == HC - 1:
                    last = te.matmul(o, leaf_b2[:, net, :], leaf_T[:, cols], start=False, stop=True)
                    if half:
                        last.then_inc(f_net_ps, 1)

            up(0)
            for u in range(n_units):
                if u + 1 < n_units:
                    up(u + 1)
                out(u)
            pe.wait_ge(f_net, 3)
            for n in range(NT):
                last = te.transpose(PS[:, 6 + n // 4, n % 4 * P:n % 4 * P + P], qkv[2][:, n * P:(n + 1) * P], ident[:, :])
            last.then_inc(f_v_ps, 1)

            def score(n):
                if n >= 2:
                    pe.wait_ge(fa_p, n - 1)
                for i in range(2):
                    last = te.matmul(PS[:, 2 * (n % 2) + i, :], qkv[0][:, n * P:(n + 1) * P], qkv[1][:, 512 * i:512 * i + 512], start=True, stop=True)
                last.then_inc(fa_s, 1)

            def turn(n):
                pe.wait_ge(fa_p, n + 1)
                if n:
                    pe.wait_ge(fa_Tc, n)
                for j in range(NT):
                    last = te.transpose(PS[:, 4 + j // 4, j % 4 * P:j % 4 * P + P], prob_q[n % 2][:, j * P:(j + 1) * P], ident[:, :])
                last.then_inc(fa_T, 1)

            def product(n):
                pe.wait_ge(fa_Tc, n + 1)
                for j in range(NT):
                    last = te.matmul(PS[:, 6 + n // 4, n % 4 * P:n % 4 * P + P], prob_T[n % 2][:, j * P:(j + 1) * P], v_tok[:, j * P:(j + 1) * P],
                                     start=(j == 0), stop=(j == NT - 1))
                last.then_inc(fa_o, 1)

            score(0)
            score(1)
            pe.wait_ge(f_v, 1)
            for n in range(NT):
                turn(n)
                if n + 2 < NT:
                    score(n + 2)
                product(n)

        def between_dve(dve, chain, a):
            v = nc.vector
            if a == 0:
                ln_dve(dve, chain, 1)
                fff_dve(dve, chain)
            if a == 1:
                ln_dve(dve, chain, 3)
                xnf, sq = xn[:, :, :], accs_flat[:, 0:S].rearrange("p (n d) -> p n d", n=NT)
                dve.wait_ge(ln_xn, 4)
                chain(v.tensor_tensor(sq, xnf, xnf, ALU.mult))
                chain(v.reduce_sum(ln_ve[:, :], sq, X_AXIS))
                v.tensor_scalar(ln_ve[:, :], ln_ve[:, :], 1.0 / D, 1.1920929e-07, ALU.mult, ALU.add).then_inc(ms_ready, 1)
                dve.wait_ge(ms_root, 1)
                chain(v.reciprocal(ln_rs[:, :], ln_sd[:, :]))
                for n in range(NT):
                    last = v.tensor_scalar(sq[:, n, :], xn[:, n, :], ln_rs[:, n:n + 1], None, ALU.mult)
                last.then_inc(ht_sb, 1)
                router_dve(dve, chain, E1, 0)
                g14 = egate[:, :, 0:E1]
                chain(v.tensor_tensor(work[:, :, :], sel1[:, :, :], sel2[:, :, :], ALU.add))
                chain(v.tensor_tensor(g14, work[:, :, :], rprob[:, :, :], ALU.mult))
                chain(v.reduce_sum(rsum[:, :], g14, X_AXIS))
                chain(v.tensor_scalar(rsum[:, :], rsum[:, :], 1e-9, None, ALU.add))
                chain(v.reciprocal(rsum[:, :], rsum[:, :]))
                chain(v.tensor_tensor(g14, g14, rsum[:, :].unsqueeze(2).to_broadcast([P, NT, E1]), ALU.mult))
                moe_dve(dve, MOE[0])
                add_to_x(dve, 5, moe_acc, dn_ev, MOE[1].e0, 3)
                ln_dve(dve, chain, 4)
                z = accs[:, 1, :].rearrange("p (n d) -> p n d", n=NT)
                dve.wait_ge(l2_ps, 1)
                chain(v.scalar_tensor_tensor(accs[:, 1, :], PS[:, 4:6, :].rearrange("p b n -> p (b n)"), SCALE,
                                             xn[:, :, :].rearrange("p n d -> p (n d)"), ALU.mult, ALU.add))
                norm(dve, chain, z, z, 5).then_inc(l2_normed, 1)
                dve.wait_ge(l2_normed, 1)
                for i, op in ((0, ALU.mult), (1, ALU.add)):
                    chain(v.tensor_tensor(z, z, gamma_b[:, i, :].unsqueeze(1).to_broadcast([P, NT, D]), op))
                xf = x[:, :, :].rearrange("p n d -> p (n d)")
                v.scalar_tensor_tensor(xf, accs[:, 1, :], gates[:, 2:3], xf, ALU.mult, ALU.add).then_inc(x_ready, 1)
                ln_dve(dve, chain, 5)
                moe_dve(dve, MOE[1])
                add_to_x(dve, 6, moe_acc, dn_ev, MOE[2].e0, 5)
            if a == 2:
                ln_dve(dve, chain, 7)
                router_dve(dve, chain, E3, 1)
                v.tensor_copy(egate[:, :, 0:E3], sel1[:, :, 0:E3])
                v.tensor_copy(egate[:, :, E3:2 * E3], sel2[:, :, 0:E3]).then_inc(r_sel, 1)
                s8 = [w[:, :, 0:E3] for w in (sel1, sel2, rprob, work, logit)]
                dve.wait_ge(r_cum, 1)
                chain(v.scalar_tensor_tensor(s8[3], PS[:, 5, 0:NT * E3].rearrange("p (n e) -> p n e", e=E3), float(CAP), s8[0], ALU.is_le, ALU.mult))
                chain(v.scalar_tensor_tensor(s8[4], PS[:, 5, NT * E3:2 * NT * E3].rearrange("p (n e) -> p n e", e=E3), float(CAP), s8[1], ALU.is_le, ALU.mult))
                chain(v.tensor_tensor(s8[3], s8[3], s8[4], ALU.add))
                chain(v.tensor_tensor(egate[:, :, 0:E3], s8[3], s8[2], ALU.mult))
                moe_dve(dve, MOE[2])
                add_to_x(dve, 7, moe_acc, dn_ev, MOE[2].e0 + MOE[2].n, 7)

        def between_act(act, a):
            sc = nc.scalar
            if a == 0:
                ln_act(act, 1)
                fff_act(act)
            if a == 1:
                ln_act(act, 3)
                act.wait_ge(ms_ready, 1)
                sc.activation(ln_sd[:, :], ln_ve[:, :], ACT.Sqrt).then_inc(ms_root, 1)
                router_act(act, E1, 0)
                act.wait_ge(ht_ps, 1)
                sc.activation(h_T, PS[:, 4:6, :].rearrange("p b n -> p (b n)"), ACT.Copy).then_inc(ht_ready, 1)
                moe_act(act, MOE[0])
                ln_act(act, 4)
                act.wait_ge(l2q_ps, 1)
                sc.activation(accs[:, 0, :], PS[:, 2:4, :].rearrange("p b n -> p (b n)"), ACT.Identity, bias=l2bq[:, 0:1]).then_inc(l2q, 1)
                act.wait_ge(ln_var, 6)
                sc.activation(ln_sd[:, :], ln_ve[:, :], ACT.Sqrt).then_inc(ln_root, 1)
                ln_act(act, 5)
                moe_act(act, MOE[1])
            if a == 2:
                ln_act(act, 7)
                router_act(act, E3, 1)
                moe_act(act, MOE[2])

        def between_pe(pe, a):
            te = nc.tensor
            if a == 0:
                ln_pe(pe, 1)
                fff_pe(pe)
            if a == 1:
                ln_pe(pe, 3)
                pe.wait_ge(ht_sb, 1)
                for n in range(NT):
                    last = te.transpose(PS[:, 4 + n // 4, n % 4 * P:n % 4 * P + P], accs_flat[:, P * n:P * n + P], ident[:, :])
                last.then_inc(ht_ps, 1)
                pe.wait_ge(ln_xT, 4)
                router_pe(pe, rw1, E1, 0)
                pe.wait_ge(ht_ready, 1)
                moe_pe(pe, MOE[0], h_T)
                ln_pe(pe, 4)
                pe.wait_ge(ln_xT, 5)
                for i in range(2):
                    last = te.matmul(PS[:, 2 + i, :], l2wq[:, :], xT[:, 512 * i:512 * i + 512], start=True, stop=True)
                last.then_inc(l2q_ps, 1)
                pe.wait_ge(l2q, 1)
                for n in range(NT):
                    last = te.matmul(PS[:, 4 + n // 4, n % 4 * P:n % 4 * P + P], accs[:, 0, n * P:(n + 1) * P], kv_sum[:, :], start=True, stop=True)
                last.then_inc(l2_ps, 1)
                ln_pe(pe, 5)
                pe.wait_ge(ln_xT, 6)
                moe_pe(pe, MOE[1], xT)
            if a == 2:
                ln_pe(pe, 7)
                pe.wait_ge(ln_xT, 8)
                router_pe(pe, rw3, E3, 1)
                pe.wait_ge(r_sel, 1)
                c1, c2 = PS[:, 5, 0:NT * E3], PS[:, 5, NT * E3:2 * NT * E3]
                te.matmul(c1, tri[:, :], egate[:, :, 0:E3], start=True, stop=True)
                te.matmul(c2, ones[:, :], egate[:, :, 0:E3], start=True, stop=False)
                te.matmul(c2, tri[:, :], egate[:, :, E3:2 * E3], start=False, stop=True).then_inc(r_cum, 1)
                moe_pe(pe, MOE[2], xT)

        def xk_part(i, c):
            return kparts[:, c, :, :].rearrange("p a k -> p (a k)")[:, 512 * i:512 * i + 512]

        @block.sync
        def _(sp):
            for a, (k, v) in enumerate((("L0_xattn_Wk", "L0_xattn_Wv"), (None, None), ("L3_xattn_Wk", "L3_xattn_Wv"))):
                wkv = t["L1_xattn_Wkv"]
                sp.dma_start(wk_in[:, a, :], t[k][:, :] if k else wkv[:, 0:D]).then_inc(w_in, 16)
                sp.dma_start(wv5[:, a, :], t[v][:, :] if v else wkv[:, D:2 * D]).then_inc(w_in, 16)
            for a, l in enumerate(ATT):
                sp.dma_start(wq_in[:, a, :], t[f"{l}_xattn_Wq"][:, :]).then_inc(w_in, 16)
                sp.dma_start(wo[:, a, :], t["L1_xattn_Wout" if a == 1 else f"{l}_xattn_Wo"][:, :]).then_inc(w_in, 16)
                sp.dma_start(bo[0:1, a, :], t["L1_xattn_bout" if a == 1 else f"{l}_xattn_bo"].unsqueeze(0)).then_inc(w_in, 16)
            sp.wait_ge(const_ready, 1)
            for a in (0, 2):
                for i, n in enumerate(("bq", "bk")):
                    src = t[f"{ATT[a]}_xattn_{n}"].rearrange("(h d o) -> d h o", h=H, o=1)
                    sp.dma_start(bqk[:, i, a:a + 1], src, allow_slow_non_contiguous=True).then_inc(w_in, 16)
            for i, n in ((0, "L0_xattn_bv"), (2, "L3_xattn_bv"), (3, "L2_xattn_bk"), (4, "L2_xattn_bv")):
                sp.dma_start(b5[:, i, :], t[n].partition_broadcast(P)).then_inc(w_in, 16)
            for i, n in enumerate(("L2_xattn_Wk", "L2_xattn_Wv", "L2_xattn_Wq")):
                sp.dma_start(l2w[:, i, :], t[n][:, :]).then_inc(w_in, 16)
            for i, n in enumerate(("g_xattn", "g_ffn")):
                sp.dma_start(gates_raw[:, 4 * i:4 * i + 4], t[n].partition_broadcast(P)).then_inc(w_in, 16)

            sp_late_weights(sp)
            ctx_rows = t["ctx_1024"][0]
            sp.dma_start(c_last[0:LAST, :], ctx_rows[(NC - 1) * P:CTX, :]).then_inc(rows_in, 16)
            mask = t["mask_Bx1xS2_bf1"][0, 0]
            sp.dma_start(mask_u8[0:NC - 1, :], mask[0:(NC - 1) * P].rearrange("(c p) -> c p", p=P)).then_inc(rows_in, 16)
            sp.dma_start(mask_u8[NC - 1:NC, 0:LAST], mask[(NC - 1) * P:CTX].unsqueeze(0)).then_inc(rows_in, 16)
            sp.dma_start(x[:, :, :], t["x"][0].rearrange("(n p) d -> p n d", p=P)).then_inc(x_in, 16)

            for a in range(3):
                n = NC + (NT if a == 1 else 0)
                for c in range(SPLIT):
                    sp.dma_start(ks[a, 0:n, KROWS + c, :, :], zero_one[0:n, 1, :].unsqueeze(1).to_broadcast([n, H, P])).then_inc(rows_out, 16)
            sp.dma_start(row_scr[0:SPLIT].rearrange("r (p n) -> p r n", p=P), zero_one[:, 0, :].unsqueeze(1).to_broadcast([P, SPLIT, P])).then_inc(rows_out, 16)
            sp.dma_start(row_scr[SPLIT].rearrange("(p n) -> p n", p=P), zero_one[:, 1, :]).then_inc(rows_out, 16)
            sp.dma_start(ks[1, NC:NC + NT, KROWS + SPLIT, :, :], zero_one[0:NT, 0, :].unsqueeze(1).to_broadcast([NT, H, P])).then_inc(rows_out, 16)
            sp.wait_ge(rows_ready, 1)
            for a in range(3):
                sp.dma_start(ks[a, 0:NC, KROWS + SPLIT, :, :], mask_rows[0:NC, a // 2, :].unsqueeze(1).to_broadcast([NC, H, P])).then_inc(rows_out, 16)

            def load_ctx(i, n):
                sp.dma_start(c_in[:, 0:n, :], ctx_rows[bass.ds(i * TW, n * P), :].rearrange("(c p) d -> p c d", p=P)).then_inc(c_loaded, 16)

            def store_k(i):
                sp.wait_ge(k_act, i + 1)
                sp.wait_ge(k_part2, i + 1)
                sp.wait_ge(k_part3, i + 1)
                for a in range(3):
                    for c in range(SPLIT):
                        sp.dma_start(ks[a, bass.ds(i * TC, TC), HD * c:HD * c + HD, :, :].rearrange("c d h k -> (d h) c k"),
                                     kparts[:, c, a, :].rearrange("p (c k) -> p c k", c=TC)).then_inc(k_out, 16)

            def store_v(i):
                sp.wait_ge(v_ev, i * TC + TC)
                for m in range(2):
                    sp.dma_start(v_scr[m, :, bass.ds(i * TC, TC), :],
                                 v_next[:, :, m, :, :].rearrange("p c h v -> p c (h v)")).then_inc(v_out, 16)

            load_ctx(0, TC)
            with sp.Fori(0, NTILE - 2) as i:
                sp.wait_ge(ct_ps, i + 1)
                load_ctx(i + 1, TC)
                store_k(i)
                store_v(i)
            sp.wait_ge(ct_ps, NTILE - 1)
            load_ctx(NTILE - 1, TC - 1)
            for i in (NTILE - 2, NTILE - 1):
                store_k(i)
                store_v(i)
            sp.wait_ge(rows_out, 16 * (SPLIT * 3 + 6))

            for a in range(3):
                if ATT[a] == "L1":
                    for i in range(2):
                        sp.wait_ge(k_act, NTILE + i + 1)
                        sp.wait_ge(k_part2, NTILE + i + 1)
                        sp.wait_ge(k_part3, NTILE + i + 1)
                        for c in range(SPLIT):
                            sp.dma_start(ks[1, NC + 4 * i:NC + 4 * i + 4, HD * c:HD * c + HD, :, :].rearrange("c d h k -> (d h) c k"),
                                         xk_part(i, c).rearrange("p (c k) -> p c k", c=4)).then_inc(k_out, 16)
                sp.wait_ge(q_act, a + 1)
                sp.wait_ge(q_split, a + 1)
                for c in range(SPLIT):
                    sp.dma_start(q_scr[c], qparts[:, c, :]).then_inc(q_out, 16)
                sp.wait_ge(bound_ready, a + 1)
                sp.dma_start(bound_row[0:1, :], bound[32 * a:32 * a + H, 0:1]).then_inc(bound_in, 16)
                sp.wait_ge(q_out, 16 * SPLIT * (a + 1))
                for c in range(SPLIT):
                    for r in range(SPLIT):
                        row = KROWS * c + HD * r
                        sp.dma_start(qs[row:row + HD, :, :], q_scr[c].rearrange("(d h) n -> d h n", d=HD)).then_inc(qs_in, 16)
                sp.dma_start(qs[SPLIT * KROWS:SROWS, :, :], row_scr.rearrange("r (h n) -> r h n", h=H)).then_inc(qs_in, 16)
                sp.wait_ge(qs_in, 16 * 10 * (a + 1))
                sp.wait_ge(k_out, 16 * (9 * NTILE + (2 * SPLIT if a >= 1 else 0)))

                def load_keys(b, c, hh, done):
                    h0 = hh * (H // 2)
                    parts = ks[a, bass.ds(c, 1), 0:KROWS, h0:h0 + H // 2, :].rearrange("c r h k -> (c r) (h k)")
                    sp.dma_start(kr[b][0:SPLIT * KROWS, :, :].rearrange("r h k -> r (h k)"),
                                 parts.unsqueeze(0).to_broadcast([SPLIT, KROWS, H // 2 * P])).then_inc(done, 16)
                    rows = ks[a, bass.ds(c, 1), KROWS:KROWS + SPLIT + 1, h0:h0 + H // 2, :].rearrange("c r h k -> (c r) (h k)")
                    sp.dma_start(kr[b][SPLIT * KROWS:SROWS, :, :].rearrange("r h k -> r (h k)"), rows).then_inc(done, 16)

                sp.wait_ge(flag_ready, a + 1)
                need_max = sp.value_load(flag[0:1, a:a + 1], min_val=0, max_val=1)
                with sp.If(need_max > 0):
                    for hh in range(2):
                        q0 = 4 * hh * (NC + (NT if a == 1 else 0))
                        if hh:
                            sp.wait_ge(mx_ps[a], q0)
                        load_keys(0, 0, hh, mx_in[a])
                        with sp.Fori(1, NC) as c:
                            sp.wait_ge(mx_ps[a], q0 + 4 * c)
                            load_keys(0, c, hh, mx_in[a])
                        for c in range(NC, NC + (NT if a == 1 else 0)):
                            sp.wait_ge(mx_ps[a], q0 + 4 * c)
                            load_keys(0, c, hh, mx_in[a])
                    sp.wait_ge(mx_dve[a], 1)
                    for c in range(SPLIT):
                        sp.dma_start(m_scr[c], mparts[:, c, :]).then_inc(mx_out[a], 16)
                    sp.wait_ge(mx_out[a], 16 * SPLIT)
                    sp.dma_start(qs[SPLIT * KROWS:SPLIT * KROWS + SPLIT, :, :],
                                 m_scr.rearrange("c (h t) k -> c h (t k)", h=H)).then_inc(mx_out[a], 16)
                    sp.wait_ge(mx_out[a], 16 * SPLIT + 16)
                sp.end_ifs()

                for s in SWEEPS[4 * a:4 * a + 4]:
                    for c in range(TC):
                        if s.w:
                            sp.wait_ge(s_ready, s.pairs + (4 * c - 8 if s.aligned else 0))
                        load_keys(c, c, s.hh, kr_in[c])
                    with sp.Fori(1, NTILE) as i:
                        for b in range(TC):
                            sp.wait_ge(s_ready, i * (4 * TC) + (s.pairs + 4 * b - 8))
                            load_keys(b, i * TC + b, s.hh, kr_in[b])
                    for c in range(NC, s.n):
                        sp.wait_ge(s_ready, s.pairs + 4 * c - 8)
                        load_keys(c % TC, c, s.hh, kr_in[c % TC])
                end = SWEEPS[4 * a + 3]
                sp.wait_ge(s_ready, end.pairs + 4 * end.n)
                if a < 2:
                    sp.wait_ge(v_copied, SWEEPS[4 * a + 3].chunks + SWEEPS[4 * a + 3].n)
                    sp.wait_ge(v_out, 32 * NTILE)
                    sp.dma_start(vs[:, 0:NC, :, :].rearrange("p c h v -> p c (h v)"), v_scr[a]).then_inc(v_in, 16)
                between_sp(sp, a)
            sp.wait_ge(x_ready, 8)
            sp.dma_start(out[0].rearrange("(n p) d -> p n d", p=P), x[:, :, :]).then_inc(x_out, 16)
            sp.wait_ge(x_out, 16)

        @block.gpsimd
        def _(pool):
            g = nc.gpsimd
            chain = Chain(pool, pool_c)
            chain(g.memset(ident[:, :], 0.0))
            chain(g.affine_select(out=ident[:, :], in_=ident[:, :], compare_op=ALU.not_equal, fill=1.0,
                                  base=0, pattern=[[-1, P]], channel_multiplier=1))
            chain(g.tensor_copy(ident_b[:, :], ident[:, :]))
            chain(g.memset(head_of[:, :], 0.0))
            for d in range(HD):
                chain(g.affine_select(out=head_of[:, :], in_=head_of[:, :], compare_op=ALU.not_equal, fill=1.0,
                                      base=-H * d, pattern=[[-1, 32]], channel_multiplier=1))
            chain(g.memset(head_of[:, H:32], 0.0))
            chain(g.memset(stair[:, :], 0.0))
            chain(g.affine_select(out=stair[:, :], in_=stair[:, :], compare_op=ALU.is_ge, fill=-BIG,
                                  base=-384, pattern=[[1, 896]], channel_multiplier=-1))
            chain(g.memset(upper[:, :], 0.0))
            chain(g.affine_select(out=upper[:, :], in_=upper[:, :], compare_op=ALU.is_ge, fill=-BIG,
                                  base=0, pattern=[[-1, P]], channel_multiplier=1))
            g.memset(ones_row[:, :], 1.0)
            g.memset(zero_one[:, 0, :], 0.0)
            g.memset(zero_one[:, 1, :], 1.0)
            chain(g.memset(valid[:, :], 1.0))
            chain(g.affine_select(out=valid[:, :], in_=valid[:, :], compare_op=ALU.is_ge, fill=0.0,
                                  base=CTX - 1, pattern=[[-1, P]], channel_multiplier=-P))
            chain(g.memset(valid_last[:, :], 0.0))
            chain(g.memset(valid_last[0:LAST, :], 1.0))
            chain(g.memset(mask_u8[:, :], 0))
            chain(g.memset(c_last[:, :], 0.0))
            g.memset(bqk[:, :, :], 0.0)
            g.memset(b5[:, 1, :], 0.0)
            for b in range(TC):
                g.memset(vr[b][:, :, :], 0.0)
            const_pool(g, chain)
            chain(g.memset(kv_mask[:, :], 1.0))
            kvm = kv_mask[:, :].rearrange("p (h d) -> p h d", h=H)
            chain(g.affine_select(out=kvm, in_=kvm, compare_op=ALU.is_ge, fill=0.0,
                                  base=0, pattern=[[-HD, H], [0, HD]], channel_multiplier=1))
            chain(g.affine_select(out=kvm, in_=kvm, compare_op=ALU.is_ge, fill=0.0,
                                  base=HD - 1, pattern=[[HD, H], [0, HD]], channel_multiplier=-1))
            g.memset(v_next[:, :, :, :, HD:VC].rearrange("p c a h o -> p (c a h) o"), 1.0)
            g.memset(vs[:, :, :, HD:VC].rearrange("p c h o -> p (c h) o"), 1.0).then_inc(const_ready, 1)

            def third_parts(i, r1, p2, p3):
                pool.wait_ge(k_part2, i + 1)
                g.tensor_tensor(p3, r1, p2, ALU.subtract).then_inc(k_part3, 1)

            k1d = [kparts[:, c, :, :].rearrange("p a k -> p (a k)") for c in range(SPLIT)]
            k_restf = k_rest[:, :, :].rearrange("p a k -> p (a k)")
            third_parts(0, k_restf, k1d[1], k1d[2])
            with pool.Fori(1, NTILE) as i:
                pool.wait_ge(k_out, i * (16 * 9))
                third_parts(i, k_restf, k1d[1], k1d[2])

            for a in range(3):
                if ATT[a] == "L1":
                    for i in range(2):
                        if i == 0:
                            pool.wait_ge(k_out, 16 * 9 * NTILE)
                        cols = slice(512 * i, 512 * i + 512)
                        third_parts(NTILE + i, k_restf[:, cols], k1d[1][:, cols], k1d[2][:, cols])
                pool.wait_ge(v_final, a + 1)
                if ATT[a] == "L1":
                    pool.wait_ge(xv_ready, 1)
                for s in SWEEPS[4 * a:4 * a + 4]:
                    h0 = s.hh * (H // 2)

                    def copy_values(b, c):
                        g.tensor_copy(vr[b][:, :, 0:VC], vs[:, bass.ds(c, 1), h0:h0 + H // 2, :].rearrange("p o h v -> p (o h) v")).then_inc(v_copied, 1)

                    for c in range(TC):
                        if s.w:
                            pool.wait_ge(pv_done, s.groups + (2 * c - 4 if s.aligned else 0))
                        copy_values(c, c)
                    with pool.Fori(1, NTILE) as i:
                        for b in range(TC):
                            pool.wait_ge(pv_done, i * (2 * TC) + (s.groups + 2 * b - 4))
                            copy_values(b, i * TC + b)
                    for c in range(NC, s.n):
                        pool.wait_ge(pv_done, s.groups + 2 * c - 4)
                        copy_values(c % TC, c)
                between_pool(pool, a)

        @block.scalar
        def _(act):
            sc = nc.scalar
            chain = Chain(act, act_c)
            act.wait_ge(w_in, WEIGHTS_IN)
            sc.activation(gates[:, :], gates_raw[:, :], ACT.Tanh).then_inc(wprep_ready, 1)

            def k_step(i, first):
                act.wait_ge(ct_ps, i + 1)
                if not first:
                    act.wait_ge(v_ps, i * TC)
                sc.activation(c_T[:, :], PS[:, 0, 0:TW], ACT.Copy).then_inc(ct_ready, 1)
                act.wait_ge(k_ps, i + 1)
                if not first:
                    act.wait_ge(k_r1, i)
                    act.wait_ge(k_out, i * (16 * 9))
                    act.wait_ge(kn_ps, i)
                for a in range(3):
                    sc.activation(kf[:, a, :], PS[:, 1 + a, 0:TW], ACT.Identity, bias=bqk[:, 1, a:a + 1])
                    sc.activation(kparts[:, 0, a, :], PS[:, 1 + a, 0:TW], ACT.Identity, bias=bqk[:, 1, a:a + 1])
                    last = sc.activation(ksq[:, a, :], PS[:, 1 + a, 0:TW], ACT.Square, bias=bqk[:, 1, a:a + 1])
                last.then_inc(k_act, 1)

            k_step(0, True)
            with act.Fori(1, NTILE) as i:
                k_step(i, False)

            for a in range(3):
                ln_act(act, 2 * a + (a == 2) * 2)
                if ATT[a] == "L1":
                    for i in range(2):
                        act.wait_ge(k_ps, NTILE + i + 1)
                        if i == 0:
                            act.wait_ge(k_out, 16 * 9 * NTILE)
                        cols = slice(512 * i, 512 * i + 512)
                        flat = [v[:, :, :].rearrange("p a k -> p (a k)")[:, cols] for v in (kf, kparts[:, 0], ksq)]
                        sc.activation(flat[0], PS[:, 4 + i, :], ACT.Copy)
                        sc.activation(flat[1], PS[:, 4 + i, :], ACT.Copy)
                        sc.activation(flat[2], PS[:, 4 + i, :], ACT.Square).then_inc(k_act, 1)
                act.wait_ge(q_ps, a + 1)
                psq = PS[:, 2:4, :].rearrange("p b n -> p (b n)")
                sc.activation(qf, psq, ACT.Identity, bias=bqk[:, 0, a:a + 1])
                sc.activation(qparts[:, 0, :], psq, ACT.Identity, bias=bqk[:, 0, a:a + 1])
                sc.activation(qsq, psq, ACT.Square, bias=bqk[:, 0, a:a + 1]).then_inc(q_act, 1)

                for s in SWEEPS[4 * a:4 * a + 4]:
                    def exps(b, c, first=False):
                        for p in range(4):
                            act.wait_ge(s_ready, 4 * c + (s.pairs + p + 1))
                            if not (first and s.w == 0 and c < 1):
                                act.wait_ge(pv_done, 2 * c + (s.groups + p // 2 - 1))
                            slot = (b + p) % 3
                            sc.activation(prob[p][:, :, :], PS[:, 2 * slot:2 * slot + 2, :], ACT.Exp, scale=SCALE).then_inc(p_ready, 1)

                    for c in range(TC):
                        exps(c, c, True)
                    with act.Fori(1, NTILE) as i:
                        for b in range(TC):
                            exps(b, i * TC + b)
                    for c in range(NC, s.n):
                        exps(c % TC, c)
                act.wait_ge(atT_ps, a + 1)
                sc.activation(att_T[:, :], PS[:, 0:2, :].rearrange("p b n -> p (b n)"), ACT.Copy).then_inc(atT_ready, 1)
                between_act(act, a)

        @block.tensor
        def _(pe):
            te = nc.tensor
            pe.wait_ge(const_ready, 1)
            pe.wait_ge(w_in, WEIGHTS_IN)
            for i in range(3):
                last = te.transpose(PS[:, 0, i * D:(i + 1) * D], l2w[:, i, :], ident[:, :])
            last.then_inc(wprep_ps, 1)
            pe.wait_ge(rows_ready, 1)
            te.transpose(PS[:, 1, 0:64], mask_f[0:64, :], ident[0:64, 0:64]).then_inc(wprep_ps, 1)
            pe.wait_ge(f_in, SMALL_IN)
            te.transpose(PS[:, 2, 0:96], rows_w[0:96, :], ident[0:96, 0:96]).then_inc(f_cols_ps, 1)
            pe.wait_ge(wprep_ready, 4)
            pe.wait_ge(f_cols, 1)

            def k_step(i, first, tail):
                pe.wait_ge(c_loaded, i * 16 + 16)
                for b in range(TC):
                    src = c_last[:, :] if tail and b == TC - 1 else c_in[:, b, :]
                    if not first and b == 0:
                        pe.wait_ge(ct_ready, i)
                    last = te.transpose(PS[:, 0, b * P:(b + 1) * P], src, ident[:, :])
                last.then_inc(ct_ps, 1)
                pe.wait_ge(ct_ready, i + 1)
                if not first:
                    pe.wait_ge(k_act, i)
                for a in range(3):
                    last = te.matmul(PS[:, 1 + a, 0:TW], wk[:, a, :], c_T[:, :], start=True, stop=True)
                last.then_inc(k_ps, 1)

                def kv_product(b, n):
                    pe.wait_ge(v_ev, i * TC + (b + 1))
                    te.matmul(PS[:, 6, 0:P], kv2[0:n, b, 0:D], kv2[0:n, b, D:2 * D], start=(first and b == 0),
                              stop=True, skip_group_check=True).then_inc(kv_mm, 1)

                for b in range(TC):
                    if b:
                        pe.wait_ge(v_ev, i * TC + b)
                    elif not first:
                        pe.wait_ge(v_ev, i * TC)
                    cT = c_T[:, b * P:(b + 1) * P]
                    te.matmul(PS[:, 4, :], cT, wv5[:, 0:4, :].rearrange("p a d -> p (a d)"), start=True, stop=True)
                    te.matmul(PS[:, 5, 0:D], cT, wv5[:, 4, :], start=True, stop=True).then_inc(v_ps, 1)
                    if b:
                        kv_product(b - 1, P)
                kv_product(TC - 1, LAST if tail else P)
                pe.wait_ge(k_act, i + 1)
                if not first:
                    pe.wait_ge(kn_ev, i)
                for a in range(3):
                    last = te.matmul(PS[32 * a:32 * a + 32, 7, 0:TW], head_of[:, :], ksq[:, a, :], start=True, stop=True)
                last.then_inc(kn_ps, 1)

            k_step(0, True, False)
            with pe.Fori(1, NTILE - 1) as i:
                k_step(i, False, False)
            k_step(NTILE - 1, False, True)

            for a in range(3):
                k = 2 * a + (a == 2) * 2
                ln_pe(pe, k)
                if ATT[a] == "L1":
                    pe.wait_ge(ln_xT, k + 1)
                    for i in range(2):
                        te.matmul(PS[:, 4 + i, :], wk[:, a, :], xT[:, 512 * i:512 * i + 512], start=True, stop=True).then_inc(k_ps, 1)
                    for n in range(NT):
                        last = te.matmul(PS[:, 6 + n // 4, n % 4 * P:n % 4 * P + P], xT[:, n * P:(n + 1) * P], wv5[:, 1, :], start=True, stop=True)
                        if n % 4 == 3:
                            last.then_inc(v_ps, 1)
                    for i in range(2):
                        pe.wait_ge(k_act, NTILE + i + 1)
                        te.matmul(PS[0:32, i, :], head_of[:, :], ksq[:, :, :].rearrange("p a k -> p (a k)")[:, 512 * i:512 * i + 512],
                                  start=True, stop=True).then_inc(kn_ps, 1)
                pe.wait_ge(ln_xT, k + 1)
                for i in range(2):
                    last = te.matmul(PS[:, 2 + i, :], wq[:, a, :], xT[:, 512 * i:512 * i + 512], start=True, stop=True)
                last.then_inc(q_ps, 1)
                pe.wait_ge(q_act, a + 1)
                if ATT[a] == "L1":
                    pe.wait_ge(kn_ev, NTILE + 2)
                for i in range(2):
                    last = te.matmul(PS[32 * a:32 * a + 32, 4 + i, :], head_of[:, :], qsq[:, 512 * i:512 * i + 512], start=True, stop=True)
                last.then_inc(qn_ps, 1)

                pe.wait_ge(flag_ready, a + 1)
                need_max = pe.value_load(flag[0:1, a:a + 1], min_val=0, max_val=1)
                with pe.If(need_max > 0):
                    def max_scores(c, hh, q0, first=False, xc=None):
                        pe.wait_ge(mx_in[a], 32 * c + (32 * (q0 // 4) + 32))
                        for r in range(4):
                            if not (first and hh == 0 and r < 2):
                                pe.wait_ge(mx_red[a], 4 * c + (q0 + r - 1))
                            for e in range(2):
                                for n in range(0 if xc is None else xc, NT):
                                    o = PS[:, 4 * (r % 2) + 2 * e + n // 4, n % 4 * P:n % 4 * P + P]
                                    h = 2 * r + e
                                    diag = xc == n
                                    last = te.matmul(o, qs[:, hh * 8 + h, n * P:(n + 1) * P], kr[0][:, h, :], start=True, stop=not diag)
                                    if diag:
                                        last = te.matmul(o, ident_b[:, :], upper[:, :], start=False, stop=True)
                            last.then_inc(mx_ps[a], 1)

                    nx = NT if a == 1 else 0
                    for hh in range(2):
                        q0 = 4 * hh * (NC + nx)
                        max_scores(0, hh, q0, first=True)
                        with pe.Fori(1, NC) as c:
                            max_scores(c, hh, q0)
                        for xc in range(nx):
                            max_scores(NC + xc, hh, q0, xc=xc)
                    pe.wait_ge(mx_red[a], 8 * (NC + nx))
                    pe.wait_ge(mx_run[a], 8 * (NC + nx) - 8)
                    te.transpose(PS[:, 0, 0:P], run_max[:, :, :].rearrange("p h n -> p (h n)"), ident[:, :]).then_inc(mx_tp[a], 1)
                pe.end_ifs()

                for s in SWEEPS[4 * a:4 * a + 4]:
                    if s.w:
                        pe.wait_ge(p_ready, s.pairs)

                    def scores(b, c, j, loads, first=False, xc=None):
                        if j == 0:
                            pe.wait_ge(kr_in[b], loads)
                        if not (first and 4 * c + j < 3):
                            pe.wait_ge(p_ready, 4 * c + (s.pairs + j - 2))
                        for e in range(2):
                            h = 2 * j + e
                            o = PS[:, 2 * ((b + j) % 3) + e, :]
                            late = xc is not None and xc >= 4 * s.qh
                            last = te.matmul(o, kr[b][:, h, :], qs[:, s.hh * 8 + h, s.qh * 512:s.qh * 512 + 512], start=True, stop=not late)
                            if late:
                                off = 384 - P * (xc - 4 * s.qh)
                                last = te.matmul(o, ident_b[:, :], stair[:, off:off + 512], start=False, stop=True)
                        last.then_inc(s_ready, 1)

                    def values(b, c, g, first=False):
                        if g == 0:
                            pe.wait_ge(v_copied, c + (s.chunks + 1))
                        pe.wait_ge(p_ready, 4 * c + (s.pairs + 2 * g + 2))
                        if first and c == 0 and s.w:
                            pe.wait_ge(acc_ev, s.w)
                        for j in range(4):
                            last = te.matmul(PS[32 * j:32 * j + 32, 6 + g, :], vr[b][:, 4 * g + j, :], prob[2 * g + j // 2][:, j % 2, :],
                                             start=(first and c == 0), stop=True, skip_group_check=True)
                        last.then_inc(pv_done, 1)

                    for c in range(TC):
                        ld = 32 * (s.ring[c] + 1)
                        scores(c, c, 0, ld, True)
                        scores(c, c, 1, ld, True)
                        if c:
                            values(c - 1, c - 1, 1, True)
                        scores(c, c, 2, ld, True)
                        scores(c, c, 3, ld, True)
                        values(c, c, 0, True)
                    with pe.Fori(1, NTILE) as i:
                        for b in range(TC):
                            c = i * TC + b
                            ld = i * 32 + 32 * (s.ring[b] + 1)
                            scores(b, c, 0, ld)
                            scores(b, c, 1, ld)
                            values((b - 1) % TC, i * TC + (b - 1), 1)
                            scores(b, c, 2, ld)
                            scores(b, c, 3, ld)
                            values(b, c, 0)
                    for c in range(NC, s.n):
                        b = c % TC
                        ld = 32 * (s.ring[b] + c // TC + 1)
                        scores(b, c, 0, ld, xc=c - NC)
                        scores(b, c, 1, ld, xc=c - NC)
                        values((b - 1) % TC, c - 1, 1)
                        scores(b, c, 2, ld, xc=c - NC)
                        scores(b, c, 3, ld, xc=c - NC)
                        values(b, c, 0)
                    values((s.n - 1) % TC, s.n - 1, 1)

                pe.wait_ge(acc_ev, NSW * (a + 1))
                for n in range(NT):
                    for g in range(4):
                        last = te.transpose(PS[:, n, g * P:(g + 1) * P], accs[:, g, n * P:(n + 1) * P], ident[:, :])
                    last.then_inc(at_ps, 1)
                for n in range(NT):
                    pe.wait_ge(at_rd, NT * a + max(n + 1, 2))
                    last = te.transpose(PS[:, n // 4, n % 4 * P:n % 4 * P + P], att[:, n, :], ident[:, :])
                last.then_inc(atT_ps, 1)
                pe.wait_ge(atT_ready, a + 1)
                for n in range(NT):
                    o = PS[:, 2 + n // 4, n % 4 * P:n % 4 * P + P]
                    te.matmul(o, att_T[:, n * P:(n + 1) * P], wo[:, a, :], start=True, stop=False)
                    last = te.matmul(o, ones_row[0:1, :], bo[0:1, a, :], start=False, stop=True)
                last.then_inc(y_ps, 1)
                between_pe(pe, a)

        @block.vector
        def _(dve):
            v = nc.vector
            chain = Chain(dve, dve_c)
            dve.wait_ge(w_in, WEIGHTS_IN)
            for a in range(3):
                v.tensor_copy(wk[:, a, :].rearrange("p (d h) -> p d h", d=HD), dh(wk_in[:, a, :]))
                last = v.tensor_copy(wq[:, a, :].rearrange("p (d h) -> p d h", d=HD), dh(wq_in[:, a, :]))
            last.then_inc(wprep_ready, 1)
            dve.wait_ge(const_ready, 1)
            dve.wait_ge(rows_in, 48)
            chain(v.tensor_copy(mask_f[:, :], mask_u8[:, :]))
            v.tensor_scalar(mask_rows[:, 0, :], valid[:, :], -1.0, BIG, ALU.add, ALU.mult)
            v.tensor_scalar(mask_rows[:, 1, :], mask_f[:, :], -1.0, BIG, ALU.add, ALU.mult).then_inc(rows_ready, 1)
            dve.wait_ge(wprep_ps, 2)
            v.tensor_copy(wv5[:, 3:5, :].rearrange("p a d -> p (a d)"), PS[:, 0, 0:2 * D])
            v.tensor_copy(l2wq[:, :], PS[:, 0, 2 * D:3 * D]).then_inc(wprep_ready, 1)
            v.tensor_copy(mask_T[:, :], PS[:, 1, 0:64]).then_inc(wprep_ready, 1)
            dve.wait_ge(f_cols_ps, 1)
            v.tensor_copy(cols_w[:, :], PS[:, 2, 0:96]).then_inc(f_cols, 1)

            def k_step(i, first):
                dve.wait_ge(k_act, i + 1)
                if not first:
                    dve.wait_ge(k_part3, i)
                    dve.wait_ge(k_out, i * (16 * 9))
                v.tensor_tensor(k_rest[:, :, :], kf[:, :, :], kparts[:, 0, :, :], ALU.subtract).then_inc(k_r1, 1)
                dve.wait_ge(k_r1, i + 1)
                v.tensor_copy(kparts[:, 1, :, :], k_rest[:, :, :]).then_inc(k_part2, 1)
                for b in range(TC):
                    dve.wait_ge(v_ps, i * TC + (b + 1))
                    if not first:
                        dve.wait_ge(kv_mm, i * TC + (b - 2))
                        dve.wait_ge(v_out, i * 32)
                    for o, m in ((vs[:, bass.ds(i * TC + b, 1), :, 0:HD].rearrange("p o h d -> p (o h) d"), slice(0, 1)),
                                 (v_next[:, b, :, :, 0:HD].rearrange("p a h d -> p (a h) d"), slice(1, 3))):
                        v.tensor_tensor(o, PS[:, 4, m.start * D:m.stop * D].rearrange("p (m d) -> p m d", d=HD),
                                        b5[:, m, :].rearrange("p a (h d) -> p (a h) d", d=HD), ALU.add)
                    v.tensor_tensor(kv2[:, b, :], PS[:, 4:6, :].rearrange("p b n -> p (b n)")[:, 3 * D:5 * D],
                                    b5[:, 3:5, :].rearrange("p a d -> p (a d)"), ALU.add).then_inc(v_ev, 1)
                dve.wait_ge(kn_ps, i + 1)
                v.reduce_max(kmax[0:96, bass.ds(i, 1)], PS[0:96, 7, 0:TW], X_AXIS).then_inc(kn_ev, 1)

            k_step(0, True)
            with dve.Fori(1, NTILE) as i:
                k_step(i, False)
            dve.wait_ge(v_ev, NTILE * TC)
            dve.wait_ge(kv_mm, NTILE * TC)
            v.tensor_tensor(kv_sum[:, :], PS[:, 6, 0:P], kv_mask[:, :], ALU.mult)
            dve.wait_ge(x_in, 16)

            for a in range(3):
                k = 2 * a + (a == 2) * 2
                if a:
                    dve.wait_ge(v_in, 16 * a)
                if ATT[a] == "L3":
                    flat = vs[:, 0:NC, :, :].rearrange("p c h v -> p c (h v)")
                    v.tensor_tensor(flat, flat, mask_T[:, 0:NC].unsqueeze(2).to_broadcast([P, NC, H * VC]), ALU.mult).then_inc(v_final, 1)
                else:
                    vl = vs[:, NC - 1, :, :]
                    v.tensor_scalar(vl, vl, valid_last[:, 0:1], None, ALU.mult).then_inc(v_final, 1)
                ln_dve(dve, chain, k)
                if ATT[a] == "L1":
                    for i in range(2):
                        cols = slice(512 * i, 512 * i + 512)
                        f = [w[:, :, :].rearrange("p a k -> p (a k)")[:, cols] for w in (kf, k_rest, kparts[:, 0], kparts[:, 1])]
                        dve.wait_ge(k_act, NTILE + i + 1)
                        if i == 0:
                            dve.wait_ge(k_part3, NTILE)
                            dve.wait_ge(k_out, 16 * 9 * NTILE)
                        v.tensor_tensor(f[1], f[0], f[2], ALU.subtract).then_inc(k_r1, 1)
                        dve.wait_ge(k_r1, NTILE + i + 1)
                        v.tensor_copy(f[3], f[1]).then_inc(k_part2, 1)
                    for i in range(2):
                        dve.wait_ge(v_ps, NC + i + 1)
                        last = v.tensor_copy(vs[:, NC + 4 * i:NC + 4 * i + 4, :, 0:HD],
                                             PS[:, 6 + i, :].rearrange("p (c h d) -> p c h d", c=4, h=H))
                    last.then_inc(xv_ready, 1)
                    for i in range(2):
                        dve.wait_ge(kn_ps, NTILE + i + 1)
                        v.reduce_max(kmax[0:32, NTILE + i:NTILE + i + 1], PS[0:32, i, :], X_AXIS).then_inc(kn_ev, 1)
                    dve.wait_ge(kn_ev, NTILE + 2)
                    chain(v.tensor_copy(kmax[32:64, NTILE:NTILE + 2], kmax[0:32, NTILE:NTILE + 2]))
                dve.wait_ge(q_act, a + 1)
                chain(v.tensor_tensor(qr1, qf, qparts[:, 0, :], ALU.subtract))
                chain(v.tensor_copy(qparts[:, 1, :], qr1))
                v.tensor_tensor(qparts[:, 2, :], qr1, qparts[:, 1, :], ALU.subtract).then_inc(q_split, 1)
                own = slice(32 * a, 32 * a + 32)
                dve.wait_ge(qn_ps, a + 1)
                dve.wait_ge(kn_ev, NTILE)
                v.reduce_max(q_max[own, :], PS[own, 4:6, :].rearrange("p b n -> p (b n)"), X_AXIS)
                chain(v.reduce_max(k_max[own, :], kmax[own, 0:NTILE + (2 if a == 1 else 0)], X_AXIS))
                v.tensor_tensor(bound[own, :], q_max[own, :], k_max[own, :], ALU.mult).then_inc(bound_ready, 1)
                dve.wait_ge(bound_in, 16 * (a + 1))
                chain(v.reduce_max(bound_max[:, :], bound_row[:, :], X_AXIS))
                v.tensor_scalar(flag[0:1, a:a + 1], bound_max[:, :], (SAFE / SCALE) ** 2, None, ALU.is_ge).then_inc(flag_ready, 1)
                dve.wait_ge(flag_ready, a + 1)
                need_max = dve.value_load(flag[0:1, a:a + 1], min_val=0, max_val=1)
                with dve.If(need_max > 0):
                    def reduce_scores(c, hh, q0, first=False, xc=0):
                        for r in range(4):
                            ps = PS[:, 4 * (r % 2):4 * (r % 2) + 4, :].rearrange("p b (n k) -> p (b n) k", k=P).rearrange("p (e n) k -> p e n k", e=2)[:, :, xc:, :]
                            run = run_max[:, hh * 8 + 2 * r:hh * 8 + 2 * r + 2, xc:]
                            new = new_max[:, :].rearrange("p (e n) -> p e n", e=2)[:, :, xc:]
                            dve.wait_ge(mx_ps[a], 4 * c + (q0 + r + 1))
                            if first:
                                v.reduce_max(run, ps, X_AXIS).then_inc(mx_red[a], 1)
                                dve.wait_ge(mx_red[a], 4 * c + (q0 + r + 1))
                            else:
                                v.reduce_max(new, ps, X_AXIS).then_inc(mx_red[a], 1)
                                dve.wait_ge(mx_red[a], 4 * c + (q0 + r + 1))
                                v.tensor_tensor(run, run, new, ALU.max).then_inc(mx_run[a], 1)
                                dve.wait_ge(mx_run[a], 4 * c + (q0 - 4 * hh - 3 + r))

                    nx = NT if a == 1 else 0
                    for hh in range(2):
                        q0 = 4 * hh * (NC + nx)
                        reduce_scores(0, hh, q0, first=True)
                        with dve.Fori(1, NC) as c:
                            reduce_scores(c, hh, q0)
                        for xc in range(nx):
                            reduce_scores(NC + xc, hh, q0, xc=xc)
                    dve.wait_ge(mx_tp[a], 1)
                    n0 = 8 * (NC + nx) - 8
                    for i, (o, i0, i1) in enumerate(((mneg, None, None), (mparts[:, 0], mneg, None), (mr1, mneg, mparts[:, 0]),
                                                     (mparts[:, 1], mr1, None), (mparts[:, 2], mr1, mparts[:, 1]))):
                        if i == 0:
                            ins = v.tensor_scalar(o[:, :], PS[:, 0, 0:P], -1.0, None, ALU.mult)
                        elif i1 is None:
                            ins = v.tensor_copy(o[:, :], i0[:, :])
                        else:
                            ins = v.tensor_tensor(o[:, :], i0[:, :], i1[:, :], ALU.subtract)
                        if i == 4:
                            ins.then_inc(mx_dve[a], 1)
                        else:
                            ins.then_inc(mx_run[a], 1)
                            dve.wait_ge(mx_run[a], n0 + i + 1)
                dve.end_ifs()

                for s in SWEEPS[4 * a:4 * a + 4]:
                    dve.wait_ge(pv_done, s.groups + 2 * s.n)
                    v.tensor_copy(accs[:, 2 * s.hh:2 * s.hh + 2, 512 * s.qh:512 * s.qh + 512], PS[:, 6:8, :]).then_inc(acc_ev, 1)
                for n in range(NT):
                    dve.wait_ge(at_ps, NT * a + n + 1)
                    heads = PS[:, n, :].rearrange("p (h w) -> p h w", w=32)
                    chain(v.reciprocal(rden[:, n, :].unsqueeze(2), heads[:, :, HD:VC]))
                    v.tensor_tensor(att[:, n, :].rearrange("p (h d) -> p h d", h=H), heads[:, :, 0:HD],
                                    rden[:, n, :].unsqueeze(2).to_broadcast([P, H, HD]), ALU.mult).then_inc(at_rd, 1)
                add_to_x(dve, (0, 1, 3)[a], PS[:, 2:4, :].rearrange("p b n -> p (b n)"), y_ps, a + 1, k)
                between_dve(dve, chain, a)


def kernel(**inputs):
    import numpy as _np
    import concourse.bacc as _bacc
    from concourse import mybir as _mybir
    from concourse.bass_utils import run_bass_kernel_spmd as _run

    nc = _bacc.Bacc("TRN2", target_bir_lowering=False, num_devices=1)
    arrays, t = {}, {}
    for name, value in inputs.items():
        a = _np.ascontiguousarray(value)
        arrays[f"in_{name}"] = a
        t[name] = nc.dram_tensor(f"in_{name}", a.shape, _mybir.dt.from_np(a.dtype), kind="ExternalInput").ap()
    out = nc.dram_tensor("out", (1, S, D), F32, kind="ExternalOutput").ap()
    ks = nc.dram_tensor("key_parts", (3, NC + NT, KROWS + SPLIT + 1, H, P), BF16, kind="Internal").ap()
    v_scr = nc.dram_tensor("values", (2, P, NC, H * VC), F32, kind="Internal").ap()
    q_scr = nc.dram_tensor("query_parts", (SPLIT, P, S), BF16, kind="Internal").ap()
    m_scr = nc.dram_tensor("maximum_parts", (SPLIT, P, P), BF16, kind="Internal").ap()
    row_scr = nc.dram_tensor("constant_rows", (SPLIT + 1, H * S), BF16, kind="Internal").ap()
    flamingo_decoder(nc, t, out, ks, v_scr, q_scr, m_scr, row_scr)
    r = _run(nc, [arrays], core_ids=[0])
    return r.results[0]["out"]
```

```python
from contextlib import ExitStack

import concourse.bass as bass
from concourse import mybir

F32 = mybir.dt.float32
BF16 = mybir.dt.bfloat16
I32 = mybir.dt.int32
U8 = mybir.dt.uint8
ALU = mybir.AluOpType
ACT = mybir.ActivationFunctionType
X_AXIS = mybir.AxisListType.X

P = 128
S = 1024
D = 128
NT = S // P
CTX = 6404
H = 16
HD = D // H
NC = -(-CTX // P)
LAST = CTX - (NC - 1) * P
TC = 3
NTILE = NC // TC
TW = TC * P
UNROLL = 4
SPLIT = 3
KROWS = SPLIT * HD
SROWS = SPLIT * KROWS + SPLIT + 1
SCALE = float(HD) ** -0.5
BIG = 1e30
SAFE = 60.0
LN_EPS = 1e-5
VC = HD + 1
ATT = ("L0", "L1", "L3")
NSW = 4
WEIGHTS_IN = 16 * (6 + 4 + 4 + 1)
WEIGHTS_LATE = 16 * (9 + 3 + 2)
assert NTILE * TC == NC and (NTILE - 1) % UNROLL == 0 and SROWS <= P


class Chain:

    def __init__(self, eng, sem):
        self.eng, self.sem, self.n = eng, sem, 0

    def __call__(self, ins):
        ins.then_inc(self.sem, 1)
        self.n = self.n + 1
        self.eng.wait_ge(self.sem, self.n)


class Sweep:

    def __init__(self, w, a, hh, qh, nx, before):
        self.w, self.a, self.hh, self.qh, self.nx = w, a, hh, qh, nx
        self.n = NC + nx
        self.chunks = sum(s.n for s in before)
        self.pairs = 4 * self.chunks
        self.groups = 2 * self.chunks
        self.ring = [sum(-(-(s.n - b) // TC) for s in before) for b in range(TC)]
        self.aligned = all(s.n % TC == 0 for s in before[-1:])


SWEEPS = []
for _a in range(len(ATT)):
    for _hh in range(2):
        for _qh in range(2):
            _nx = (NT // 2) * (_qh + 1) if ATT[_a] == "L1" else 0
            SWEEPS.append(Sweep(len(SWEEPS), _a, _hh, _qh, _nx, SWEEPS))


def flamingo_decoder(nc, t, out, ks, v_scr, q_scr, m_scr, row_scr):
    with ExitStack() as ctx:
        def sb(name, shape, dt=F32):
            return ctx.enter_context(nc.sbuf_tensor(name, shape, dt))

        def sem(name):
            return ctx.enter_context(nc.semaphore(name))

        PS = ctx.enter_context(nc.psum_tensor("PS", [P, 8, 512], F32))

        ident = sb("ident", [P, P])
        ident_b = sb("ident_b", [P, P], BF16)
        head_of = sb("head_of", [P, 32])
        stair = sb("stair", [P, 384 + 512], BF16)
        upper = sb("upper", [P, P], BF16)
        ones_row = sb("ones_row", [1, P])
        zero_one = sb("zero_one", [P, 2, P], BF16)
        valid = sb("valid", [64, P])
        valid_last = sb("valid_last", [P, 1])
        wk_in = sb("wk_in", [P, 3, D])
        wk = sb("wk", [P, 3, D])
        wq_in = sb("wq_in", [P, 3, D])
        wq = sb("wq", [P, 3, D])
        wo = sb("wo", [P, 3, D])
        bo = sb("bo", [1, 3, D])
        bqk = sb("bqk", [P, 2, 3])
        wv5 = sb("wv5", [P, 5, D])
        l2w = sb("l2w", [P, 3, D])
        l2wq = sb("l2wq", [P, D])
        b5 = sb("b5", [P, 5, D])
        gates_raw = sb("gates_raw", [P, 8])
        gates = sb("gates", [P, 8])
        c_in0 = sb("c_in0", [P, TC, D + 1])
        c_last = sb("c_last", [P, D + 1])
        c_T0 = sb("c_T0", [P, TW])
        kf = sb("kf", [P, TC, 3, P])
        k_rest = sb("k_rest", [P, TC, 3, P])
        ksq = sb("ksq", [P, 3, TW])
        kparts = sb("kparts", [P, SPLIT, TC, 3, P], BF16)
        gram = sb("gram", [P, D + 1])
        sum_bk = sb("sum_bk", [P, D])
        n_bv = sb("n_bv", [1, D])
        gram_v = sb("gram_v", [P, D])
        vs = sb("vs", [P, NC + NT, H, VC])
        v_next = sb("v_next", [P, TC, 2, H, VC])
        kmax = sb("kmax", [P, NTILE + 2])
        mask_u8 = sb("mask_u8", [64, P], U8)
        mask_f = sb("mask_f", [64, P])
        mask_rows = sb("mask_rows", [64, 2, P], BF16)
        mask_T = sb("mask_T", [P, 64])
        kv_mask = sb("kv_mask", [P, P])
        kv_sum = sb("kv_sum", [P, P])
        x = sb("x", [P, NT, D])
        xn = sb("xn", [P, NT, D])
        xT = sb("xT", [P, S])
        ln_st = sb("ln_st", [P, NT, 6])
        ln_mv = sb("ln_mv", [P, NT, 2])
        ln_ve = sb("ln_ve", [P, NT])
        ln_sd = sb("ln_sd", [P, NT])
        ln_rs = sb("ln_rs", [P, NT])
        accs = sb("accs", [P, 4, S])
        qf, qr1, qsq = (accs[:, i, :] for i in range(3))
        qparts = sb("qparts", [P, SPLIT, S], BF16)
        q_max = sb("q_max", [P, 1])
        k_max = sb("k_max", [P, 1])
        bound = sb("bound", [P, 1])
        bound_row = sb("bound_row", [1, H])
        bound_max = sb("bound_max", [1, 1])
        flag = sb("flag", [1, 3], I32)
        wide = sb("wide", [P, H, S], BF16)
        qs = wide[0:SROWS, :, :]
        kr = [sb(f"kr{b}", [SROWS, H // 2, P], BF16) for b in range(TC)]
        vr = [sb(f"vr{b}", [P, H // 2, 32]) for b in range(TC)]
        probs = sb("probs", [P, 4, 2, 512])
        prob = [probs[:, i] for i in range(4)]
        spare = probs[:, :, :, :].rearrange("p i e n -> p (i e n)")
        spare2 = accs[:, :, :].rearrange("p g n -> p (g n)")
        at_v = SPLIT * 3 * TW // 2
        kparts2 = [kparts[:, :, :, :, :], spare[:, 0:at_v].bitcast(BF16).rearrange("p (s c a k) -> p s c a k", s=SPLIT, c=TC, a=3)]
        v_next2 = [v_next[:, :, :, :, :], spare[:, at_v:at_v + TC * 2 * H * VC].rearrange("p (c a h v) -> p c a h v", c=TC, a=2, h=H)]
        kf2 = [kf[:, :, :, :], spare2[:, 0:3 * TW].rearrange("p (c a k) -> p c a k", c=TC, a=3)]
        at_c = [3 * TW + TC * (D + 1) * i for i in range(UNROLL)]
        c_in = [c_in0[:, :, :]] + [spare2[:, o:o + TC * (D + 1)].rearrange("p (c d) -> p c d", c=TC) for o in at_c[:-1]]
        c_T = [c_T0[:, :], spare2[:, at_c[-1]:at_c[-1] + TW]]
        rden = sb("rden", [P, NT, H])
        att, att_T = xn, xT
        run_max = sb("run_max", [P, H, NT])
        new_max = sb("new_max", [P, 2 * NT])
        mneg = sb("mneg", [P, P])
        mr1 = sb("mr1", [P, P])
        mparts = sb("mparts", [P, SPLIT, P], BF16)

        first_const = sem("first_const")
        const_ready = sem("const_ready")
        w_in = sem("w_in")
        w_late = sem("w_late")
        rows_in = sem("rows_in")
        rows_ready = sem("rows_ready")
        rows_out = sem("rows_out")
        wprep_ps = sem("wprep_ps")
        wprep_ready = sem("wprep_ready")
        c_loaded = [sem(f"c_loaded{b}") for b in range(UNROLL)]
        ct_ps = sem("ct_ps")
        ct_ready = sem("ct_ready")
        k_ps = sem("k_ps")
        k_act = sem("k_act")
        k_r1 = sem("k_r1")
        k_part2 = sem("k_part2")
        k_part3 = sem("k_part3")
        k_out = [sem(f"k_out{b}") for b in range(2)]
        v_ps = sem("v_ps")
        v_ev = sem("v_ev")
        gram_mm = sem("gram_mm")
        gram_sb = sem("gram_sb")
        gram_ps = sem("gram_ps")
        kn_ps = sem("kn_ps")
        kn_ev = sem("kn_ev")
        v_out = [sem(f"v_out{b}") for b in range(2)]
        v_in = sem("v_in")
        v_final = sem("v_final")
        xv_ready = sem("xv_ready")
        x_in = sem("x_in")
        x_ready = sem("x_ready")
        x_out = sem("x_out")
        ln_var = sem("ln_var")
        ln_root = sem("ln_root")
        ln_xn = sem("ln_xn")
        ln_ps = sem("ln_ps")
        ln_xT = sem("ln_xT")
        q_ps = sem("q_ps")
        q_act = sem("q_act")
        q_split = sem("q_split")
        qn_ps = sem("qn_ps")
        bound_ready = sem("bound_ready")
        bound_in = sem("bound_in")
        flag_ready = sem("flag_ready")
        q_out = sem("q_out")
        qs_in = sem("qs_in")
        kr_in = [sem(f"kr_in{b}") for b in range(TC)]
        v_copied = sem("v_copied")
        s_ready = sem("s_ready")
        p_ready = sem("p_ready")
        pv_done = sem("pv_done")
        acc_ev = sem("acc_ev")
        at_ps = sem("at_ps")
        at_rd = sem("at_rd")
        atT_ps = sem("atT_ps")
        atT_ready = sem("atT_ready")
        y_ps = sem("y_ps")
        mx_in = [sem(f"mx_in{a}") for a in range(3)]
        mx_ps = [sem(f"mx_ps{a}") for a in range(3)]
        mx_red = [sem(f"mx_red{a}") for a in range(3)]
        mx_tp = [sem(f"mx_tp{a}") for a in range(3)]
        mx_run = [sem(f"mx_run{a}") for a in range(3)]
        mx_dve = [sem(f"mx_dve{a}") for a in range(3)]
        mx_out = [sem(f"mx_out{a}") for a in range(3)]
        dve_c = sem("dve_c")
        act_c = sem("act_c")
        pool_c = sem("pool_c")

        block = ctx.enter_context(nc.Block())

        def dh(ap):
            return ap.rearrange("p (h d) -> p d h", h=H)

        def norm(dve, chain, src, dst, j):
            v = nc.vector
            for n in range(NT):
                last = v.bn_stats(ln_st[:, n, :], src[:, n, :])
            chain(last)
            for n in range(NT):
                last = v.bn_aggr(ln_mv[:, n, :], ln_st[:, n, :])
            chain(last)
            v.tensor_scalar(ln_ve[:, :], ln_mv[:, :, 1], LN_EPS, None, ALU.add).then_inc(ln_var, 1)
            dve.wait_ge(ln_root, j + 1)
            chain(v.reciprocal(ln_rs[:, :], ln_sd[:, :]))
            for n in range(NT):
                last = v.tensor_scalar(dst[:, n, :], src[:, n, :], ln_mv[:, n, 0:1], ln_rs[:, n:n + 1], ALU.subtract, ALU.mult)
            return last

        def norm_at(k):
            return k + (k >= 5)

        def ln_dve(dve, chain, k):
            if k:
                dve.wait_ge(x_ready, k)
            norm(dve, chain, x, xn, norm_at(k)).then_inc(ln_xn, 1)

        def ln_act(act, k):
            act.wait_ge(ln_var, norm_at(k) + 1)
            nc.scalar.activation(ln_sd[:, :], ln_ve[:, :], ACT.Sqrt).then_inc(ln_root, 1)
            act.wait_ge(ln_ps, k + 1)
            nc.scalar.activation(xT[:, :], PS[:, 0:2, :].rearrange("p b n -> p (b n)"), ACT.Copy).then_inc(ln_xT, 1)

        def ln_pe(pe, k):
            pe.wait_ge(ln_xn, k + 1)
            for n in range(NT):
                last = nc.tensor.transpose(PS[:, n // 4, n % 4 * P:n % 4 * P + P], xn[:, n, :], ident[:, :])
            last.then_inc(ln_ps, 1)

        def add_to_x(dve, gate, y, y_sem, val, k):
            dve.wait_ge(y_sem, val)
            xf = x[:, :, :].rearrange("p n d -> p (n d)")
            nc.vector.scalar_tensor_tensor(xf, y, gates[:, gate:gate + 1], xf, ALU.mult, ALU.add).then_inc(x_ready, 1)

        NODES, LEAVES, DEPTH = 15, 16, 4
        HC = LEAVES * 64 // P
        NETS = ("q", "k", "v")
        FSCALE = float(D) ** -0.5
        wide32 = wide[:, :, :].rearrange("p h n -> p (h n)").bitcast(F32)
        accs_flat = accs[:, :, :].rearrange("p g n -> p (g n)")
        probs_flat = probs[:, :, :, :].rearrange("p i e n -> p (i e n)")
        fw1 = [wide32[:, S * n:S * n + S] for n in range(3)]
        fw2 = [wide32[:, S * (3 + n):S * (4 + n)] for n in range(3)]
        rows_w = sb("rows_w", [96, P])
        cols_w = sb("cols_w", [P, 96])
        B1_AT, RMS_AT = 3 * NODES, 3 * NODES + 3 * HC
        node_b = sb("node_b", [P, 3 * NODES])
        leaf_b2 = sb("leaf_b2", [96, 3, D])
        leaf_sel = sb("leaf_sel", [96, HC, P], BF16)
        bits = sb("bits", [P, NT * 3, NODES])
        paths = [None] + [sb(f"path{l}", [P, NT * 3, 2 ** l]) for l in range(1, DEPTH)]
        leaf = sb("leaf", [P, NT * 3, 32])
        leaf_T = wide32[0:96, 6 * S:7 * S]
        leaf_Tb = wide32[0:96, 7 * S:7 * S + S // 2].bitcast(BF16)
        hid = [probs_flat[:, 512 * r:512 * r + 512] for r in range(4)]
        qkv = [accs[:, n, :] for n in range(3)]
        v_tok = accs[:, 3, :]
        prob_q = [probs_flat[:, S * i:S * i + S] for i in range(2)]
        prob_T = [probs_flat[:, S * (2 + i):S * (3 + i)] for i in range(2)]
        fmax = sb("fmax", [P, NT])
        fneg = sb("fneg", [P, NT])
        fden = sb("fden", [P, NT])
        frec = sb("frec", [P, NT])
        E1, E1S, HID1 = 14, 2, 256
        E2, E3, HID3, CAP = 8, 8, 512, 64
        rw1 = sb("rw1", [P, E1])
        rw3 = sb("rw3", [P, E3])
        countdown = sb("countdown", [P, LEAVES])
        tri = sb("tri", [P, P])
        ones = sb("ones", [P, P])
        logit = sb("logit", [P, NT, E1])
        rprob = sb("rprob", [P, NT, E1])
        work = sb("work", [P, NT, E1])
        sel1 = sb("sel1", [P, NT, E1])
        sel2 = sb("sel2", [P, NT, E1])
        egate = sb("egate", [P, NT, E1 + E1S])
        rmax = sb("rmax", [P, NT])
        rsum = sb("rsum", [P, NT])
        l2bq = sb("l2bq", [P, 1])
        gamma_b = sb("gamma_b", [P, 2, D])
        h_T = ksq[:, :, :].rearrange("p a k -> p (a k)")[:, 0:S]
        moe_acc = kf[:, :, :, :].rearrange("p c a k -> p (c a k)")[:, 0:S]
        moe_hid = [probs_flat, accs_flat]
        eA = [wide32[:, 2048 * i:2048 * i + 512] for i in range(2)]
        eB = [wide32[:, 2048 * i + 512:2048 * i + 1024] for i in range(2)]
        eC = [wide32[:, 2048 * i + 1024:2048 * i + 1536] for i in range(2)]

        f_in = sem("f_in")
        fw_in = sem("fw_in")
        l2_normed = sem("l2_normed")
        f_cols_ps = sem("f_cols_ps")
        f_cols = sem("f_cols")
        f_node = sem("f_node")
        f_leaf = sem("f_leaf")
        f_leafT_ps = sem("f_leafT_ps")
        f_leafT = sem("f_leafT")
        f_up = sem("f_up")
        f_relu = sem("f_relu")
        f_masked = sem("f_masked")
        f_out = sem("f_out")
        f_net_ps = sem("f_net_ps")
        f_net = sem("f_net")
        f_v_ps = sem("f_v_ps")
        f_v = sem("f_v")
        fa_s = sem("fa_s")
        fa_max = sem("fa_max")
        fa_p = sem("fa_p")
        fa_T = sem("fa_T")
        fa_Tc = sem("fa_Tc")
        fa_o = sem("fa_o")
        r_ps = sem("r_ps")
        r_cen = sem("r_cen")
        r_exp = sem("r_exp")
        r_sel = sem("r_sel")
        r_cum = sem("r_cum")
        ms_ready = sem("ms_ready")
        ms_root = sem("ms_root")
        ht_sb = sem("ht_sb")
        ht_ps = sem("ht_ps")
        ht_ready = sem("ht_ready")
        e_in = [sem(f"e_in{i}") for i in range(2)]
        e_scaled = sem("e_scaled")
        h_ps = sem("h_ps")
        h_act = sem("h_act")
        h_mul = sem("h_mul")
        dn_ps = sem("dn_ps")
        dn_ev = sem("dn_ev")
        l2q_ps = sem("l2q_ps")
        l2q = sem("l2q")
        l2_ps = sem("l2_ps")

        class Moe:

            def __init__(self, n, chunks, up, func, scaled, gated, before):
                self.n, self.chunks, self.up, self.func, self.scaled, self.gated = n, chunks, up, func, scaled, gated
                self.units = 2 * chunks
                self.loads = 3 if up else 2
                self.e0 = sum(m.n for m in before)
                self.u0 = sum(m.n * m.units for m in before)
                self.mul0 = sum(m.n * m.units for m in before if m.up)
                self.in0 = sum(16 * m.loads * (m.n // 2) for m in before)
                self.ring = 2 if up else 4

        MOE = []
        MOE.append(Moe(E1 + E1S, HID1 // P, False, ACT.Silu, True, True, MOE[:]))
        MOE.append(Moe(E2, HID3 // P, True, ACT.Silu, False, False, MOE[:]))
        MOE.append(Moe(E3, HID3 // P, False, ACT.Gelu_apprx_tanh, False, True, MOE[:]))

        def late_weights(act):
            for n, net in enumerate(NETS):
                act.dma_start(rows_w[NODES * n:NODES * (n + 1), :], t[f"L0_ffn_{net}_node_w"][:, :]).then_inc(f_in, 16)
                act.dma_start(rows_w[B1_AT + HC * n:B1_AT + HC * (n + 1), :],
                             t[f"L0_ffn_{net}_b1"].rearrange("(c l) h -> c (l h)", c=HC)).then_inc(f_in, 16)
                act.dma_start(node_b[:, NODES * n:NODES * (n + 1)], t[f"L0_ffn_{net}_node_b"].partition_broadcast(P)).then_inc(f_in, 16)
                act.dma_start(leaf_b2[32 * n:32 * n + LEAVES, n, :], t[f"L0_ffn_{net}_b2"][:, :]).then_inc(f_in, 16)
            act.dma_start(rows_w[RMS_AT:RMS_AT + E1, :], t["L1_ffn_rms_w"][:, :]).then_inc(f_in, 16)
            act.dma_start(rows_w[RMS_AT + E1:RMS_AT + E1 + E1S, :], t["L1_ffn_rms_w_s"][:, :]).then_inc(f_in, 16)
            act.dma_start(rw1[:, :], t["L1_ffn_router_w"][:, :]).then_inc(f_in, 16)
            act.dma_start(rw3[:, :], t["L3_ffn_w_router"][:, :]).then_inc(f_in, 16)
            act.dma_start(l2bq[:, :], t["L2_xattn_bq"].unsqueeze(1), allow_slow_non_contiguous=True).then_inc(f_in, 16)
            act.dma_start(gamma_b[:, 0, :], t["L2_xattn_ln_gamma"].partition_broadcast(P)).then_inc(f_in, 16)
            act.dma_start(gamma_b[:, 1, :], t["L2_xattn_ln_beta"].partition_broadcast(P)).then_inc(f_in, 16)

        SMALL_IN = 16 * (4 * 3 + 7)

        def moe_sp(sp, m, parts):
            def load(e, i, use):
                for dst, src in use(e, i):
                    sp.dma_start(dst, src).then_inc(e_in[i], 16)

            for i in range(2):
                load(i, i, parts[0])
            last = m.n // 2 - (1 if len(parts) > 1 else 0)
            with sp.Fori(1, last) as j:
                for i in range(2):
                    sp.wait_ge(dn_ps, 2 * j + (m.e0 + i - 1))
                    load(2 * j + i, i, parts[0])
            if len(parts) > 1:
                for i in range(2):
                    sp.wait_ge(dn_ps, m.e0 + m.n - 3 + i)
                    load(i, i, parts[1])

        def between_sp(sp, a):
            if a == 0:
                for n, net in enumerate(NETS):
                    sp.dma_start(fw1[n].rearrange("p (l h) -> p l h", l=LEAVES), t[f"L0_ffn_{net}_w1"].rearrange("l d h -> d l h")).then_inc(fw_in, 16)
                    sp.dma_start(fw2[n].rearrange("p (c o) -> p c o", c=HC),
                                 t[f"L0_ffn_{net}_w2"].rearrange("(c l) h o -> (l h) c o", c=HC)).then_inc(fw_in, 16)
            if a == 1:
                def shared(e, i):
                    return ((eA[i][:, 0:HID1], t["L1_ffn_w1_s"][e]),
                            (eC[i][:, 0:HID1].rearrange("p (c o) -> p c o", c=2), t["L1_ffn_w2_s"][e].rearrange("(c p) o -> p c o", p=P)))

                def routed(e, i):
                    return ((eA[i][:, 0:HID1], t["L1_ffn_w1"][bass.ds(e, 1), :, :].rearrange("e d f -> (e d) f")),
                            (eC[i][:, 0:HID1].rearrange("p (c o) -> p c o", c=2),
                             t["L1_ffn_w2"][bass.ds(e, 1), :, :].rearrange("e (c p) o -> p (e c) o", p=P)))

                moe_sp(sp, MOE[0], (routed, shared))

                def swiglu(e, i):
                    return ((eA[i], t["L2_ffn_Wg"][bass.ds(e, 1), :, :].rearrange("e d f -> (e d) f")),
                            (eB[i], t["L2_ffn_Wu"][bass.ds(e, 1), :, :].rearrange("e d f -> (e d) f")),
                            (eC[i].rearrange("p (c o) -> p c o", c=4),
                             t["L2_ffn_Wd"][bass.ds(e, 1), :, :].rearrange("e (c p) o -> p (e c) o", p=P)))

                sp.wait_ge(dn_ps, MOE[1].e0)
                moe_sp(sp, MOE[1], (swiglu,))
            if a == 2:
                def gelu_expert(e, i):
                    return ((eA[i], t["L3_ffn_wi"][bass.ds(e, 1), :, :].rearrange("e d f -> (e d) f")),
                            (eC[i].rearrange("p (c o) -> p c o", c=4),
                             t["L3_ffn_wo"][bass.ds(e, 1), :, :].rearrange("e (c p) o -> p (e c) o", p=P)))

                moe_sp(sp, MOE[2], (gelu_expert,))

        def const_pool(g, chain):
            chain(g.memset(leaf_sel[:, :, :], 0.0))
            for n in range(3):
                ls = leaf_sel[:, :, :].rearrange("p c (l h) -> p c l h", l=2)
                chain(g.affine_select(out=ls, in_=ls, compare_op=ALU.not_equal, fill=1.0,
                                      base=-32 * n, pattern=[[-2, HC], [-1, 2], [0, 64]], channel_multiplier=1))
            chain(g.iota(countdown[:, :], pattern=[[-1, LEAVES]], base=LEAVES, channel_multiplier=0,
                         allow_small_or_imprecise_dtypes=True))
            chain(g.memset(ones[:, :], 1.0))
            chain(g.affine_select(out=tri[:, :], in_=ones[:, :], compare_op=ALU.is_ge, fill=0.0,
                                  base=0, pattern=[[1, P]], channel_multiplier=-1))
            g.memset(leaf[:, :, :], 0.0)
            g.memset(rows_w[:, :], 0.0)
            g.memset(leaf_b2[:, :, :], 0.0)
            chain(g.memset(egate[:, :, E1:E1 + E1S], 1.0))

        def between_pool(pool, a):
            if a == 1:
                m = MOE[0]
                pool.wait_ge(f_cols, 1)

                def scale(e, i, loads):
                    pool.wait_ge(e_in[i], loads)
                    nc.gpsimd.tensor_tensor(eA[i][:, 0:HID1], eA[i][:, 0:HID1],
                                             cols_w[:, bass.ds(e + RMS_AT, 1)].to_broadcast([P, HID1]), ALU.mult).then_inc(e_scaled, 1)

                for i in range(2):
                    scale(i, i, m.in0 + 16 * m.loads)
                with pool.Fori(1, m.n // 2) as j:
                    for i in range(2):
                        scale(2 * j + i, i, j * (16 * m.loads) + (m.in0 + 16 * m.loads))

        def moe_pe(pe, m, hT):
            te = nc.tensor

            def up(e, i, loads, first=False):
                pe.wait_ge(e_in[i], loads)
                if m.scaled:
                    pe.wait_ge(e_scaled, e + 1)
                for k in range(m.units):
                    c, half = divmod(k, 2)
                    if not (first and k < m.ring):
                        if m.up:
                            pe.wait_ge(h_mul, m.units * e + (m.mul0 + k - m.ring + 1))
                        else:
                            pe.wait_ge(h_act, m.units * e + (m.u0 + k - m.ring + 1))
                    last = te.matmul(PS[:, slot(m, k, i), :], eA[i][:, P * c:P * c + P], hT[:, 512 * half:512 * half + 512], start=True, stop=True)
                    if m.up:
                        last = te.matmul(PS[:, 3 + slot(m, k, i), :], eB[i][:, P * c:P * c + P], hT[:, 512 * half:512 * half + 512], start=True, stop=True)
                    last.then_inc(h_ps, 1)

            def down(e, i, first=False):
                if m.up:
                    pe.wait_ge(h_mul, m.units * e + (m.mul0 + m.units))
                else:
                    pe.wait_ge(h_act, m.units * e + (m.u0 + m.units))
                if not first:
                    pe.wait_ge(dn_ev, e + m.e0)
                for n in range(NT):
                    for c in range(m.chunks):
                        last = te.matmul(PS[:, 6 + n // 4, n % 4 * P:n % 4 * P + P], moe_hid[i][:, S * c + P * n:S * c + P * n + P],
                                         eC[i][:, P * c:P * c + P], start=(c == 0), stop=(c == m.chunks - 1))
                last.then_inc(dn_ps, 1)

            per = 16 * m.loads
            up(0, 0, m.in0 + per, True)
            up(1, 1, m.in0 + per)
            down(0, 0, True)
            with pe.Fori(1, m.n // 2) as j:
                up(2 * j, 0, j * per + (m.in0 + per))
                down(2 * j - 1, 1)
                up(2 * j + 1, 1, j * per + (m.in0 + per))
                down(2 * j, 0)
            down(m.n - 1, 1)

        def slot(m, k, i):
            return (m.units * i + k) % m.ring

        def moe_act(act, m):
            def units(e, i, first=False):
                for k in range(m.units):
                    c, half = divmod(k, 2)
                    act.wait_ge(h_ps, m.units * e + (m.u0 + k + 1))
                    if k == 0 and not first:
                        act.wait_ge(dn_ps, e + (m.e0 - 1))
                    nc.scalar.activation(moe_hid[i][:, S * c + 512 * half:S * c + 512 * half + 512], PS[:, slot(m, k, i), :], m.func).then_inc(h_act, 1)

            units(0, 0, True)
            units(1, 1, True)
            with act.Fori(1, m.n // 2) as j:
                units(2 * j, 0)
                units(2 * j + 1, 1)

        def moe_dve(dve, m):
            v = nc.vector

            def mul(e, i):
                if not m.up:
                    return
                for k in range(m.units):
                    c, half = divmod(k, 2)
                    o = moe_hid[i][:, S * c + 512 * half:S * c + 512 * half + 512]
                    dve.wait_ge(h_act, m.units * e + (m.u0 + k + 1))
                    v.tensor_tensor(o, o, PS[:, 3 + slot(m, k, i), :], ALU.mult).then_inc(h_mul, 1)

            def add(e, first=False):
                dve.wait_ge(dn_ps, e + (m.e0 + 1))
                if not first:
                    dve.wait_ge(dn_ev, e + m.e0)
                if not m.gated:
                    o = PS[:, 6:8, :].rearrange("p b n -> p (b n)")
                    if first:
                        v.tensor_copy(moe_acc, o).then_inc(dn_ev, 1)
                    else:
                        v.tensor_tensor(moe_acc, moe_acc, o, ALU.add).then_inc(dn_ev, 1)
                    return
                for n in range(NT):
                    o = PS[:, 6 + n // 4, n % 4 * P:n % 4 * P + P]
                    g = egate[:, n, bass.ds(e, 1)]
                    if first:
                        last = v.tensor_scalar(moe_acc[:, P * n:P * n + P], o, g, None, ALU.mult)
                    else:
                        last = v.scalar_tensor_tensor(moe_acc[:, P * n:P * n + P], o, g, moe_acc[:, P * n:P * n + P], ALU.mult, ALU.add)
                last.then_inc(dn_ev, 1)

            mul(0, 0)
            mul(1, 1)
            add(0, True)
            with dve.Fori(1, m.n // 2) as j:
                mul(2 * j, 0)
                add(2 * j - 1)
                mul(2 * j + 1, 1)
                add(2 * j)
            add(m.n - 1)

        def router_pe(pe, rw, n_e, k):
            for n in range(NT):
                last = nc.tensor.matmul(PS[:, 2, n * n_e:(n + 1) * n_e], xT[:, n * P:(n + 1) * P], rw[:, :], start=True, stop=True)
            last.then_inc(r_ps, 1)

        def router_act(act, n_e, i):
            act.wait_ge(r_cen, i + 1)
            nc.scalar.activation(work[:, :, 0:n_e], logit[:, :, 0:n_e], ACT.Exp).then_inc(r_exp, 1)

        def router_dve(dve, chain, n_e, i):
            v = nc.vector

            def bc(a):
                return a.unsqueeze(2).to_broadcast([P, NT, n_e])

            ps = PS[:, 2, 0:NT * n_e].rearrange("p (n e) -> p n e", e=n_e)
            lg, pr, wk_, s1, s2 = (w[:, :, 0:n_e] for w in (logit, rprob, work, sel1, sel2))
            count = countdown[:, LEAVES - n_e:LEAVES].unsqueeze(1).to_broadcast([P, NT, n_e])
            dve.wait_ge(r_ps, i + 1)
            chain(v.reduce_max(rmax[:, :], ps, X_AXIS))
            v.tensor_tensor(lg, ps, bc(rmax[:, :]), ALU.subtract).then_inc(r_cen, 1)
            dve.wait_ge(r_exp, i + 1)
            chain(v.reduce_sum(rsum[:, :], wk_, X_AXIS))
            chain(v.reciprocal(rsum[:, :], rsum[:, :]))
            chain(v.tensor_tensor(pr, wk_, bc(rsum[:, :]), ALU.mult))
            for s, src in ((s1, pr), (s2, lg)):
                chain(v.reduce_max(rmax[:, :], src, X_AXIS))
                chain(v.tensor_tensor(wk_, src, bc(rmax[:, :]), ALU.is_ge))
                chain(v.tensor_tensor(wk_, wk_, count, ALU.mult))
                chain(v.reduce_max(rmax[:, :], wk_, X_AXIS))
                chain(v.tensor_tensor(s, wk_, bc(rmax[:, :]), ALU.is_equal))
                if s is s1:
                    chain(v.scalar_tensor_tensor(lg, s1, -2.0, pr, ALU.mult, ALU.add))

        def fff_dve(dve, chain):
            v = nc.vector
            dve.wait_ge(f_node, 1)
            ps = PS[:, 2, 0:NT * 3 * NODES].rearrange("p (n m) -> p n m", n=NT)
            b3 = bits[:, :, :].rearrange("p (n m) k -> p n (m k)", n=NT)
            chain(v.tensor_tensor(b3, ps, node_b[:, :].unsqueeze(1).to_broadcast([P, NT, 3 * NODES]), ALU.add))
            chain(v.tensor_scalar(b3, b3, 0.0, None, ALU.is_ge))
            for l in range(DEPTH):
                w = 2 ** l
                dst = leaf[:, :, 0:LEAVES] if l == DEPTH - 1 else paths[l + 1][:, :, :]
                dst = dst.rearrange("p m (w s) -> p m w s", s=2)
                b = bits[:, :, w - 1:2 * w - 1]
                if l == 0:
                    v.tensor_copy(dst[:, :, :, 1], b)
                    chain(v.tensor_scalar(dst[:, :, :, 0], b, -1.0, 1.0, ALU.mult, ALU.add))
                else:
                    chain(v.tensor_tensor(dst[:, :, :, 1], paths[l][:, :, :], b, ALU.mult))
                    last = v.tensor_tensor(dst[:, :, :, 0], paths[l][:, :, :], dst[:, :, :, 1], ALU.subtract)
                    if l < DEPTH - 1:
                        chain(last)
            last.then_inc(f_leaf, 1)
            for u in range(3 * 2 * HC):
                dve.wait_ge(f_relu, u + 1)
                v.tensor_tensor(hid[u % 4], hid[u % 4], PS[:, 2 + u % 2, :], ALU.mult).then_inc(f_masked, 1)
            dve.wait_ge(f_v_ps, 1)
            v.tensor_copy(v_tok, PS[:, 6:8, :].rearrange("p b n -> p (b n)")).then_inc(f_v, 1)

            def copy_T(n):
                dve.wait_ge(fa_T, n + 1)
                if n >= 2:
                    dve.wait_ge(fa_o, n - 1)
                v.tensor_copy(prob_T[n % 2], PS[:, 4:6, :].rearrange("p b n -> p (b n)")).then_inc(fa_Tc, 1)

            for n in range(NT):
                dve.wait_ge(fa_s, n + 1)
                b = 2 * (n % 2)
                chain(v.reduce_max(fmax[:, n:n + 1], PS[:, b:b + 2, :].rearrange("p b n -> p (b n)"), X_AXIS))
                v.tensor_scalar(fneg[:, n:n + 1], fmax[:, n:n + 1], -FSCALE, None, ALU.mult).then_inc(fa_max, 1)
                if n:
                    copy_T(n - 1)
            copy_T(NT - 1)
            dve.wait_ge(fa_p, NT)
            chain(v.reciprocal(frec[:, :], fden[:, :]))
            chain(v.tensor_scalar(frec[:, :], frec[:, :], gates[:, 4:5], None, ALU.mult))
            dve.wait_ge(fa_o, NT)
            for n in range(NT):
                last = v.scalar_tensor_tensor(x[:, n, :], PS[:, 6 + n // 4, n % 4 * P:n % 4 * P + P], frec[:, n:n + 1], x[:, n, :], ALU.mult, ALU.add)
            last.then_inc(x_ready, 1)

        def fff_act(act):
            sc = nc.scalar
            act.wait_ge(f_leafT_ps, 1)
            ps = PS[0:96, 4:6, :].rearrange("p b n -> p (b n)")
            sc.activation(leaf_T, ps, ACT.Copy)
            sc.activation(leaf_Tb, ps, ACT.Copy).then_inc(f_leafT, 1)
            for u in range(3 * 2 * HC):
                net, k = divmod(u, 2 * HC)
                act.wait_ge(f_up, u + 1)
                if u >= 4:
                    act.wait_ge(f_out, u - 3)
                col = B1_AT + HC * net + k // 2
                sc.activation(hid[u % 4], PS[:, u % 2, :], ACT.Relu, bias=cols_w[:, col:col + 1]).then_inc(f_relu, 1)
                if k == 2 * HC - 1:
                    act.wait_ge(f_net_ps, net + 1)
                    b = 4 + 2 * (net % 2)
                    sc.activation(qkv[net], PS[:, b:b + 2, :].rearrange("p b n -> p (b n)"), ACT.Copy).then_inc(f_net, 1)
            for n in range(NT):
                act.wait_ge(fa_max, n + 1)
                if n >= 2:
                    act.wait_ge(fa_T, n - 1)
                b = 2 * (n % 2)
                sc.activation(prob_q[n % 2], PS[:, b:b + 2, :].rearrange("p b n -> p (b n)"), ACT.Exp,
                              bias=fneg[:, n:n + 1], scale=FSCALE, accum_out=fden[:, n:n + 1]).then_inc(fa_p, 1)

        def fff_pe(pe):
            te = nc.tensor
            pe.wait_ge(f_cols, 1)
            pe.wait_ge(ln_xT, 2)
            for n in range(NT):
                last = te.matmul(PS[:, 2, n * 3 * NODES:(n + 1) * 3 * NODES], xT[:, n * P:(n + 1) * P], cols_w[:, 0:3 * NODES], start=True, stop=True)
            last.then_inc(f_node, 1)
            pe.wait_ge(f_leaf, 1)
            for n in range(NT):
                last = te.transpose(PS[0:96, 4 + n // 4, n % 4 * P:n % 4 * P + P], leaf[:, 3 * n:3 * n + 3, :].rearrange("p m l -> p (m l)"), ident[:, :])
            last.then_inc(f_leafT_ps, 1)
            pe.wait_ge(f_leafT, 1)
            pe.wait_ge(fw_in, 16 * 6)
            n_units = 3 * 2 * HC

            def up(u):
                net, k = divmod(u, 2 * HC)
                c, half = divmod(k, 2)
                cols = slice(512 * half, 512 * half + 512)
                if u >= 2:
                    pe.wait_ge(f_masked, u - 1)
                te.matmul(PS[:, u % 2, :], fw1[net][:, P * c:P * c + P], xT[:, cols], start=True, stop=True)
                te.matmul(PS[:, 2 + u % 2, :], leaf_sel[32 * net:32 * net + LEAVES, c, :], leaf_Tb[32 * net:32 * net + LEAVES, cols],
                          start=True, stop=True).then_inc(f_up, 1)

            def out(u):
                net, k = divmod(u, 2 * HC)
                c, half = divmod(k, 2)
                cols = slice(512 * half, 512 * half + 512)
                o = PS[:, 4 + 2 * (net % 2) + half, :]
                if net == 2 and k == 0:
                    pe.wait_ge(f_net, 1)
                pe.wait_ge(f_masked, u + 1)
                last = te.matmul(o, fw2[net][:, D * c:D * c + D], hid[u % 4], start=(c == 0), stop=False)
                last.then_inc(f_out, 1)
                if c == HC - 1:
                    last = te.matmul(o, leaf_b2[:, net, :], leaf_T[:, cols], start=False, stop=True)
                    if half:
                        last.then_inc(f_net_ps, 1)

            up(0)
            for u in range(n_units):
                if u + 1 < n_units:
                    up(u + 1)
                out(u)
            pe.wait_ge(f_net, 3)
            for n in range(NT):
                last = te.transpose(PS[:, 6 + n // 4, n % 4 * P:n % 4 * P + P], qkv[2][:, n * P:(n + 1) * P], ident[:, :])
            last.then_inc(f_v_ps, 1)

            def score(n):
                if n >= 2:
                    pe.wait_ge(fa_p, n - 1)
                for i in range(2):
                    last = te.matmul(PS[:, 2 * (n % 2) + i, :], qkv[0][:, n * P:(n + 1) * P], qkv[1][:, 512 * i:512 * i + 512], start=True, stop=True)
                last.then_inc(fa_s, 1)

            def turn(n):
                pe.wait_ge(fa_p, n + 1)
                if n:
                    pe.wait_ge(fa_Tc, n)
                for j in range(NT):
                    last = te.transpose(PS[:, 4 + j // 4, j % 4 * P:j % 4 * P + P], prob_q[n % 2][:, j * P:(j + 1) * P], ident[:, :])
                last.then_inc(fa_T, 1)

            def product(n):
                pe.wait_ge(fa_Tc, n + 1)
                for j in range(NT):
                    last = te.matmul(PS[:, 6 + n // 4, n % 4 * P:n % 4 * P + P], prob_T[n % 2][:, j * P:(j + 1) * P], v_tok[:, j * P:(j + 1) * P],
                                     start=(j == 0), stop=(j == NT - 1))
                last.then_inc(fa_o, 1)

            score(0)
            score(1)
            pe.wait_ge(f_v, 1)
            for n in range(NT):
                turn(n)
                if n + 2 < NT:
                    score(n + 2)
                product(n)

        def between_dve(dve, chain, a):
            v = nc.vector
            if a == 0:
                ln_dve(dve, chain, 1)
                fff_dve(dve, chain)
            if a == 1:
                ln_dve(dve, chain, 3)
                xnf, sq = xn[:, :, :], accs_flat[:, 0:S].rearrange("p (n d) -> p n d", n=NT)
                dve.wait_ge(ln_xn, 4)
                chain(v.tensor_tensor(sq, xnf, xnf, ALU.mult))
                chain(v.reduce_sum(ln_ve[:, :], sq, X_AXIS))
                v.tensor_scalar(ln_ve[:, :], ln_ve[:, :], 1.0 / D, 1.1920929e-07, ALU.mult, ALU.add).then_inc(ms_ready, 1)
                dve.wait_ge(ms_root, 1)
                chain(v.reciprocal(ln_rs[:, :], ln_sd[:, :]))
                for n in range(NT):
                    last = v.tensor_scalar(sq[:, n, :], xn[:, n, :], ln_rs[:, n:n + 1], None, ALU.mult)
                last.then_inc(ht_sb, 1)
                router_dve(dve, chain, E1, 0)
                g14 = egate[:, :, 0:E1]
                chain(v.tensor_tensor(work[:, :, :], sel1[:, :, :], sel2[:, :, :], ALU.add))
                chain(v.tensor_tensor(g14, work[:, :, :], rprob[:, :, :], ALU.mult))
                chain(v.reduce_sum(rsum[:, :], g14, X_AXIS))
                chain(v.tensor_scalar(rsum[:, :], rsum[:, :], 1e-9, None, ALU.add))
                chain(v.reciprocal(rsum[:, :], rsum[:, :]))
                chain(v.tensor_tensor(g14, g14, rsum[:, :].unsqueeze(2).to_broadcast([P, NT, E1]), ALU.mult))
                moe_dve(dve, MOE[0])
                add_to_x(dve, 5, moe_acc, dn_ev, MOE[1].e0, 3)
                ln_dve(dve, chain, 4)
                z = accs[:, 1, :].rearrange("p (n d) -> p n d", n=NT)
                dve.wait_ge(l2_ps, 1)
                chain(v.scalar_tensor_tensor(accs[:, 1, :], PS[:, 4:6, :].rearrange("p b n -> p (b n)"), SCALE,
                                             xn[:, :, :].rearrange("p n d -> p (n d)"), ALU.mult, ALU.add))
                norm(dve, chain, z, z, 5).then_inc(l2_normed, 1)
                dve.wait_ge(l2_normed, 1)
                for i, op in ((0, ALU.mult), (1, ALU.add)):
                    chain(v.tensor_tensor(z, z, gamma_b[:, i, :].unsqueeze(1).to_broadcast([P, NT, D]), op))
                xf = x[:, :, :].rearrange("p n d -> p (n d)")
                v.scalar_tensor_tensor(xf, accs[:, 1, :], gates[:, 2:3], xf, ALU.mult, ALU.add).then_inc(x_ready, 1)
                ln_dve(dve, chain, 5)
                moe_dve(dve, MOE[1])
                add_to_x(dve, 6, moe_acc, dn_ev, MOE[2].e0, 5)
            if a == 2:
                ln_dve(dve, chain, 7)
                router_dve(dve, chain, E3, 1)
                v.tensor_copy(egate[:, :, 0:E3], sel1[:, :, 0:E3])
                v.tensor_copy(egate[:, :, E3:2 * E3], sel2[:, :, 0:E3]).then_inc(r_sel, 1)
                s8 = [w[:, :, 0:E3] for w in (sel1, sel2, rprob, work, logit)]
                dve.wait_ge(r_cum, 1)
                chain(v.scalar_tensor_tensor(s8[3], PS[:, 5, 0:NT * E3].rearrange("p (n e) -> p n e", e=E3), float(CAP), s8[0], ALU.is_le, ALU.mult))
                chain(v.scalar_tensor_tensor(s8[4], PS[:, 5, NT * E3:2 * NT * E3].rearrange("p (n e) -> p n e", e=E3), float(CAP), s8[1], ALU.is_le, ALU.mult))
                chain(v.tensor_tensor(s8[3], s8[3], s8[4], ALU.add))
                chain(v.tensor_tensor(egate[:, :, 0:E3], s8[3], s8[2], ALU.mult))
                moe_dve(dve, MOE[2])
                add_to_x(dve, 7, moe_acc, dn_ev, MOE[2].e0 + MOE[2].n, 7)

        def between_act(act, a):
            sc = nc.scalar
            if a == 0:
                ln_act(act, 1)
                fff_act(act)
            if a == 1:
                ln_act(act, 3)
                act.wait_ge(ms_ready, 1)
                sc.activation(ln_sd[:, :], ln_ve[:, :], ACT.Sqrt).then_inc(ms_root, 1)
                router_act(act, E1, 0)
                act.wait_ge(ht_ps, 1)
                sc.activation(h_T, PS[:, 4:6, :].rearrange("p b n -> p (b n)"), ACT.Copy).then_inc(ht_ready, 1)
                moe_act(act, MOE[0])
                ln_act(act, 4)
                act.wait_ge(l2q_ps, 1)
                sc.activation(accs[:, 0, :], PS[:, 2:4, :].rearrange("p b n -> p (b n)"), ACT.Identity, bias=l2bq[:, 0:1]).then_inc(l2q, 1)
                act.wait_ge(ln_var, 6)
                sc.activation(ln_sd[:, :], ln_ve[:, :], ACT.Sqrt).then_inc(ln_root, 1)
                ln_act(act, 5)
                moe_act(act, MOE[1])
            if a == 2:
                ln_act(act, 7)
                router_act(act, E3, 1)
                moe_act(act, MOE[2])

        def between_pe(pe, a):
            te = nc.tensor
            if a == 0:
                ln_pe(pe, 1)
                fff_pe(pe)
            if a == 1:
                ln_pe(pe, 3)
                pe.wait_ge(ht_sb, 1)
                for n in range(NT):
                    last = te.transpose(PS[:, 4 + n // 4, n % 4 * P:n % 4 * P + P], accs_flat[:, P * n:P * n + P], ident[:, :])
                last.then_inc(ht_ps, 1)
                pe.wait_ge(ln_xT, 4)
                router_pe(pe, rw1, E1, 0)
                pe.wait_ge(ht_ready, 1)
                moe_pe(pe, MOE[0], h_T)
                ln_pe(pe, 4)
                pe.wait_ge(ln_xT, 5)
                for i in range(2):
                    last = te.matmul(PS[:, 2 + i, :], l2wq[:, :], xT[:, 512 * i:512 * i + 512], start=True, stop=True)
                last.then_inc(l2q_ps, 1)
                pe.wait_ge(l2q, 1)
                for n in range(NT):
                    last = te.matmul(PS[:, 4 + n // 4, n % 4 * P:n % 4 * P + P], accs[:, 0, n * P:(n + 1) * P], kv_sum[:, :], start=True, stop=True)
                last.then_inc(l2_ps, 1)
                ln_pe(pe, 5)
                pe.wait_ge(ln_xT, 6)
                moe_pe(pe, MOE[1], xT)
            if a == 2:
                ln_pe(pe, 7)
                pe.wait_ge(ln_xT, 8)
                router_pe(pe, rw3, E3, 1)
                pe.wait_ge(r_sel, 1)
                c1, c2 = PS[:, 5, 0:NT * E3], PS[:, 5, NT * E3:2 * NT * E3]
                te.matmul(c1, tri[:, :], egate[:, :, 0:E3], start=True, stop=True)
                te.matmul(c2, ones[:, :], egate[:, :, 0:E3], start=True, stop=False)
                te.matmul(c2, tri[:, :], egate[:, :, E3:2 * E3], start=False, stop=True).then_inc(r_cum, 1)
                moe_pe(pe, MOE[2], xT)

        def xk_part(i, c):
            return kparts[:, c].rearrange("p c a k -> p (c a k)")[:, 512 * i:512 * i + 512]

        def at(j, off, per, add):
            return off * per + add if j is None else j * (UNROLL * per) + (off * per + add)

        USES = [(NTILE + 1) // 2, NTILE // 2]
        KEYS_OUT = [16 * SPLIT * u for u in USES]
        ROUNDS = (NTILE - 1) // UNROLL - 1
        TAIL = range(ROUNDS * UNROLL + 1, NTILE)

        def buffer_out(eng, done, per, j, off):
            if j is not None:
                eng.wait_ge(done[off % 2], j * (UNROLL // 2 * per) + off // 2 * per)
            elif off >= 2:
                eng.wait_ge(done[off % 2], off // 2 * per)

        @block.sync
        def _(sp):
            ctx_rows = t["ctx_1024"][0]

            def load_ctx(j, off, n=TC):
                sp.dma_start(c_in[off % UNROLL][:, 0:n, 0:D],
                             ctx_rows[bass.ds(at(j, off, TW, 0), n * P), :].rearrange("(c p) d -> p c d", p=P)).then_inc(c_loaded[off % UNROLL], 16)

            for a, (k, v) in enumerate((("L0_xattn_Wk", "L0_xattn_Wv"), (None, None), ("L3_xattn_Wk", "L3_xattn_Wv"))):
                wkv = t["L1_xattn_Wkv"]
                sp.dma_start(wk_in[:, a, :], t[k][:, :] if k else wkv[:, 0:D]).then_inc(w_in, 16)
                sp.dma_start(wv5[:, a, :], t[v][:, :] if v else wkv[:, D:2 * D]).then_inc(w_in, 16)
                load_ctx(None, a)
            load_ctx(None, UNROLL - 1)
            sp.wait_ge(first_const, 1)
            for a in (0, 2):
                for i, n in enumerate(("bq", "bk")):
                    src = t[f"{ATT[a]}_xattn_{n}"].rearrange("(h d o) -> d h o", h=H, o=1)
                    sp.dma_start(bqk[:, i, a:a + 1], src, allow_slow_non_contiguous=True).then_inc(w_in, 16)
            for i, n in ((0, "L0_xattn_bv"), (2, "L3_xattn_bv"), (3, "L2_xattn_bk"), (4, "L2_xattn_bv")):
                sp.dma_start(b5[:, i, :], t[n].partition_broadcast(P)).then_inc(w_in, 16)
            sp.dma_start(c_last[0:LAST, 0:D], ctx_rows[(NC - 1) * P:CTX, :]).then_inc(w_in, 16)

            def k_step(j, off, ahead=TC):
                b = off % 2
                for c, (done, n) in enumerate(((k_act, 3), (k_part2, 1), (k_part3, 1))):
                    sp.wait_ge(done, at(j, off, n, n))
                    sp.dma_start(ks[bass.ds(at(j, off, TC, 0), TC), :, HD * c:HD * c + HD, :, :].rearrange("c a d h k -> (d h) (c a) k"),
                                 kparts2[b][:, c].rearrange("p c a k -> p (c a) k")).then_inc(k_out[b], 16)
                    if ahead and c == 0:
                        sp.wait_ge(gram_mm, at(j, off, 1, 1))
                        load_ctx(j, off + UNROLL, ahead)
                sp.wait_ge(v_ev, at(j, off, TC, TC))
                sp.dma_start(v_scr[:, bass.ds(at(j, off, TC, 0), TC), :, :].rearrange("p c m v -> p (c m v)"),
                             v_next2[b].rearrange("p c m h v -> p (c m h v)")).then_inc(v_out[b], 16)

            k_step(None, 0)
            with sp.Fori(0, ROUNDS - 1) as j:
                for off in range(1, UNROLL + 1):
                    k_step(j, off)
            for i in range((ROUNDS - 1) * UNROLL + 1, NTILE):
                n = i + UNROLL
                k_step(None, i, 0 if n >= NTILE else TC - 1 if n == NTILE - 1 else TC)
            sp.wait_ge(rows_out, 16 * (SPLIT * 3 + 6))

            for a in range(3):
                if ATT[a] == "L1":
                    for i in range(2):
                        sp.wait_ge(k_act, 3 * NTILE + i + 1)
                        sp.wait_ge(k_part2, NTILE + i + 1)
                        sp.wait_ge(k_part3, NTILE + i + 1)
                        for c in range(SPLIT):
                            sp.dma_start(ks[NC + 4 * i:NC + 4 * i + 4, 1, HD * c:HD * c + HD, :, :].rearrange("c d h k -> (d h) c k"),
                                         xk_part(i, c).rearrange("p (c k) -> p c k", c=4)).then_inc(k_out[i], 16)
                sp.wait_ge(q_act, a + 1)
                sp.wait_ge(q_split, a + 1)
                for c in range(SPLIT):
                    sp.dma_start(q_scr[c], qparts[:, c, :]).then_inc(q_out, 16)
                sp.wait_ge(bound_ready, a + 1)
                sp.dma_start(bound_row[0:1, :], bound[32 * a:32 * a + H, 0:1]).then_inc(bound_in, 16)
                sp.wait_ge(q_out, 16 * SPLIT * (a + 1))
                for c in range(SPLIT):
                    for r in range(SPLIT):
                        row = KROWS * c + HD * r
                        sp.dma_start(qs[row:row + HD, :, :], q_scr[c].rearrange("(d h) n -> d h n", d=HD)).then_inc(qs_in, 16)
                sp.dma_start(qs[SPLIT * KROWS:SROWS, :, :], row_scr.rearrange("r (h n) -> r h n", h=H)).then_inc(qs_in, 16)
                sp.wait_ge(qs_in, 16 * 10 * (a + 1))
                for b in range(2):
                    sp.wait_ge(k_out[b], KEYS_OUT[b] + (16 * SPLIT if a >= 1 else 0))

                def load_keys(b, c, hh, done):
                    h0 = hh * (H // 2)
                    parts = ks[bass.ds(c, 1), a, 0:KROWS, h0:h0 + H // 2, :].rearrange("c r h k -> (c r) (h k)")
                    sp.dma_start(kr[b][0:SPLIT * KROWS, :, :].rearrange("r h k -> r (h k)"),
                                 parts.unsqueeze(0).to_broadcast([SPLIT, KROWS, H // 2 * P])).then_inc(done, 16)
                    rows = ks[bass.ds(c, 1), a, KROWS:KROWS + SPLIT + 1, h0:h0 + H // 2, :].rearrange("c r h k -> (c r) (h k)")
                    sp.dma_start(kr[b][SPLIT * KROWS:SROWS, :, :].rearrange("r h k -> r (h k)"), rows).then_inc(done, 16)

                sp.wait_ge(flag_ready, a + 1)
                need_max = sp.value_load(flag[0:1, a:a + 1], min_val=0, max_val=1)
                with sp.If(need_max > 0):
                    for hh in range(2):
                        q0 = 4 * hh * (NC + (NT if a == 1 else 0))
                        if hh:
                            sp.wait_ge(mx_ps[a], q0)
                        load_keys(0, 0, hh, mx_in[a])
                        with sp.Fori(1, NC) as c:
                            sp.wait_ge(mx_ps[a], q0 + 4 * c)
                            load_keys(0, c, hh, mx_in[a])
                        for c in range(NC, NC + (NT if a == 1 else 0)):
                            sp.wait_ge(mx_ps[a], q0 + 4 * c)
                            load_keys(0, c, hh, mx_in[a])
                    sp.wait_ge(mx_dve[a], 1)
                    for c in range(SPLIT):
                        sp.dma_start(m_scr[c], mparts[:, c, :]).then_inc(mx_out[a], 16)
                    sp.wait_ge(mx_out[a], 16 * SPLIT)
                    sp.dma_start(qs[SPLIT * KROWS:SPLIT * KROWS + SPLIT, :, :],
                                 m_scr.rearrange("c (h t) k -> c h (t k)", h=H)).then_inc(mx_out[a], 16)
                    sp.wait_ge(mx_out[a], 16 * SPLIT + 16)
                sp.end_ifs()

                for s in SWEEPS[4 * a:4 * a + 4]:
                    for c in range(TC):
                        if s.w:
                            sp.wait_ge(s_ready, s.pairs + (4 * c - 8 if s.aligned else 0))
                        load_keys(c, c, s.hh, kr_in[c])
                    with sp.Fori(1, NTILE) as i:
                        for b in range(TC):
                            sp.wait_ge(s_ready, i * (4 * TC) + (s.pairs + 4 * b - 8))
                            load_keys(b, i * TC + b, s.hh, kr_in[b])
                    for c in range(NC, s.n):
                        sp.wait_ge(s_ready, s.pairs + 4 * c - 8)
                        load_keys(c % TC, c, s.hh, kr_in[c % TC])
                end = SWEEPS[4 * a + 3]
                sp.wait_ge(s_ready, end.pairs + 4 * end.n)
                if a < 2:
                    sp.wait_ge(v_copied, SWEEPS[4 * a + 3].chunks + SWEEPS[4 * a + 3].n)
                    for b in range(2):
                        sp.wait_ge(v_out[b], 16 * USES[b])
                    sp.dma_start(vs[:, 0:NC, :, :].rearrange("p c h v -> p c (h v)"), v_scr[:, :, a, :]).then_inc(v_in, 16)
                between_sp(sp, a)
            sp.wait_ge(x_ready, 8)
            sp.dma_start(out[0].rearrange("(n p) d -> p n d", p=P), x[:, :, :]).then_inc(x_out, 16)
            sp.wait_ge(x_out, 16)

        @block.gpsimd
        def _(pool):
            g = nc.gpsimd
            chain = Chain(pool, pool_c)
            g.memset(mask_u8[:, :], 0)
            chain(g.memset(c_last[:, :], 0.0))
            g.memset(c_last[0:LAST, D:D + 1], 1.0)
            for b in range(UNROLL):
                g.memset(c_in[b][:, :, D:D + 1], 1.0)
            for b in range(2):
                g.memset(v_next2[b][:, :, :, :, HD:VC].rearrange("p c a h o -> p (c a h) o"), 1.0)
            g.memset(bqk[:, :, :], 0.0)
            g.memset(b5[:, 1, :], 0.0)
            chain(g.memset(ident[:, :], 0.0))
            chain(g.affine_select(out=ident[:, :], in_=ident[:, :], compare_op=ALU.not_equal, fill=1.0,
                                  base=0, pattern=[[-1, P]], channel_multiplier=1))
            chain(g.memset(head_of[:, :], 0.0))
            for d in range(HD):
                chain(g.affine_select(out=head_of[:, :], in_=head_of[:, :], compare_op=ALU.not_equal, fill=1.0,
                                      base=-H * d, pattern=[[-1, 32]], channel_multiplier=1))
            chain(g.memset(head_of[:, H:32], 0.0))
            g.memset(vs[:, :, :, HD:VC].rearrange("p c h o -> p (c h) o"), 1.0).then_inc(first_const, 1)
            pool.wait_ge(first_const, 1)
            chain(g.tensor_copy(ident_b[:, :], ident[:, :]))
            chain(g.memset(stair[:, :], 0.0))
            chain(g.affine_select(out=stair[:, :], in_=stair[:, :], compare_op=ALU.is_ge, fill=-BIG,
                                  base=-384, pattern=[[1, 896]], channel_multiplier=-1))
            chain(g.memset(upper[:, :], 0.0))
            chain(g.affine_select(out=upper[:, :], in_=upper[:, :], compare_op=ALU.is_ge, fill=-BIG,
                                  base=0, pattern=[[-1, P]], channel_multiplier=1))
            g.memset(ones_row[:, :], 1.0)
            g.memset(zero_one[:, 0, :], 0.0)
            g.memset(zero_one[:, 1, :], 1.0)
            chain(g.memset(valid[:, :], 1.0))
            chain(g.affine_select(out=valid[:, :], in_=valid[:, :], compare_op=ALU.is_ge, fill=0.0,
                                  base=CTX - 1, pattern=[[-1, P]], channel_multiplier=-P))
            chain(g.memset(valid_last[:, :], 0.0))
            chain(g.memset(valid_last[0:LAST, :], 1.0))
            for b in range(TC):
                g.memset(vr[b][:, :, :], 0.0)
            const_pool(g, chain)
            chain(g.memset(kv_mask[:, :], 1.0))
            kvm = kv_mask[:, :].rearrange("p (h d) -> p h d", h=H)
            chain(g.affine_select(out=kvm, in_=kvm, compare_op=ALU.is_ge, fill=0.0,
                                  base=0, pattern=[[-HD, H], [0, HD]], channel_multiplier=1))
            chain(g.affine_select(out=kvm, in_=kvm, compare_op=ALU.is_ge, fill=0.0,
                                  base=HD - 1, pattern=[[HD, H], [0, HD]], channel_multiplier=-1))
            g.memset(run_max[:, :, :], 0.0).then_inc(const_ready, 1)

            def third_parts(i, r1, p2, p3):
                pool.wait_ge(k_part2, i + 1)
                g.tensor_tensor(p3, r1, p2, ALU.subtract).then_inc(k_part3, 1)

            k_restf = k_rest[:, :, :, :].rearrange("p c a k -> p (c a k)")

            def flat_part(b, c):
                return kparts2[b][:, c].rearrange("p c a k -> p (c a k)")

            def k_step(j, off):
                b = off % 2
                buffer_out(pool, k_out, 16 * SPLIT, j, off)
                third_parts(at(j, off, 1, 0), k_restf, flat_part(b, 1), flat_part(b, 2))

            k_step(None, 0)
            with pool.Fori(0, ROUNDS) as j:
                for off in range(1, UNROLL + 1):
                    k_step(j, off)
            for i in TAIL:
                k_step(None, i)

            for a in range(3):
                if ATT[a] == "L1":
                    for i in range(2):
                        if i == 0:
                            for b in range(2):
                                pool.wait_ge(k_out[b], KEYS_OUT[b])
                        cols = slice(512 * i, 512 * i + 512)
                        third_parts(NTILE + i, k_restf[:, cols], flat_part(0, 1)[:, cols], flat_part(0, 2)[:, cols])
                pool.wait_ge(v_final, a + 1)
                if ATT[a] == "L1":
                    pool.wait_ge(xv_ready, 1)
                for s in SWEEPS[4 * a:4 * a + 4]:
                    h0 = s.hh * (H // 2)

                    def copy_values(b, c):
                        g.tensor_copy(vr[b][:, :, 0:VC], vs[:, bass.ds(c, 1), h0:h0 + H // 2, :].rearrange("p o h v -> p (o h) v")).then_inc(v_copied, 1)

                    for c in range(TC):
                        if s.w:
                            pool.wait_ge(pv_done, s.groups + (2 * c - 4 if s.aligned else 0))
                        copy_values(c, c)
                    with pool.Fori(1, NTILE) as i:
                        for b in range(TC):
                            pool.wait_ge(pv_done, i * (2 * TC) + (s.groups + 2 * b - 4))
                            copy_values(b, i * TC + b)
                    for c in range(NC, s.n):
                        pool.wait_ge(pv_done, s.groups + 2 * c - 4)
                        copy_values(c % TC, c)
                between_pool(pool, a)

        @block.scalar
        def _(act):
            sc = nc.scalar
            chain = Chain(act, act_c)
            act.wait_ge(const_ready, 1)
            mask = t["mask_Bx1xS2_bf1"][0, 0]
            act.dma_start(mask_u8[0:NC - 1, :], mask[0:(NC - 1) * P].rearrange("(c p) -> c p", p=P)).then_inc(rows_in, 16)
            act.dma_start(mask_u8[NC - 1:NC, 0:LAST], mask[(NC - 1) * P:CTX].unsqueeze(0)).then_inc(rows_in, 16)

            def k_step(j, off, first=False, last=False):
                b = off % 2
                buffer_out(act, k_out, 16 * SPLIT, j, off)
                for a in range(3):
                    act.wait_ge(k_ps, at(j, off, 3, a + 1))
                    if a == 0 and not first:
                        act.wait_ge(kn_ps, at(j, off, 1, 0))
                        if j is not None or off > 1:
                            act.wait_ge(k_r1, at(j, off, 1, -1))
                    keys = PS[:, 1 + a, 0:TW].rearrange("p (c k) -> p c k", c=TC)
                    sc.activation(kf2[b][:, :, a, :], keys, ACT.Identity, bias=bqk[:, 1, a:a + 1])
                    sc.activation(kparts2[b][:, 0, :, a, :], keys, ACT.Identity, bias=bqk[:, 1, a:a + 1])
                    sc.activation(ksq[:, a, :], PS[:, 1 + a, 0:TW], ACT.Square, bias=bqk[:, 1, a:a + 1]).then_inc(k_act, 1)
                    if a == 0 and not last:
                        rows(j, off + 1, first)

            def rows(j, off, first=False):
                act.wait_ge(ct_ps, at(j, off, 1, 1))
                if not first:
                    act.wait_ge(v_ps, at(j, off, TC, -TC))
                sc.activation(c_T[off % 2], PS[:, 0, 0:TW], ACT.Copy).then_inc(ct_ready, 1)

            act.wait_ge(w_in, WEIGHTS_IN)
            rows(None, 0, True)
            k_step(None, 0, first=True)
            act.dma_start(x[:, :, :], t["x"][0].rearrange("(n p) d -> p n d", p=P)).then_inc(x_in, 16)
            for a, l in enumerate(ATT):
                act.dma_start(wq_in[:, a, :], t[f"{l}_xattn_Wq"][:, :]).then_inc(w_late, 16)
                act.dma_start(wo[:, a, :], t["L1_xattn_Wout" if a == 1 else f"{l}_xattn_Wo"][:, :]).then_inc(w_late, 16)
                act.dma_start(bo[0:1, a, :], t["L1_xattn_bout" if a == 1 else f"{l}_xattn_bo"].unsqueeze(0)).then_inc(w_late, 16)
            for i, n in enumerate(("L2_xattn_Wk", "L2_xattn_Wv", "L2_xattn_Wq")):
                act.dma_start(l2w[:, i, :], t[n][:, :]).then_inc(w_late, 16)
            for i, n in enumerate(("g_xattn", "g_ffn")):
                act.dma_start(gates_raw[:, 4 * i:4 * i + 4], t[n].partition_broadcast(P)).then_inc(w_late, 16)
            late_weights(act)
            for a in range(3):
                n = NC + (NT if a == 1 else 0)
                for c in range(SPLIT):
                    act.dma_start(ks[0:n, a, KROWS + c, :, :], zero_one[0:n, 1, :].unsqueeze(1).to_broadcast([n, H, P])).then_inc(rows_out, 16)
            act.dma_start(row_scr[0:SPLIT].rearrange("r (p n) -> p r n", p=P), zero_one[:, 0, :].unsqueeze(1).to_broadcast([P, SPLIT, P])).then_inc(rows_out, 16)
            act.dma_start(row_scr[SPLIT].rearrange("(p n) -> p n", p=P), zero_one[:, 1, :]).then_inc(rows_out, 16)
            act.dma_start(ks[NC:NC + NT, 1, KROWS + SPLIT, :, :], zero_one[0:NT, 0, :].unsqueeze(1).to_broadcast([NT, H, P])).then_inc(rows_out, 16)
            act.wait_ge(rows_ready, 1)
            for a in range(3):
                act.dma_start(ks[0:NC, a, KROWS + SPLIT, :, :], mask_rows[0:NC, a // 2, :].unsqueeze(1).to_broadcast([NC, H, P])).then_inc(rows_out, 16)

            with act.Fori(0, ROUNDS) as j:
                for off in range(1, UNROLL + 1):
                    k_step(j, off)
            for i in TAIL:
                k_step(None, i, last=(i == NTILE - 1))
            act.wait_ge(w_late, WEIGHTS_LATE)
            sc.activation(gates[:, :], gates_raw[:, :], ACT.Tanh).then_inc(wprep_ready, 1)

            for a in range(3):
                ln_act(act, 2 * a + (a == 2) * 2)
                if ATT[a] == "L1":
                    for i in range(2):
                        act.wait_ge(k_ps, 3 * NTILE + i + 1)
                        if i == 0:
                            for b in range(2):
                                act.wait_ge(k_out[b], KEYS_OUT[b])
                        cols = slice(512 * i, 512 * i + 512)
                        flat = [kf[:, :, :, :].rearrange("p c a k -> p (c a k)")[:, cols], kparts[:, 0].rearrange("p c a k -> p (c a k)")[:, cols],
                                ksq[:, :, :].rearrange("p a k -> p (a k)")[:, cols]]
                        sc.activation(flat[0], PS[:, 4 + i, :], ACT.Copy)
                        sc.activation(flat[1], PS[:, 4 + i, :], ACT.Copy)
                        sc.activation(flat[2], PS[:, 4 + i, :], ACT.Square).then_inc(k_act, 1)
                act.wait_ge(q_ps, a + 1)
                psq = PS[:, 2:4, :].rearrange("p b n -> p (b n)")
                sc.activation(qf, psq, ACT.Identity, bias=bqk[:, 0, a:a + 1])
                sc.activation(qparts[:, 0, :], psq, ACT.Identity, bias=bqk[:, 0, a:a + 1])
                sc.activation(qsq, psq, ACT.Square, bias=bqk[:, 0, a:a + 1]).then_inc(q_act, 1)

                for s in SWEEPS[4 * a:4 * a + 4]:
                    def exps(b, c, first=False):
                        for p in range(4):
                            act.wait_ge(s_ready, 4 * c + (s.pairs + p + 1))
                            if not (first and s.w == 0 and c < 1):
                                act.wait_ge(pv_done, 2 * c + (s.groups + p // 2 - 1))
                            slot = (b + p) % 3
                            sc.activation(prob[p][:, :, :], PS[:, 2 * slot:2 * slot + 2, :], ACT.Exp, scale=SCALE).then_inc(p_ready, 1)

                    for c in range(TC):
                        exps(c, c, True)
                    with act.Fori(1, NTILE) as i:
                        for b in range(TC):
                            exps(b, i * TC + b)
                    for c in range(NC, s.n):
                        exps(c % TC, c)
                act.wait_ge(atT_ps, a + 1)
                sc.activation(att_T[:, :], PS[:, 0:2, :].rearrange("p b n -> p (b n)"), ACT.Copy).then_inc(atT_ready, 1)
                between_act(act, a)

        @block.tensor
        def _(pe):
            te = nc.tensor
            pe.wait_ge(first_const, 1)
            pe.wait_ge(w_in, WEIGHTS_IN)
            pe.wait_ge(wprep_ready, 1)

            def rows(j, off, last=False):
                b = off % UNROLL
                if j is None:
                    pe.wait_ge(c_loaded[b], 16 * (off // UNROLL + 1))
                else:
                    pe.wait_ge(c_loaded[b], j * 16 + 16 * (off // UNROLL + 1))
                for c in range(TC):
                    src = c_last[:, 0:D] if last and c == TC - 1 else c_in[b][:, c, 0:D]
                    ins = te.transpose(PS[:, 0, c * P:(c + 1) * P], src, ident[:, :])
                ins.then_inc(ct_ps, 1)

            def norms(j, off, first=False):
                pe.wait_ge(k_act, at(j, off, 3, 3))
                if not first:
                    pe.wait_ge(kn_ev, at(j, off, 1, 0))
                for a in range(3):
                    ins = te.matmul(PS[32 * a:32 * a + 32, 7, 0:TW], head_of[:, :], ksq[:, a, :], start=True, stop=True)
                ins.then_inc(kn_ps, 1)

            def k_step(j, off, first=False, last=False, before_last=False):
                b = off % 2
                pe.wait_ge(ct_ready, at(j, off, 1, 1))
                for a in range(3):
                    if not first:
                        pe.wait_ge(k_act, at(j, off, 3, a - 2))
                    te.matmul(PS[:, 1 + a, 0:TW], wk[:, a, :], c_T[b], start=True, stop=True).then_inc(k_ps, 1)
                if not last:
                    rows(j, off + 1, before_last)
                if not first:
                    norms(j, off - 1)
                for c in range(TC):
                    if not (first and c < 2):
                        pe.wait_ge(v_ev, at(j, off, TC, c - 1))
                    te.matmul(PS[:, 4 + (off + c) % 2, 0:3 * D], c_T[b][:, c * P:(c + 1) * P], wv5[:, 0:3, :].rearrange("p a d -> p (a d)"),
                              start=True, stop=True).then_inc(v_ps, 1)
                for c in range(TC):
                    src = c_last[:, :] if last and c == TC - 1 else c_in[off % UNROLL][:, c, :]
                    ins = te.matmul(PS[:, 6, 0:D + 1], src[:, 0:D], src, start=(first and c == 0), stop=True, skip_group_check=True)
                ins.then_inc(gram_mm, 1)

            rows(None, 0)
            k_step(None, 0, first=True)
            with pe.Fori(0, ROUNDS) as j:
                for off in range(1, UNROLL + 1):
                    k_step(j, off)
            for i in TAIL:
                k_step(None, i, last=(i == NTILE - 1), before_last=(i == NTILE - 2))
            norms(None, NTILE - 1)

            pe.wait_ge(w_late, WEIGHTS_LATE)
            pe.wait_ge(v_ev, NTILE * TC)
            for i in range(3):
                last = te.transpose(PS[:, 4, i * D:(i + 1) * D], l2w[:, i, :], ident[:, :])
            last.then_inc(wprep_ps, 1)
            pe.wait_ge(rows_ready, 1)
            te.transpose(PS[:, 5, 0:64], mask_f[0:64, :], ident[0:64, 0:64]).then_inc(wprep_ps, 1)
            pe.wait_ge(f_in, SMALL_IN)
            pe.wait_ge(k_act, 3 * NTILE)
            te.transpose(PS[:, 3, 0:96], rows_w[0:96, :], ident[0:96, 0:96]).then_inc(f_cols_ps, 1)
            pe.wait_ge(wprep_ready, 4)
            pe.wait_ge(f_cols, 1)

            for a in range(3):
                k = 2 * a + (a == 2) * 2
                ln_pe(pe, k)
                if ATT[a] == "L1":
                    pe.wait_ge(ln_xT, k + 1)
                    for i in range(2):
                        te.matmul(PS[:, 4 + i, :], wk[:, a, :], xT[:, 512 * i:512 * i + 512], start=True, stop=True).then_inc(k_ps, 1)
                    for n in range(NT):
                        last = te.matmul(PS[:, 6 + n // 4, n % 4 * P:n % 4 * P + P], xT[:, n * P:(n + 1) * P], wv5[:, 1, :], start=True, stop=True)
                        if n % 4 == 3:
                            last.then_inc(v_ps, 1)
                    for i in range(2):
                        pe.wait_ge(k_act, 3 * NTILE + i + 1)
                        te.matmul(PS[0:32, i, :], head_of[:, :], ksq[:, :, :].rearrange("p a k -> p (a k)")[:, 512 * i:512 * i + 512],
                                  start=True, stop=True).then_inc(kn_ps, 1)
                pe.wait_ge(ln_xT, k + 1)
                for i in range(2):
                    last = te.matmul(PS[:, 2 + i, :], wq[:, a, :], xT[:, 512 * i:512 * i + 512], start=True, stop=True)
                last.then_inc(q_ps, 1)
                pe.wait_ge(q_act, a + 1)
                if ATT[a] == "L1":
                    pe.wait_ge(kn_ev, NTILE + 2)
                for i in range(2):
                    last = te.matmul(PS[32 * a:32 * a + 32, 4 + i, :], head_of[:, :], qsq[:, 512 * i:512 * i + 512], start=True, stop=True)
                last.then_inc(qn_ps, 1)
                if a == 0:
                    pe.wait_ge(gram_sb, 1)
                    pe.wait_ge(kn_ev, NTILE)
                    te.matmul(PS[:, 7, 0:D], gram[:, 0:D], wv5[:, 4, :], start=True, stop=True).then_inc(gram_ps, 1)
                    pe.wait_ge(gram_sb, 2)
                    te.matmul(PS[:, 6, 0:D], wv5[:, 3, :], gram_v[:, :], start=True, stop=False)
                    te.matmul(PS[:, 6, 0:D], sum_bk[:, :], wv5[:, 4, :], start=False, stop=False)
                    te.matmul(PS[:, 6, 0:D], b5[0:1, 3, :], n_bv[0:1, :], start=False, stop=True).then_inc(gram_ps, 1)
                    pe.wait_ge(gram_sb, 3)

                pe.wait_ge(flag_ready, a + 1)
                need_max = pe.value_load(flag[0:1, a:a + 1], min_val=0, max_val=1)
                with pe.If(need_max > 0):
                    def max_scores(c, hh, q0, first=False, xc=None):
                        pe.wait_ge(mx_in[a], 32 * c + (32 * (q0 // 4) + 32))
                        for r in range(4):
                            if not (first and hh == 0 and r < 2):
                                pe.wait_ge(mx_red[a], 4 * c + (q0 + r - 1))
                            for e in range(2):
                                for n in range(0 if xc is None else xc, NT):
                                    o = PS[:, 4 * (r % 2) + 2 * e + n // 4, n % 4 * P:n % 4 * P + P]
                                    h = 2 * r + e
                                    diag = xc == n
                                    last = te.matmul(o, qs[:, hh * 8 + h, n * P:(n + 1) * P], kr[0][:, h, :], start=True, stop=not diag)
                                    if diag:
                                        last = te.matmul(o, ident_b[:, :], upper[:, :], start=False, stop=True)
                            last.then_inc(mx_ps[a], 1)

                    nx = NT if a == 1 else 0
                    for hh in range(2):
                        q0 = 4 * hh * (NC + nx)
                        max_scores(0, hh, q0, first=True)
                        with pe.Fori(1, NC) as c:
                            max_scores(c, hh, q0)
                        for xc in range(nx):
                            max_scores(NC + xc, hh, q0, xc=xc)
                    pe.wait_ge(mx_red[a], 8 * (NC + nx))
                    pe.wait_ge(mx_run[a], 8 * (NC + nx) - 8)
                    te.transpose(PS[:, 0, 0:P], run_max[:, :, :].rearrange("p h n -> p (h n)"), ident[:, :]).then_inc(mx_tp[a], 1)
                pe.end_ifs()

                for s in SWEEPS[4 * a:4 * a + 4]:
                    if s.w:
                        pe.wait_ge(p_ready, s.pairs)

                    def scores(b, c, j, loads, first=False, xc=None):
                        if j == 0:
                            pe.wait_ge(kr_in[b], loads)
                        if not (first and 4 * c + j < 3):
                            pe.wait_ge(p_ready, 4 * c + (s.pairs + j - 2))
                        for e in range(2):
                            h = 2 * j + e
                            o = PS[:, 2 * ((b + j) % 3) + e, :]
                            late = xc is not None and xc >= 4 * s.qh
                            last = te.matmul(o, kr[b][:, h, :], qs[:, s.hh * 8 + h, s.qh * 512:s.qh * 512 + 512], start=True, stop=not late)
                            if late:
                                off = 384 - P * (xc - 4 * s.qh)
                                last = te.matmul(o, ident_b[:, :], stair[:, off:off + 512], start=False, stop=True)
                        last.then_inc(s_ready, 1)

                    def values(b, c, g, first=False):
                        if g == 0:
                            pe.wait_ge(v_copied, c + (s.chunks + 1))
                        pe.wait_ge(p_ready, 4 * c + (s.pairs + 2 * g + 2))
                        if first and c == 0 and s.w:
                            pe.wait_ge(acc_ev, s.w)
                        for j in range(4):
                            last = te.matmul(PS[32 * j:32 * j + 32, 6 + g, :], vr[b][:, 4 * g + j, :], prob[2 * g + j // 2][:, j % 2, :],
                                             start=(first and c == 0), stop=True, skip_group_check=True)
                        last.then_inc(pv_done, 1)

                    for c in range(TC):
                        ld = 32 * (s.ring[c] + 1)
                        scores(c, c, 0, ld, True)
                        scores(c, c, 1, ld, True)
                        if c:
                            values(c - 1, c - 1, 1, True)
                        scores(c, c, 2, ld, True)
                        scores(c, c, 3, ld, True)
                        values(c, c, 0, True)
                    with pe.Fori(1, NTILE) as i:
                        for b in range(TC):
                            c = i * TC + b
                            ld = i * 32 + 32 * (s.ring[b] + 1)
                            scores(b, c, 0, ld)
                            scores(b, c, 1, ld)
                            values((b - 1) % TC, i * TC + (b - 1), 1)
                            scores(b, c, 2, ld)
                            scores(b, c, 3, ld)
                            values(b, c, 0)
                    for c in range(NC, s.n):
                        b = c % TC
                        ld = 32 * (s.ring[b] + c // TC + 1)
                        scores(b, c, 0, ld, xc=c - NC)
                        scores(b, c, 1, ld, xc=c - NC)
                        values((b - 1) % TC, c - 1, 1)
                        scores(b, c, 2, ld, xc=c - NC)
                        scores(b, c, 3, ld, xc=c - NC)
                        values(b, c, 0)
                    values((s.n - 1) % TC, s.n - 1, 1)

                pe.wait_ge(acc_ev, NSW * (a + 1))
                for n in range(NT):
                    for g in range(4):
                        last = te.transpose(PS[:, n, g * P:(g + 1) * P], accs[:, g, n * P:(n + 1) * P], ident[:, :])
                    last.then_inc(at_ps, 1)
                for n in range(NT):
                    pe.wait_ge(at_rd, NT * a + max(n + 1, 2))
                    last = te.transpose(PS[:, n // 4, n % 4 * P:n % 4 * P + P], att[:, n, :], ident[:, :])
                last.then_inc(atT_ps, 1)
                pe.wait_ge(atT_ready, a + 1)
                for n in range(NT):
                    o = PS[:, 2 + n // 4, n % 4 * P:n % 4 * P + P]
                    te.matmul(o, att_T[:, n * P:(n + 1) * P], wo[:, a, :], start=True, stop=False)
                    last = te.matmul(o, ones_row[0:1, :], bo[0:1, a, :], start=False, stop=True)
                last.then_inc(y_ps, 1)
                between_pe(pe, a)

        @block.vector
        def _(dve):
            v = nc.vector
            chain = Chain(dve, dve_c)
            dve.wait_ge(w_in, WEIGHTS_IN)
            for a in range(3):
                last = v.tensor_copy(wk[:, a, :].rearrange("p (d h) -> p d h", d=HD), dh(wk_in[:, a, :]))
            last.then_inc(wprep_ready, 1)
            dve.wait_ge(first_const, 1)

            def k_step(j, off, first=False):
                b = off % 2
                buffer_out(dve, v_out, 16, j, off)
                for c in range(TC):
                    dve.wait_ge(v_ps, at(j, off, TC, c + 1))
                    bank = 4 + (off + c) % 2
                    for o, m in ((vs[:, bass.ds(at(j, off, TC, c), 1), :, 0:HD].rearrange("p o h d -> p (o h) d"), slice(0, 1)),
                                 (v_next2[b][:, c, :, :, 0:HD].rearrange("p a h d -> p (a h) d"), slice(1, 3))):
                        last = v.tensor_tensor(o, PS[:, bank, m.start * D:m.stop * D].rearrange("p (m d) -> p m d", d=HD),
                                               b5[:, m, :].rearrange("p a (h d) -> p (a h) d", d=HD), ALU.add)
                    last.then_inc(v_ev, 1)
                dve.wait_ge(k_act, at(j, off, 3, 3))
                if not first:
                    dve.wait_ge(k_part3, at(j, off, 1, 0))
                v.tensor_tensor(k_rest[:, :, :, :], kf2[b], kparts2[b][:, 0], ALU.subtract).then_inc(k_r1, 1)
                buffer_out(dve, k_out, 16 * SPLIT, j, off)
                dve.wait_ge(k_r1, at(j, off, 1, 1))
                v.tensor_copy(kparts2[b][:, 1], k_rest[:, :, :, :]).then_inc(k_part2, 1)
                if not first:
                    longest(j, off - 1)

            def longest(j, off):
                dve.wait_ge(kn_ps, at(j, off, 1, 1))
                v.reduce_max(kmax[0:96, bass.ds(at(j, off, 1, 0), 1)], PS[0:96, 7, 0:TW], X_AXIS).then_inc(kn_ev, 1)

            k_step(None, 0, first=True)
            dve.wait_ge(const_ready, 1)
            dve.wait_ge(rows_in, 32)
            chain(v.tensor_copy(mask_f[:, :], mask_u8[:, :]))
            v.tensor_scalar(mask_rows[:, 0, :], valid[:, :], -1.0, BIG, ALU.add, ALU.mult)
            v.tensor_scalar(mask_rows[:, 1, :], mask_f[:, :], -1.0, BIG, ALU.add, ALU.mult).then_inc(rows_ready, 1)
            with dve.Fori(0, ROUNDS) as j:
                for off in range(1, UNROLL + 1):
                    k_step(j, off)
            for i in TAIL:
                k_step(None, i)
            longest(None, NTILE - 1)

            dve.wait_ge(w_late, WEIGHTS_LATE)
            for a in range(3):
                v.tensor_copy(wq[:, a, :].rearrange("p (d h) -> p d h", d=HD), dh(wq_in[:, a, :]))
            dve.wait_ge(wprep_ps, 1)
            v.tensor_copy(wv5[:, 3:5, :].rearrange("p a d -> p (a d)"), PS[:, 4, 0:2 * D])
            v.tensor_copy(l2wq[:, :], PS[:, 4, 2 * D:3 * D]).then_inc(wprep_ready, 1)
            dve.wait_ge(wprep_ps, 2)
            v.tensor_copy(mask_T[:, :], PS[:, 5, 0:64]).then_inc(wprep_ready, 1)
            dve.wait_ge(f_cols_ps, 1)
            v.tensor_copy(cols_w[:, :], PS[:, 3, 0:96]).then_inc(f_cols, 1)
            dve.wait_ge(x_in, 16)

            for a in range(3):
                k = 2 * a + (a == 2) * 2
                if a:
                    dve.wait_ge(v_in, 16 * a)
                if ATT[a] == "L3":
                    flat = vs[:, 0:NC, :, :].rearrange("p c h v -> p c (h v)")
                    v.tensor_tensor(flat, flat, mask_T[:, 0:NC].unsqueeze(2).to_broadcast([P, NC, H * VC]), ALU.mult).then_inc(v_final, 1)
                else:
                    vl = vs[:, NC - 1, :, :]
                    v.tensor_scalar(vl, vl, valid_last[:, 0:1], None, ALU.mult).then_inc(v_final, 1)
                ln_dve(dve, chain, k)
                if ATT[a] == "L1":
                    for i in range(2):
                        cols = slice(512 * i, 512 * i + 512)
                        f = [w.rearrange("p c a k -> p (c a k)")[:, cols] for w in (kf[:, :, :, :], k_rest[:, :, :, :], kparts[:, 0], kparts[:, 1])]
                        dve.wait_ge(k_act, 3 * NTILE + i + 1)
                        if i == 0:
                            dve.wait_ge(k_part3, NTILE)
                            for b in range(2):
                                dve.wait_ge(k_out[b], KEYS_OUT[b])
                        v.tensor_tensor(f[1], f[0], f[2], ALU.subtract).then_inc(k_r1, 1)
                        dve.wait_ge(k_r1, NTILE + i + 1)
                        v.tensor_copy(f[3], f[1]).then_inc(k_part2, 1)
                    for i in range(2):
                        dve.wait_ge(v_ps, NC + i + 1)
                        last = v.tensor_copy(vs[:, NC + 4 * i:NC + 4 * i + 4, :, 0:HD],
                                             PS[:, 6 + i, :].rearrange("p (c h d) -> p c h d", c=4, h=H))
                    last.then_inc(xv_ready, 1)
                    for i in range(2):
                        dve.wait_ge(kn_ps, NTILE + i + 1)
                        v.reduce_max(kmax[0:32, NTILE + i:NTILE + i + 1], PS[0:32, i, :], X_AXIS).then_inc(kn_ev, 1)
                    dve.wait_ge(kn_ev, NTILE + 2)
                    chain(v.tensor_copy(kmax[32:64, NTILE:NTILE + 2], kmax[0:32, NTILE:NTILE + 2]))
                dve.wait_ge(q_act, a + 1)
                chain(v.tensor_tensor(qr1, qf, qparts[:, 0, :], ALU.subtract))
                chain(v.tensor_copy(qparts[:, 1, :], qr1))
                v.tensor_tensor(qparts[:, 2, :], qr1, qparts[:, 1, :], ALU.subtract).then_inc(q_split, 1)
                own = slice(32 * a, 32 * a + 32)
                dve.wait_ge(qn_ps, a + 1)
                dve.wait_ge(kn_ev, NTILE)
                v.reduce_max(q_max[own, :], PS[own, 4:6, :].rearrange("p b n -> p (b n)"), X_AXIS)
                chain(v.reduce_max(k_max[own, :], kmax[own, 0:NTILE + (2 if a == 1 else 0)], X_AXIS))
                v.tensor_tensor(bound[own, :], q_max[own, :], k_max[own, :], ALU.mult).then_inc(bound_ready, 1)
                if a == 0:
                    dve.wait_ge(gram_mm, NTILE)
                    chain(v.tensor_copy(gram[:, :], PS[:, 6, 0:D + 1]))
                    v.tensor_scalar(n_bv[:, :], b5[0:1, 4, :], float(CTX), None, ALU.mult)
                    v.tensor_scalar(sum_bk[:, :], b5[:, 3, :], gram[:, D:D + 1], None, ALU.mult).then_inc(gram_sb, 1)
                    dve.wait_ge(gram_ps, 1)
                    v.scalar_tensor_tensor(gram_v[:, :], b5[:, 4, :], gram[:, D:D + 1], PS[:, 7, 0:D], ALU.mult, ALU.add).then_inc(gram_sb, 1)
                    dve.wait_ge(gram_ps, 2)
                    v.tensor_tensor(kv_sum[:, :], PS[:, 6, 0:D], kv_mask[:, :], ALU.mult).then_inc(gram_sb, 1)
                dve.wait_ge(bound_in, 16 * (a + 1))
                chain(v.reduce_max(bound_max[:, :], bound_row[:, :], X_AXIS))
                v.tensor_scalar(flag[0:1, a:a + 1], bound_max[:, :], (SAFE / SCALE) ** 2, None, ALU.is_ge).then_inc(flag_ready, 1)
                dve.wait_ge(flag_ready, a + 1)
                need_max = dve.value_load(flag[0:1, a:a + 1], min_val=0, max_val=1)
                with dve.If(need_max > 0):
                    def reduce_scores(c, hh, q0, first=False, xc=0):
                        for r in range(4):
                            ps = PS[:, 4 * (r % 2):4 * (r % 2) + 4, :].rearrange("p b (n k) -> p (b n) k", k=P).rearrange("p (e n) k -> p e n k", e=2)[:, :, xc:, :]
                            run = run_max[:, hh * 8 + 2 * r:hh * 8 + 2 * r + 2, xc:]
                            new = new_max[:, :].rearrange("p (e n) -> p e n", e=2)[:, :, xc:]
                            dve.wait_ge(mx_ps[a], 4 * c + (q0 + r + 1))
                            if first:
                                v.reduce_max(run, ps, X_AXIS).then_inc(mx_red[a], 1)
                                dve.wait_ge(mx_red[a], 4 * c + (q0 + r + 1))
                            else:
                                v.reduce_max(new, ps, X_AXIS).then_inc(mx_red[a], 1)
                                dve.wait_ge(mx_red[a], 4 * c + (q0 + r + 1))
                                v.tensor_tensor(run, run, new, ALU.max).then_inc(mx_run[a], 1)
                                dve.wait_ge(mx_run[a], 4 * c + (q0 - 4 * hh - 3 + r))

                    nx = NT if a == 1 else 0
                    for hh in range(2):
                        q0 = 4 * hh * (NC + nx)
                        reduce_scores(0, hh, q0, first=True)
                        with dve.Fori(1, NC) as c:
                            reduce_scores(c, hh, q0)
                        for xc in range(nx):
                            reduce_scores(NC + xc, hh, q0, xc=xc)
                    dve.wait_ge(mx_tp[a], 1)
                    n0 = 8 * (NC + nx) - 8
                    for i, (o, i0, i1) in enumerate(((mneg, None, None), (mparts[:, 0], mneg, None), (mr1, mneg, mparts[:, 0]),
                                                     (mparts[:, 1], mr1, None), (mparts[:, 2], mr1, mparts[:, 1]))):
                        if i == 0:
                            ins = v.tensor_scalar(o[:, :], PS[:, 0, 0:P], -1.0, None, ALU.mult)
                        elif i1 is None:
                            ins = v.tensor_copy(o[:, :], i0[:, :])
                        else:
                            ins = v.tensor_tensor(o[:, :], i0[:, :], i1[:, :], ALU.subtract)
                        if i == 4:
                            ins.then_inc(mx_dve[a], 1)
                        else:
                            ins.then_inc(mx_run[a], 1)
                            dve.wait_ge(mx_run[a], n0 + i + 1)
                dve.end_ifs()

                for s in SWEEPS[4 * a:4 * a + 4]:
                    dve.wait_ge(pv_done, s.groups + 2 * s.n)
                    v.tensor_copy(accs[:, 2 * s.hh:2 * s.hh + 2, 512 * s.qh:512 * s.qh + 512], PS[:, 6:8, :]).then_inc(acc_ev, 1)
                for n in range(NT):
                    dve.wait_ge(at_ps, NT * a + n + 1)
                    heads = PS[:, n, :].rearrange("p (h w) -> p h w", w=32)
                    chain(v.reciprocal(rden[:, n, :].unsqueeze(2), heads[:, :, HD:VC]))
                    v.tensor_tensor(att[:, n, :].rearrange("p (h d) -> p h d", h=H), heads[:, :, 0:HD],
                                    rden[:, n, :].unsqueeze(2).to_broadcast([P, H, HD]), ALU.mult).then_inc(at_rd, 1)
                add_to_x(dve, (0, 1, 3)[a], PS[:, 2:4, :].rearrange("p b n -> p (b n)"), y_ps, a + 1, k)
                between_dve(dve, chain, a)


def kernel(**inputs):
    import numpy as _np
    import concourse.bacc as _bacc
    from concourse import mybir as _mybir
    from concourse.bass_utils import run_bass_kernel_spmd as _run

    nc = _bacc.Bacc("TRN2", target_bir_lowering=False, num_devices=1)
    arrays, t = {}, {}
    for name, value in inputs.items():
        a = _np.ascontiguousarray(value)
        arrays[f"in_{name}"] = a
        t[name] = nc.dram_tensor(f"in_{name}", a.shape, _mybir.dt.from_np(a.dtype), kind="ExternalInput").ap()
    out = nc.dram_tensor("out", (1, S, D), F32, kind="ExternalOutput").ap()
    ks = nc.dram_tensor("key_parts", (NC + NT, 3, KROWS + SPLIT + 1, H, P), BF16, kind="Internal").ap()
    v_scr = nc.dram_tensor("values", (P, NC, 2, H * VC), F32, kind="Internal").ap()
    q_scr = nc.dram_tensor("query_parts", (SPLIT, P, S), BF16, kind="Internal").ap()
    m_scr = nc.dram_tensor("maximum_parts", (SPLIT, P, P), BF16, kind="Internal").ap()
    row_scr = nc.dram_tensor("constant_rows", (SPLIT + 1, H * S), BF16, kind="Internal").ap()
    flamingo_decoder(nc, t, out, ks, v_scr, q_scr, m_scr, row_scr)
    r = _run(nc, [arrays], core_ids=[0])
    return r.results[0]["out"]
```

```python
from contextlib import ExitStack

import concourse.bass as bass
from concourse import mybir

F32 = mybir.dt.float32
BF16 = mybir.dt.bfloat16
I32 = mybir.dt.int32
U8 = mybir.dt.uint8
ALU = mybir.AluOpType
ACT = mybir.ActivationFunctionType
X_AXIS = mybir.AxisListType.X

P = 128
S = 1024
D = 128
NT = S // P
CTX = 6404
H = 16
HD = D // H
NC = -(-CTX // P)
LAST = CTX - (NC - 1) * P
TC = 3
NTILE = NC // TC
TW = TC * P
UNROLL = 4
SPLIT = 3
KROWS = SPLIT * HD
SROWS = SPLIT * KROWS + SPLIT + 1
SCALE = float(HD) ** -0.5
BIG = 1e30
SAFE = 60.0
LN_EPS = 1e-5
VC = HD + 1
ATT = ("L0", "L1", "L3")
NSW = 4
WEIGHTS_LATE = 16 * (9 + 3 + 2)
assert NTILE * TC == NC and (NTILE - 1) % UNROLL == 0 and SROWS <= P


class Chain:

    def __init__(self, eng, sem):
        self.eng, self.sem, self.n = eng, sem, 0

    def __call__(self, ins):
        ins.then_inc(self.sem, 1)
        self.n = self.n + 1
        self.eng.wait_ge(self.sem, self.n)


class Sweep:

    def __init__(self, w, a, hh, qh, nx, before):
        self.w, self.a, self.hh, self.qh, self.nx = w, a, hh, qh, nx
        self.n = NC + nx
        self.chunks = sum(s.n for s in before)
        self.pairs = 4 * self.chunks
        self.groups = 2 * self.chunks
        self.ring = [sum(-(-(s.n - b) // TC) for s in before) for b in range(TC)]
        self.aligned = all(s.n % TC == 0 for s in before[-1:])

    def seen(self, c):
        return max(0, P * (c - NC - 4 * self.qh))


SWEEPS = []
for _a in range(len(ATT)):
    for _hh in range(2):
        for _qh in range(2):
            _nx = (NT // 2) * (_qh + 1) if ATT[_a] == "L1" else 0
            SWEEPS.append(Sweep(len(SWEEPS), _a, _hh, _qh, _nx, SWEEPS))


def flamingo_decoder(nc, t, out, ks, v_scr, q_scr, m_scr, row_scr):
    with ExitStack() as ctx:
        def sb(name, shape, dt=F32):
            return ctx.enter_context(nc.sbuf_tensor(name, shape, dt))

        def sem(name):
            return ctx.enter_context(nc.semaphore(name))

        PS = ctx.enter_context(nc.psum_tensor("PS", [P, 8, 512], F32))

        ident = sb("ident", [P, P])
        ident_b = sb("ident_b", [P, P], BF16)
        head_of = sb("head_of", [P, 32])
        stair = sb("stair", [P, P], BF16)
        upper = sb("upper", [P, P], BF16)
        ones_row = sb("ones_row", [1, P])
        zero_one = sb("zero_one", [P, 2, P], BF16)
        valid = sb("valid", [64, P])
        valid_last = sb("valid_last", [P, 1])
        wk_in = sb("wk_in", [P, 3, D])
        wk = sb("wk", [P, 3, D])
        wq_in = sb("wq_in", [P, 3, D])
        wq = sb("wq", [P, 3, D])
        wo = sb("wo", [P, 3, D])
        bo = sb("bo", [1, 3, D])
        bqk = sb("bqk", [P, 2, 3])
        wv5 = sb("wv5", [P, 5, D])
        l2w = sb("l2w", [P, 3, D])
        l2wq = sb("l2wq", [P, D])
        b5 = sb("b5", [P, 5, D])
        gates_raw = sb("gates_raw", [P, 8])
        gates = sb("gates", [P, 8])
        c_in0 = sb("c_in0", [P, TC, D + 1])
        c_last = sb("c_last", [P, D + 1])
        c_T0 = sb("c_T0", [P, TW])
        kf = sb("kf", [P, TC, 3, P])
        k_rest = sb("k_rest", [P, TC, 3, P])
        ksq = sb("ksq", [P, 3, TW])
        kparts = sb("kparts", [P, SPLIT, TC, 3, P], BF16)
        gram = sb("gram", [P, D + 1])
        sum_bk = sb("sum_bk", [P, D])
        n_bv = sb("n_bv", [1, D])
        gram_v = sb("gram_v", [P, D])
        vs = sb("vs", [P, NC + NT, H, VC])
        v_next = sb("v_next", [P, TC, 2, H, VC])
        kmax = sb("kmax", [P, NTILE + 2])
        mask_u8 = sb("mask_u8", [64, P], U8)
        mask_f = sb("mask_f", [64, P])
        mask_rows = sb("mask_rows", [64, 2, P], BF16)
        mask_T = sb("mask_T", [P, 64])
        kv_mask = sb("kv_mask", [P, P])
        kv_sum = sb("kv_sum", [P, P])
        x = sb("x", [P, NT, D])
        xn = sb("xn", [P, NT, D])
        xT = sb("xT", [P, S])
        ln_st = sb("ln_st", [P, NT, 6])
        ln_mv = sb("ln_mv", [P, NT, 2])
        ln_ve = sb("ln_ve", [P, NT])
        ln_sd = sb("ln_sd", [P, NT])
        ln_rs = sb("ln_rs", [P, NT])
        accs = sb("accs", [P, 4, S])
        qf, qr1, qsq = (accs[:, i, :] for i in range(3))
        qparts = sb("qparts", [P, SPLIT, S], BF16)
        q_max = sb("q_max", [P, 1])
        k_max = sb("k_max", [P, 1])
        bound = sb("bound", [P, 1])
        bound_row = sb("bound_row", [1, H])
        bound_max = sb("bound_max", [1, 1])
        flag = sb("flag", [1, 3], I32)
        wide = sb("wide", [P, H, S], BF16)
        qs = wide[0:SROWS, :, :].rearrange("p h n -> p (h n)").rearrange("p (q h n) -> p q h n", q=NSW, h=H // 2)
        kr = [sb(f"kr{b}", [SROWS, H // 2, P], BF16) for b in range(TC)]
        vr = [sb(f"vr{b}", [P, H // 2, 32]) for b in range(TC)]
        probs = sb("probs", [P, 4, 2, 512])
        prob = [probs[:, i] for i in range(4)]
        spare = probs[:, :, :, :].rearrange("p i e n -> p (i e n)")
        spare2 = accs[:, :, :].rearrange("p g n -> p (g n)")
        at_v = SPLIT * 3 * TW // 2
        kparts2 = [kparts[:, :, :, :, :], spare[:, 0:at_v].bitcast(BF16).rearrange("p (s c a k) -> p s c a k", s=SPLIT, c=TC, a=3)]
        v_next2 = [v_next[:, :, :, :, :], spare[:, at_v:at_v + TC * 2 * H * VC].rearrange("p (c a h v) -> p c a h v", c=TC, a=2, h=H)]
        kf2 = [kf[:, :, :, :], spare2[:, 0:3 * TW].rearrange("p (c a k) -> p c a k", c=TC, a=3)]
        at_c = [3 * TW + TC * (D + 1) * i for i in range(UNROLL)]
        c_in = [c_in0[:, :, :]] + [spare2[:, o:o + TC * (D + 1)].rearrange("p (c d) -> p c d", c=TC) for o in at_c[:-1]]
        c_T = [c_T0[:, :], spare2[:, at_c[-1]:at_c[-1] + TW]]
        rden = sb("rden", [P, NT, H])
        att, att_T = xn, xT
        run_max = sb("run_max", [P, H, NT])
        new_max = sb("new_max", [P, 2 * NT])
        mneg = sb("mneg", [P, P])
        mr1 = sb("mr1", [P, P])
        mparts = sb("mparts", [P, SPLIT, P], BF16)

        ident_ready = sem("ident_ready")
        first_const = sem("first_const")
        const_ready = sem("const_ready")
        w_in = sem("w_in")
        wv_in = sem("wv_in")
        b_in = sem("b_in")
        w_late = sem("w_late")
        rows_in = sem("rows_in")
        rows_ready = sem("rows_ready")
        rows_out = sem("rows_out")
        wprep_ps = sem("wprep_ps")
        wprep_ready = sem("wprep_ready")
        c_loaded = [sem(f"c_loaded{b}") for b in range(UNROLL)]
        ct_ps = sem("ct_ps")
        ct_ready = sem("ct_ready")
        k_ps = sem("k_ps")
        k_act = sem("k_act")
        k_r1 = sem("k_r1")
        k_part2 = sem("k_part2")
        k_part3 = sem("k_part3")
        k_out = [sem(f"k_out{b}") for b in range(2)]
        v_ps = sem("v_ps")
        v_ev = sem("v_ev")
        gram_mm = sem("gram_mm")
        gram_sb = sem("gram_sb")
        gram_ps = sem("gram_ps")
        kn_ps = sem("kn_ps")
        kn_ev = sem("kn_ev")
        v_out = [sem(f"v_out{b}") for b in range(2)]
        v_in = sem("v_in")
        v_final = sem("v_final")
        xv_ready = sem("xv_ready")
        x_in = sem("x_in")
        x_ready = sem("x_ready")
        x_out = sem("x_out")
        ln_var = sem("ln_var")
        ln_root = sem("ln_root")
        ln_xn = sem("ln_xn")
        ln_ps = sem("ln_ps")
        ln_xT = sem("ln_xT")
        q_ps = sem("q_ps")
        q_act = sem("q_act")
        q_split = sem("q_split")
        qn_ps = sem("qn_ps")
        bound_ready = sem("bound_ready")
        bound_in = sem("bound_in")
        flag_ready = sem("flag_ready")
        q_out = sem("q_out")
        qs_in = sem("qs_in")
        kr_in = [sem(f"kr_in{b}") for b in range(TC)]
        v_copied = sem("v_copied")
        s_ready = sem("s_ready")
        p_ready = sem("p_ready")
        pv_done = sem("pv_done")
        acc_ev = sem("acc_ev")
        at_ps = sem("at_ps")
        at_rd = sem("at_rd")
        atT_ps = sem("atT_ps")
        atT_ready = sem("atT_ready")
        y_ps = sem("y_ps")
        mx_in = [sem(f"mx_in{a}") for a in range(3)]
        mx_ps = [sem(f"mx_ps{a}") for a in range(3)]
        mx_red = [sem(f"mx_red{a}") for a in range(3)]
        mx_tp = [sem(f"mx_tp{a}") for a in range(3)]
        mx_run = [sem(f"mx_run{a}") for a in range(3)]
        mx_dve = [sem(f"mx_dve{a}") for a in range(3)]
        mx_out = [sem(f"mx_out{a}") for a in range(3)]
        dve_c = sem("dve_c")
        act_c = sem("act_c")
        pool_c = sem("pool_c")

        block = ctx.enter_context(nc.Block())

        def dh(ap):
            return ap.rearrange("p (h d) -> p d h", h=H)

        def norm_stats(chain, src):
            v = nc.vector
            for n in range(NT):
                last = v.bn_stats(ln_st[:, n, :], src[:, n, :])
            chain(last)
            for n in range(NT):
                last = v.bn_aggr(ln_mv[:, n, :], ln_st[:, n, :])
            chain(last)
            v.tensor_scalar(ln_ve[:, :], ln_mv[:, :, 1], LN_EPS, None, ALU.add).then_inc(ln_var, 1)

        def norm(dve, chain, src, dst, j, done=None, stats=True):
            v = nc.vector
            if stats:
                norm_stats(chain, src)
            dve.wait_ge(ln_root, j + 1)
            chain(v.reciprocal(ln_rs[:, :], ln_sd[:, :]))
            for n in range(NT):
                last = v.tensor_scalar(dst[:, n, :], src[:, n, :], ln_mv[:, n, 0:1], ln_rs[:, n:n + 1], ALU.subtract, ALU.mult)
                if done is not None and n % (NT // 2) == NT // 2 - 1:
                    last.then_inc(done, 1)
            return last

        def norm_at(k):
            return k + (k >= 5)

        def ln_dve(dve, chain, k):
            if k:
                dve.wait_ge(x_ready, k)
            norm(dve, chain, x, xn, norm_at(k), ln_xn, stats=(k > 0))

        def ln_act(act, k):
            act.wait_ge(ln_var, norm_at(k) + 1)
            nc.scalar.activation(ln_sd[:, :], ln_ve[:, :], ACT.Sqrt).then_inc(ln_root, 1)
            for i in range(2):
                act.wait_ge(ln_ps, 2 * k + i + 1)
                nc.scalar.activation(xT[:, 512 * i:512 * i + 512], PS[:, i, :], ACT.Copy).then_inc(ln_xT, 1)

        def ln_pe(pe, k):
            for i in range(2):
                pe.wait_ge(ln_xn, 2 * k + i + 1)
                for n in range(4):
                    last = nc.tensor.transpose(PS[:, i, n * P:n * P + P], xn[:, 4 * i + n, :], ident[:, :])
                last.then_inc(ln_ps, 1)

        def add_to_x(dve, gate, y, y_sem, val, k):
            dve.wait_ge(y_sem, val)
            xf = x[:, :, :].rearrange("p n d -> p (n d)")
            nc.vector.scalar_tensor_tensor(xf, y, gates[:, gate:gate + 1], xf, ALU.mult, ALU.add).then_inc(x_ready, 1)

        NODES, LEAVES, DEPTH = 15, 16, 4
        HC = LEAVES * 64 // P
        NETS = ("q", "k", "v")
        FSCALE = float(D) ** -0.5
        wide32 = wide[:, :, :].rearrange("p h n -> p (h n)").bitcast(F32)
        accs_flat = accs[:, :, :].rearrange("p g n -> p (g n)")
        probs_flat = probs[:, :, :, :].rearrange("p i e n -> p (i e n)")
        fw1 = [wide32[:, S * n:S * n + S] for n in range(3)]
        fw2 = [wide32[:, S * (3 + n):S * (4 + n)] for n in range(3)]
        rows_w = sb("rows_w", [96, P])
        cols_w = sb("cols_w", [P, 96])
        B1_AT, RMS_AT = 3 * NODES, 3 * NODES + 3 * HC
        node_b = sb("node_b", [P, 3 * NODES])
        leaf_b2 = sb("leaf_b2", [96, 3, D])
        leaf_sel = sb("leaf_sel", [96, HC, P], BF16)
        bits = sb("bits", [P, NT * 3, NODES])
        paths = [None] + [sb(f"path{l}", [P, NT * 3, 2 ** l]) for l in range(1, DEPTH)]
        leaf = sb("leaf", [P, NT * 3, 32])
        leaf_T = wide32[0:96, 6 * S:7 * S]
        leaf_Tb = wide32[0:96, 7 * S:7 * S + S // 2].bitcast(BF16)
        hid = [probs_flat[:, 512 * r:512 * r + 512] for r in range(4)]
        qkv = [accs[:, n, :] for n in range(3)]
        v_tok = accs[:, 3, :]
        prob_q = [probs_flat[:, S * i:S * i + S] for i in range(2)]
        prob_T = [probs_flat[:, S * (2 + i):S * (3 + i)] for i in range(2)]
        fmax = sb("fmax", [P, NT])
        fneg = sb("fneg", [P, NT])
        fden = sb("fden", [P, NT])
        frec = sb("frec", [P, NT])
        E1, E1S, HID1 = 14, 2, 256
        E2, E3, HID3, CAP = 8, 8, 512, 64
        rw1 = sb("rw1", [P, E1])
        rw3 = sb("rw3", [P, E3])
        countdown = sb("countdown", [P, LEAVES])
        tri = sb("tri", [P, P])
        ones = sb("ones", [P, P])
        logit = sb("logit", [P, NT, E1])
        rprob = sb("rprob", [P, NT, E1])
        work = sb("work", [P, NT, E1])
        sel1 = sb("sel1", [P, NT, E1])
        sel2 = sb("sel2", [P, NT, E1])
        egate = sb("egate", [P, NT, E1 + E1S])
        rmax = sb("rmax", [P, NT])
        rsum = sb("rsum", [P, NT])
        l2bq = sb("l2bq", [P, 1])
        gamma_b = sb("gamma_b", [P, 2, D])
        h_T = ksq[:, :, :].rearrange("p a k -> p (a k)")[:, 0:S]
        moe_acc = kf[:, :, :, :].rearrange("p c a k -> p (c a k)")[:, 0:S]
        moe_hid = [probs_flat, accs_flat]
        eA = [wide32[:, 2048 * i:2048 * i + 512] for i in range(2)]
        eB = [wide32[:, 2048 * i + 512:2048 * i + 1024] for i in range(2)]
        eC = [wide32[:, 2048 * i + 1024:2048 * i + 1536] for i in range(2)]

        f_in = sem("f_in")
        fw_in = [sem(f"fw_in_{net}") for net in NETS]
        l2_normed = sem("l2_normed")
        f_cols_ps = sem("f_cols_ps")
        f_cols = sem("f_cols")
        f_node = sem("f_node")
        f_leaf = sem("f_leaf")
        f_leafT_ps = sem("f_leafT_ps")
        f_leafT = sem("f_leafT")
        f_up = sem("f_up")
        f_relu = sem("f_relu")
        f_masked = sem("f_masked")
        f_out = sem("f_out")
        f_net_ps = sem("f_net_ps")
        f_net = sem("f_net")
        f_v_ps = sem("f_v_ps")
        f_v = sem("f_v")
        fa_s = sem("fa_s")
        fa_max = sem("fa_max")
        fa_p = sem("fa_p")
        fa_T = sem("fa_T")
        fa_Tc = sem("fa_Tc")
        fa_o = sem("fa_o")
        r_ps = sem("r_ps")
        r_cen = sem("r_cen")
        r_exp = sem("r_exp")
        r_sel = sem("r_sel")
        r_cum = sem("r_cum")
        ms_ready = sem("ms_ready")
        ms_root = sem("ms_root")
        ht_sb = sem("ht_sb")
        ht_ps = sem("ht_ps")
        ht_ready = sem("ht_ready")
        e_in = [sem(f"e_in{i}") for i in range(2)]
        down_in = [sem(f"down_in{i}") for i in range(2)]
        e_scaled = sem("e_scaled")
        h_ps = sem("h_ps")
        h_act = sem("h_act")
        h_mul = sem("h_mul")
        dn_ps = sem("dn_ps")
        dn_ev = sem("dn_ev")
        l2q_ps = sem("l2q_ps")
        l2q = sem("l2q")
        l2_ps = sem("l2_ps")

        class Moe:

            def __init__(self, n, chunks, up, func, scaled, gated, before):
                self.n, self.chunks, self.up, self.func, self.scaled, self.gated = n, chunks, up, func, scaled, gated
                self.units = 2 * chunks
                self.loads = 2 if up else 1
                self.e0 = sum(m.n for m in before)
                self.u0 = sum(m.n * m.units for m in before)
                self.mul0 = sum(m.n * m.units for m in before if m.up)
                self.in0 = sum(16 * m.loads * (m.n // 2) for m in before)
                self.down0 = sum(16 * (m.n // 2) for m in before)
                self.ev0 = sum(m.n for m in before if m.gated)
                self.ring = 2 if up else 4

        MOE = []
        MOE.append(Moe(E1 + E1S, HID1 // P, False, ACT.Silu, True, True, MOE[:]))
        MOE.append(Moe(E2, HID3 // P, True, ACT.Silu, False, False, MOE[:]))
        MOE.append(Moe(E3, HID3 // P, False, ACT.Gelu_apprx_tanh, False, True, MOE[:]))

        def late_weights(act):
            for n, net in enumerate(NETS):
                act.dma_start(rows_w[NODES * n:NODES * (n + 1), :], t[f"L0_ffn_{net}_node_w"][:, :]).then_inc(f_in, 16)
                act.dma_start(rows_w[B1_AT + HC * n:B1_AT + HC * (n + 1), :],
                             t[f"L0_ffn_{net}_b1"].rearrange("(c l) h -> c (l h)", c=HC)).then_inc(f_in, 16)
                act.dma_start(node_b[:, NODES * n:NODES * (n + 1)], t[f"L0_ffn_{net}_node_b"].partition_broadcast(P)).then_inc(f_in, 16)
                act.dma_start(leaf_b2[32 * n:32 * n + LEAVES, n, :], t[f"L0_ffn_{net}_b2"][:, :]).then_inc(f_in, 16)
            act.dma_start(rows_w[RMS_AT:RMS_AT + E1, :], t["L1_ffn_rms_w"][:, :]).then_inc(f_in, 16)
            act.dma_start(rows_w[RMS_AT + E1:RMS_AT + E1 + E1S, :], t["L1_ffn_rms_w_s"][:, :]).then_inc(f_in, 16)
            act.dma_start(rw1[:, :], t["L1_ffn_router_w"][:, :]).then_inc(f_in, 16)
            act.dma_start(rw3[:, :], t["L3_ffn_w_router"][:, :]).then_inc(f_in, 16)
            act.dma_start(l2bq[:, :], t["L2_xattn_bq"].unsqueeze(1), allow_slow_non_contiguous=True).then_inc(f_in, 16)
            act.dma_start(gamma_b[:, 0, :], t["L2_xattn_ln_gamma"].partition_broadcast(P)).then_inc(f_in, 16)
            act.dma_start(gamma_b[:, 1, :], t["L2_xattn_ln_beta"].partition_broadcast(P)).then_inc(f_in, 16)

        SMALL_IN = 16 * (4 * 3 + 7)

        def moe_sp(sp, m, parts, then=None):
            def first(e, i, use):
                for dst, src in use(e, i)[:-1]:
                    sp.dma_start(dst, src).then_inc(e_in[i], 16)

            def second(e, i, use):
                dst, src = use(e, i)[-1]
                sp.dma_start(dst, src).then_inc(down_in[i], 16)

            for i in range(2):
                first(i, i, parts[0])
                second(i, i, parts[0])
            if then:
                then()
            last = m.n // 2 - (1 if len(parts) > 1 else 0)
            with sp.Fori(1, last) as j:
                for i in range(2):
                    sp.wait_ge(h_ps, j * (2 * m.units) + (m.u0 + m.units * (i - 1)))
                    first(2 * j + i, i, parts[0])
                    sp.wait_ge(dn_ps, 2 * j + (m.e0 + i - 1))
                    second(2 * j + i, i, parts[0])
            if len(parts) > 1:
                for i in range(2):
                    sp.wait_ge(h_ps, m.units * (m.n - 3 + i) + m.u0)
                    first(i, i, parts[1])
                    sp.wait_ge(dn_ps, m.e0 + m.n - 3 + i)
                    second(i, i, parts[1])

        def between_sp(sp, a, load_values):
            if a == 0:
                for n, net in enumerate(NETS):
                    sp.dma_start(fw1[n].rearrange("p (l h) -> p l h", l=LEAVES), t[f"L0_ffn_{net}_w1"].rearrange("l d h -> d l h")).then_inc(fw_in[n], 16)
                    sp.dma_start(fw2[n].rearrange("p (c o) -> p c o", c=HC),
                                 t[f"L0_ffn_{net}_w2"].rearrange("(c l) h o -> (l h) c o", c=HC)).then_inc(fw_in[n], 16)
                load_values()
            if a == 1:
                def shared(e, i):
                    return ((eA[i][:, 0:HID1], t["L1_ffn_w1_s"][e]),
                            (eC[i][:, 0:HID1].rearrange("p (c o) -> p c o", c=2), t["L1_ffn_w2_s"][e].rearrange("(c p) o -> p c o", p=P)))

                def routed(e, i):
                    return ((eA[i][:, 0:HID1], t["L1_ffn_w1"][bass.ds(e, 1), :, :].rearrange("e d f -> (e d) f")),
                            (eC[i][:, 0:HID1].rearrange("p (c o) -> p c o", c=2),
                             t["L1_ffn_w2"][bass.ds(e, 1), :, :].rearrange("e (c p) o -> p (e c) o", p=P)))

                moe_sp(sp, MOE[0], (routed, shared), load_values)

                def swiglu(e, i):
                    return ((eA[i], t["L2_ffn_Wg"][bass.ds(e, 1), :, :].rearrange("e d f -> (e d) f")),
                            (eB[i], t["L2_ffn_Wu"][bass.ds(e, 1), :, :].rearrange("e d f -> (e d) f")),
                            (eC[i].rearrange("p (c o) -> p c o", c=4),
                             t["L2_ffn_Wd"][bass.ds(e, 1), :, :].rearrange("e (c p) o -> p (e c) o", p=P)))

                sp.wait_ge(dn_ps, MOE[1].e0)
                moe_sp(sp, MOE[1], (swiglu,))
            if a == 2:
                def gelu_expert(e, i):
                    return ((eA[i], t["L3_ffn_wi"][bass.ds(e, 1), :, :].rearrange("e d f -> (e d) f")),
                            (eC[i].rearrange("p (c o) -> p c o", c=4),
                             t["L3_ffn_wo"][bass.ds(e, 1), :, :].rearrange("e (c p) o -> p (e c) o", p=P)))

                moe_sp(sp, MOE[2], (gelu_expert,))

        def const_pool(g, chain):
            chain(g.memset(leaf_sel[:, :, :], 0.0))
            for n in range(3):
                ls = leaf_sel[:, :, :].rearrange("p c (l h) -> p c l h", l=2)
                chain(g.affine_select(out=ls, in_=ls, compare_op=ALU.not_equal, fill=1.0,
                                      base=-32 * n, pattern=[[-2, HC], [-1, 2], [0, 64]], channel_multiplier=1))
            chain(g.iota(countdown[:, :], pattern=[[-1, LEAVES]], base=LEAVES, channel_multiplier=0,
                         allow_small_or_imprecise_dtypes=True))
            chain(g.memset(ones[:, :], 1.0))
            chain(g.affine_select(out=tri[:, :], in_=ones[:, :], compare_op=ALU.is_ge, fill=0.0,
                                  base=0, pattern=[[1, P]], channel_multiplier=-1))
            g.memset(leaf[:, :, :], 0.0)
            g.memset(rows_w[:, :], 0.0)
            g.memset(leaf_b2[:, :, :], 0.0)
            chain(g.memset(egate[:, :, E1:E1 + E1S], 1.0))

        def between_pool(pool, a):
            if a == 1:
                m = MOE[0]
                pool.wait_ge(f_cols, 1)

                def scale(e, i, loads):
                    pool.wait_ge(e_in[i], loads)
                    nc.gpsimd.tensor_tensor(eA[i][:, 0:HID1], eA[i][:, 0:HID1],
                                             cols_w[:, bass.ds(e + RMS_AT, 1)].to_broadcast([P, HID1]), ALU.mult).then_inc(e_scaled, 1)

                for i in range(2):
                    scale(i, i, m.in0 + 16 * m.loads)
                with pool.Fori(1, m.n // 2) as j:
                    for i in range(2):
                        scale(2 * j + i, i, j * (16 * m.loads) + (m.in0 + 16 * m.loads))
                pool.wait_ge(v_in, 32)
                flat = vs[:, 0:NC, :, :].rearrange("p c h v -> p c (h v)")
                nc.gpsimd.tensor_tensor(flat, flat, mask_T[:, 0:NC].unsqueeze(2).to_broadcast([P, NC, H * VC]), ALU.mult).then_inc(v_final, 1)

        def moe_pe(pe, m, hT):
            te = nc.tensor

            def up(e, i, loads, first=False):
                pe.wait_ge(e_in[i], loads)
                if m.scaled:
                    pe.wait_ge(e_scaled, e + 1)
                for k in range(m.units):
                    c, half = divmod(k, 2)
                    if not (first and k < m.ring):
                        if m.up:
                            pe.wait_ge(h_mul, m.units * e + (m.mul0 + k - m.ring + 1))
                        else:
                            pe.wait_ge(h_act, m.units * e + (m.u0 + k - m.ring + 1))
                    last = te.matmul(PS[:, slot(m, k, i), :], eA[i][:, P * c:P * c + P], hT[:, 512 * half:512 * half + 512], start=True, stop=True)
                    if m.up:
                        last = te.matmul(PS[:, 3 + slot(m, k, i), :], eB[i][:, P * c:P * c + P], hT[:, 512 * half:512 * half + 512], start=True, stop=True)
                    last.then_inc(h_ps, 1)

            def down(e, i, loads, first=False):
                pe.wait_ge(down_in[i], loads)
                if m.up:
                    pe.wait_ge(h_mul, m.units * e + (m.mul0 + m.units))
                else:
                    pe.wait_ge(h_act, m.units * e + (m.u0 + m.units))
                if m.gated and not first:
                    pe.wait_ge(dn_ev, e + m.ev0)
                for n in range(NT):
                    for c in range(m.chunks):
                        last = te.matmul(PS[:, 6 + n // 4, n % 4 * P:n % 4 * P + P], moe_hid[i][:, S * c + P * n:S * c + P * n + P],
                                         eC[i][:, P * c:P * c + P], start=(c == 0 and (m.gated or (first and n % 4 == 0))), stop=True,
                                         skip_group_check=True)
                last.then_inc(dn_ps, 1)

            per = 16 * m.loads
            up(0, 0, m.in0 + per, True)
            up(1, 1, m.in0 + per)
            down(0, 0, m.down0 + 16, True)
            with pe.Fori(1, m.n // 2) as j:
                up(2 * j, 0, j * per + (m.in0 + per))
                down(2 * j - 1, 1, j * 16 + m.down0)
                up(2 * j + 1, 1, j * per + (m.in0 + per))
                down(2 * j, 0, j * 16 + (m.down0 + 16))
            down(m.n - 1, 1, m.down0 + m.n // 2 * 16)

        def slot(m, k, i):
            return (m.units * i + k) % m.ring

        def moe_act(act, m):
            def units(e, i, first=False):
                for k in range(m.units):
                    c, half = divmod(k, 2)
                    act.wait_ge(h_ps, m.units * e + (m.u0 + k + 1))
                    if k == 0 and not first:
                        act.wait_ge(dn_ps, e + (m.e0 - 1))
                    nc.scalar.activation(moe_hid[i][:, S * c + 512 * half:S * c + 512 * half + 512], PS[:, slot(m, k, i), :], m.func).then_inc(h_act, 1)

            units(0, 0, True)
            units(1, 1, True)
            with act.Fori(1, m.n // 2) as j:
                units(2 * j, 0)
                units(2 * j + 1, 1)

        def moe_dve(dve, m):
            v = nc.vector

            def mul(e, i):
                if not m.up:
                    return
                for k in range(m.units):
                    c, half = divmod(k, 2)
                    o = moe_hid[i][:, S * c + 512 * half:S * c + 512 * half + 512]
                    dve.wait_ge(h_act, m.units * e + (m.u0 + k + 1))
                    v.tensor_tensor(o, o, PS[:, 3 + slot(m, k, i), :], ALU.mult).then_inc(h_mul, 1)

            def add(e, first=False):
                if not m.gated:
                    return
                dve.wait_ge(dn_ps, e + (m.e0 + 1))
                if not first:
                    dve.wait_ge(dn_ev, e + m.ev0)
                for n in range(NT):
                    o = PS[:, 6 + n // 4, n % 4 * P:n % 4 * P + P]
                    g = egate[:, n, bass.ds(e, 1)]
                    if first:
                        last = v.tensor_scalar(moe_acc[:, P * n:P * n + P], o, g, None, ALU.mult)
                    else:
                        last = v.scalar_tensor_tensor(moe_acc[:, P * n:P * n + P], o, g, moe_acc[:, P * n:P * n + P], ALU.mult, ALU.add)
                last.then_inc(dn_ev, 1)

            mul(0, 0)
            mul(1, 1)
            add(0, True)
            with dve.Fori(1, m.n // 2) as j:
                mul(2 * j, 0)
                add(2 * j - 1)
                mul(2 * j + 1, 1)
                add(2 * j)
            add(m.n - 1)

        def router_pe(pe, rw, n_e, k):
            for n in range(NT):
                last = nc.tensor.matmul(PS[:, 2, n * n_e:(n + 1) * n_e], xT[:, n * P:(n + 1) * P], rw[:, :], start=True, stop=True)
            last.then_inc(r_ps, 1)

        def router_act(act, n_e, i):
            act.wait_ge(r_cen, i + 1)
            nc.scalar.activation(work[:, :, 0:n_e], logit[:, :, 0:n_e], ACT.Exp).then_inc(r_exp, 1)

        def router_dve(dve, chain, n_e, i):
            v = nc.vector

            def bc(a):
                return a.unsqueeze(2).to_broadcast([P, NT, n_e])

            ps = PS[:, 2, 0:NT * n_e].rearrange("p (n e) -> p n e", e=n_e)
            lg, pr, wk_, s1, s2 = (w[:, :, 0:n_e] for w in (logit, rprob, work, sel1, sel2))
            count = countdown[:, LEAVES - n_e:LEAVES].unsqueeze(1).to_broadcast([P, NT, n_e])
            dve.wait_ge(r_ps, i + 1)
            chain(v.reduce_max(rmax[:, :], ps, X_AXIS))
            v.tensor_tensor(lg, ps, bc(rmax[:, :]), ALU.subtract).then_inc(r_cen, 1)
            dve.wait_ge(r_exp, i + 1)
            chain(v.reduce_sum(rsum[:, :], wk_, X_AXIS))
            chain(v.reciprocal(rsum[:, :], rsum[:, :]))
            chain(v.tensor_tensor(pr, wk_, bc(rsum[:, :]), ALU.mult))
            for s, src in ((s1, pr), (s2, lg)):
                chain(v.reduce_max(rmax[:, :], src, X_AXIS))
                chain(v.tensor_tensor(wk_, src, bc(rmax[:, :]), ALU.is_ge))
                chain(v.tensor_tensor(wk_, wk_, count, ALU.mult))
                chain(v.reduce_max(rmax[:, :], wk_, X_AXIS))
                chain(v.tensor_tensor(s, wk_, bc(rmax[:, :]), ALU.is_equal))
                if s is s1:
                    chain(v.scalar_tensor_tensor(lg, s1, -2.0, pr, ALU.mult, ALU.add))

        def fff_dve(dve, chain):
            v = nc.vector
            dve.wait_ge(f_node, 1)
            ps = PS[:, 2, 0:NT * 3 * NODES].rearrange("p (n m) -> p n m", n=NT)
            b3 = bits[:, :, :].rearrange("p (n m) k -> p n (m k)", n=NT)
            chain(v.tensor_tensor(b3, ps, node_b[:, :].unsqueeze(1).to_broadcast([P, NT, 3 * NODES]), ALU.add))
            chain(v.tensor_scalar(b3, b3, 0.0, None, ALU.is_ge))
            for l in range(DEPTH):
                w = 2 ** l
                dst = leaf[:, :, 0:LEAVES] if l == DEPTH - 1 else paths[l + 1][:, :, :]
                dst = dst.rearrange("p m (w s) -> p m w s", s=2)
                b = bits[:, :, w - 1:2 * w - 1]
                if l == 0:
                    v.tensor_copy(dst[:, :, :, 1], b)
                    chain(v.tensor_scalar(dst[:, :, :, 0], b, -1.0, 1.0, ALU.mult, ALU.add))
                else:
                    chain(v.tensor_tensor(dst[:, :, :, 1], paths[l][:, :, :], b, ALU.mult))
                    last = v.tensor_tensor(dst[:, :, :, 0], paths[l][:, :, :], dst[:, :, :, 1], ALU.subtract)
                    if l < DEPTH - 1:
                        chain(last)
            last.then_inc(f_leaf, 1)
            for u in range(3 * 2 * HC):
                dve.wait_ge(f_relu, u + 1)
                v.tensor_tensor(hid[u % 4], hid[u % 4], PS[:, 2 + u % 2, :], ALU.mult).then_inc(f_masked, 1)
            dve.wait_ge(f_v_ps, 1)
            v.tensor_copy(v_tok, PS[:, 6:8, :].rearrange("p b n -> p (b n)")).then_inc(f_v, 1)

            def copy_T(n):
                dve.wait_ge(fa_T, n + 1)
                if n >= 2:
                    dve.wait_ge(fa_o, n - 1)
                v.tensor_copy(prob_T[n % 2], PS[:, 4:6, :].rearrange("p b n -> p (b n)")).then_inc(fa_Tc, 1)

            for n in range(NT):
                dve.wait_ge(fa_s, n + 1)
                b = 2 * (n % 2)
                chain(v.reduce_max(fmax[:, n:n + 1], PS[:, b:b + 2, :].rearrange("p b n -> p (b n)"), X_AXIS))
                v.tensor_scalar(fneg[:, n:n + 1], fmax[:, n:n + 1], -FSCALE, None, ALU.mult).then_inc(fa_max, 1)
                if n:
                    copy_T(n - 1)
            copy_T(NT - 1)
            dve.wait_ge(fa_p, NT)
            chain(v.reciprocal(frec[:, :], fden[:, :]))
            chain(v.tensor_scalar(frec[:, :], frec[:, :], gates[:, 4:5], None, ALU.mult))
            dve.wait_ge(fa_o, NT)
            for n in range(NT):
                last = v.scalar_tensor_tensor(x[:, n, :], PS[:, 6 + n // 4, n % 4 * P:n % 4 * P + P], frec[:, n:n + 1], x[:, n, :], ALU.mult, ALU.add)
            last.then_inc(x_ready, 1)

        def fff_act(act):
            sc = nc.scalar
            act.wait_ge(f_leafT_ps, 1)
            ps = PS[0:96, 4:6, :].rearrange("p b n -> p (b n)")
            sc.activation(leaf_T, ps, ACT.Copy)
            sc.activation(leaf_Tb, ps, ACT.Copy).then_inc(f_leafT, 1)
            for u in range(3 * 2 * HC):
                net, k = divmod(u, 2 * HC)
                act.wait_ge(f_up, u + 1)
                if u >= 4:
                    act.wait_ge(f_out, u - 3)
                col = B1_AT + HC * net + k // 2
                sc.activation(hid[u % 4], PS[:, u % 2, :], ACT.Relu, bias=cols_w[:, col:col + 1]).then_inc(f_relu, 1)
                if k == 2 * HC - 1:
                    act.wait_ge(f_net_ps, net + 1)
                    b = 4 + 2 * (net % 2)
                    sc.activation(qkv[net], PS[:, b:b + 2, :].rearrange("p b n -> p (b n)"), ACT.Copy).then_inc(f_net, 1)
            for n in range(NT):
                act.wait_ge(fa_max, n + 1)
                if n >= 2:
                    act.wait_ge(fa_T, n - 1)
                b = 2 * (n % 2)
                sc.activation(prob_q[n % 2], PS[:, b:b + 2, :].rearrange("p b n -> p (b n)"), ACT.Exp,
                              bias=fneg[:, n:n + 1], scale=FSCALE, accum_out=fden[:, n:n + 1]).then_inc(fa_p, 1)

        def fff_pe(pe):
            te = nc.tensor
            pe.wait_ge(f_cols, 1)
            pe.wait_ge(ln_xT, 4)
            for n in range(NT):
                last = te.matmul(PS[:, 2, n * 3 * NODES:(n + 1) * 3 * NODES], xT[:, n * P:(n + 1) * P], cols_w[:, 0:3 * NODES], start=True, stop=True)
            last.then_inc(f_node, 1)
            pe.wait_ge(f_leaf, 1)
            for n in range(NT):
                last = te.transpose(PS[0:96, 4 + n // 4, n % 4 * P:n % 4 * P + P], leaf[:, 3 * n:3 * n + 3, :].rearrange("p m l -> p (m l)"), ident[:, :])
            last.then_inc(f_leafT_ps, 1)
            pe.wait_ge(f_leafT, 1)
            n_units = 3 * 2 * HC

            def up(u):
                net, k = divmod(u, 2 * HC)
                c, half = divmod(k, 2)
                cols = slice(512 * half, 512 * half + 512)
                if k == 0:
                    pe.wait_ge(fw_in[net], 32)
                if u >= 2:
                    pe.wait_ge(f_masked, u - 1)
                te.matmul(PS[:, u % 2, :], fw1[net][:, P * c:P * c + P], xT[:, cols], start=True, stop=True)
                te.matmul(PS[:, 2 + u % 2, :], leaf_sel[32 * net:32 * net + LEAVES, c, :], leaf_Tb[32 * net:32 * net + LEAVES, cols],
                          start=True, stop=True).then_inc(f_up, 1)

            def out(u):
                net, k = divmod(u, 2 * HC)
                c, half = divmod(k, 2)
                cols = slice(512 * half, 512 * half + 512)
                o = PS[:, 4 + 2 * (net % 2) + half, :]
                if net == 2 and k == 0:
                    pe.wait_ge(f_net, 1)
                pe.wait_ge(f_masked, u + 1)
                last = te.matmul(o, fw2[net][:, D * c:D * c + D], hid[u % 4], start=(c == 0), stop=False)
                last.then_inc(f_out, 1)
                if c == HC - 1:
                    last = te.matmul(o, leaf_b2[:, net, :], leaf_T[:, cols], start=False, stop=True)
                    if half:
                        last.then_inc(f_net_ps, 1)

            up(0)
            for u in range(n_units):
                if u + 1 < n_units:
                    up(u + 1)
                out(u)
            pe.wait_ge(f_net, 3)
            for n in range(NT):
                last = te.transpose(PS[:, 6 + n // 4, n % 4 * P:n % 4 * P + P], qkv[2][:, n * P:(n + 1) * P], ident[:, :])
            last.then_inc(f_v_ps, 1)

            def score(n):
                if n >= 2:
                    pe.wait_ge(fa_p, n - 1)
                for i in range(2):
                    last = te.matmul(PS[:, 2 * (n % 2) + i, :], qkv[0][:, n * P:(n + 1) * P], qkv[1][:, 512 * i:512 * i + 512], start=True, stop=True)
                last.then_inc(fa_s, 1)

            def turn(n):
                pe.wait_ge(fa_p, n + 1)
                if n:
                    pe.wait_ge(fa_Tc, n)
                for j in range(NT):
                    last = te.transpose(PS[:, 4 + j // 4, j % 4 * P:j % 4 * P + P], prob_q[n % 2][:, j * P:(j + 1) * P], ident[:, :])
                last.then_inc(fa_T, 1)

            def product(n):
                pe.wait_ge(fa_Tc, n + 1)
                for j in range(NT):
                    last = te.matmul(PS[:, 6 + n // 4, n % 4 * P:n % 4 * P + P], prob_T[n % 2][:, j * P:(j + 1) * P], v_tok[:, j * P:(j + 1) * P],
                                     start=(j == 0), stop=(j == NT - 1))
                last.then_inc(fa_o, 1)

            score(0)
            score(1)
            pe.wait_ge(f_v, 1)
            for n in range(NT):
                turn(n)
                if n + 2 < NT:
                    score(n + 2)
                product(n)

        def between_dve(dve, chain, a):
            v = nc.vector
            if a == 0:
                ln_dve(dve, chain, 1)
                fff_dve(dve, chain)
            if a == 1:
                ln_dve(dve, chain, 3)
                xnf, sq = xn[:, :, :], accs_flat[:, 0:S].rearrange("p (n d) -> p n d", n=NT)
                dve.wait_ge(ln_xn, 8)
                chain(v.tensor_tensor(sq, xnf, xnf, ALU.mult))
                chain(v.reduce_sum(ln_ve[:, :], sq, X_AXIS))
                v.tensor_scalar(ln_ve[:, :], ln_ve[:, :], 1.0 / D, 1.1920929e-07, ALU.mult, ALU.add).then_inc(ms_ready, 1)
                dve.wait_ge(ms_root, 1)
                chain(v.reciprocal(ln_rs[:, :], ln_sd[:, :]))
                for n in range(NT):
                    last = v.tensor_scalar(sq[:, n, :], xn[:, n, :], ln_rs[:, n:n + 1], None, ALU.mult)
                last.then_inc(ht_sb, 1)
                router_dve(dve, chain, E1, 0)
                g14 = egate[:, :, 0:E1]
                chain(v.tensor_tensor(work[:, :, :], sel1[:, :, :], sel2[:, :, :], ALU.add))
                chain(v.tensor_tensor(g14, work[:, :, :], rprob[:, :, :], ALU.mult))
                chain(v.reduce_sum(rsum[:, :], g14, X_AXIS))
                chain(v.tensor_scalar(rsum[:, :], rsum[:, :], 1e-9, None, ALU.add))
                chain(v.reciprocal(rsum[:, :], rsum[:, :]))
                chain(v.tensor_tensor(g14, g14, rsum[:, :].unsqueeze(2).to_broadcast([P, NT, E1]), ALU.mult))
                moe_dve(dve, MOE[0])
                add_to_x(dve, 5, moe_acc, dn_ev, MOE[1].ev0, 3)
                ln_dve(dve, chain, 4)
                z = accs[:, 1, :].rearrange("p (n d) -> p n d", n=NT)
                dve.wait_ge(l2_ps, 1)
                chain(v.scalar_tensor_tensor(accs[:, 1, :], PS[:, 4:6, :].rearrange("p b n -> p (b n)"), SCALE,
                                             xn[:, :, :].rearrange("p n d -> p (n d)"), ALU.mult, ALU.add))
                norm(dve, chain, z, z, 5).then_inc(l2_normed, 1)
                dve.wait_ge(l2_normed, 1)
                for i, op in ((0, ALU.mult), (1, ALU.add)):
                    chain(v.tensor_tensor(z, z, gamma_b[:, i, :].unsqueeze(1).to_broadcast([P, NT, D]), op))
                xf = x[:, :, :].rearrange("p n d -> p (n d)")
                v.scalar_tensor_tensor(xf, accs[:, 1, :], gates[:, 2:3], xf, ALU.mult, ALU.add).then_inc(x_ready, 1)
                ln_dve(dve, chain, 5)
                moe_dve(dve, MOE[1])
                add_to_x(dve, 6, PS[:, 6:8, :].rearrange("p b n -> p (b n)"), dn_ps, MOE[2].e0, 5)
            if a == 2:
                ln_dve(dve, chain, 7)
                router_dve(dve, chain, E3, 1)
                v.tensor_copy(egate[:, :, 0:E3], sel1[:, :, 0:E3])
                v.tensor_copy(egate[:, :, E3:2 * E3], sel2[:, :, 0:E3]).then_inc(r_sel, 1)
                s8 = [w[:, :, 0:E3] for w in (sel1, sel2, rprob, work, logit)]
                dve.wait_ge(r_cum, 1)
                chain(v.scalar_tensor_tensor(s8[3], PS[:, 5, 0:NT * E3].rearrange("p (n e) -> p n e", e=E3), float(CAP), s8[0], ALU.is_le, ALU.mult))
                chain(v.scalar_tensor_tensor(s8[4], PS[:, 5, NT * E3:2 * NT * E3].rearrange("p (n e) -> p n e", e=E3), float(CAP), s8[1], ALU.is_le, ALU.mult))
                chain(v.tensor_tensor(s8[3], s8[3], s8[4], ALU.add))
                chain(v.tensor_tensor(egate[:, :, 0:E3], s8[3], s8[2], ALU.mult))
                moe_dve(dve, MOE[2])
                add_to_x(dve, 7, moe_acc, dn_ev, MOE[2].ev0 + MOE[2].n, 7)

        def between_act(act, a):
            sc = nc.scalar
            if a == 0:
                ln_act(act, 1)
                fff_act(act)
            if a == 1:
                ln_act(act, 3)
                act.wait_ge(ms_ready, 1)
                sc.activation(ln_sd[:, :], ln_ve[:, :], ACT.Sqrt).then_inc(ms_root, 1)
                router_act(act, E1, 0)
                act.wait_ge(ht_ps, 1)
                sc.activation(h_T, PS[:, 4:6, :].rearrange("p b n -> p (b n)"), ACT.Copy).then_inc(ht_ready, 1)
                moe_act(act, MOE[0])
                ln_act(act, 4)
                act.wait_ge(l2q_ps, 1)
                sc.activation(accs[:, 0, :], PS[:, 2:4, :].rearrange("p b n -> p (b n)"), ACT.Identity, bias=l2bq[:, 0:1]).then_inc(l2q, 1)
                act.wait_ge(ln_var, 6)
                sc.activation(ln_sd[:, :], ln_ve[:, :], ACT.Sqrt).then_inc(ln_root, 1)
                ln_act(act, 5)
                moe_act(act, MOE[1])
            if a == 2:
                ln_act(act, 7)
                router_act(act, E3, 1)
                moe_act(act, MOE[2])

        def between_pe(pe, a):
            te = nc.tensor
            if a == 0:
                ln_pe(pe, 1)
                fff_pe(pe)
            if a == 1:
                ln_pe(pe, 3)
                pe.wait_ge(ht_sb, 1)
                for n in range(NT):
                    last = te.transpose(PS[:, 4 + n // 4, n % 4 * P:n % 4 * P + P], accs_flat[:, P * n:P * n + P], ident[:, :])
                last.then_inc(ht_ps, 1)
                pe.wait_ge(ln_xT, 8)
                router_pe(pe, rw1, E1, 0)
                pe.wait_ge(ht_ready, 1)
                moe_pe(pe, MOE[0], h_T)
                ln_pe(pe, 4)
                pe.wait_ge(ln_xT, 10)
                for i in range(2):
                    last = te.matmul(PS[:, 2 + i, :], l2wq[:, :], xT[:, 512 * i:512 * i + 512], start=True, stop=True)
                last.then_inc(l2q_ps, 1)
                pe.wait_ge(l2q, 1)
                for n in range(NT):
                    last = te.matmul(PS[:, 4 + n // 4, n % 4 * P:n % 4 * P + P], accs[:, 0, n * P:(n + 1) * P], kv_sum[:, :], start=True, stop=True)
                last.then_inc(l2_ps, 1)
                ln_pe(pe, 5)
                pe.wait_ge(ln_xT, 12)
                moe_pe(pe, MOE[1], xT)
            if a == 2:
                ln_pe(pe, 7)
                pe.wait_ge(ln_xT, 16)
                router_pe(pe, rw3, E3, 1)
                pe.wait_ge(r_sel, 1)
                c1, c2 = PS[:, 5, 0:NT * E3], PS[:, 5, NT * E3:2 * NT * E3]
                te.matmul(c1, tri[:, :], egate[:, :, 0:E3], start=True, stop=True)
                te.matmul(c2, ones[:, :], egate[:, :, 0:E3], start=True, stop=False)
                te.matmul(c2, tri[:, :], egate[:, :, E3:2 * E3], start=False, stop=True).then_inc(r_cum, 1)
                moe_pe(pe, MOE[2], xT)

        def xk_part(i, c):
            return kparts[:, c].rearrange("p c a k -> p (c a k)")[:, 512 * i:512 * i + 512]

        def at(j, off, per, add):
            return off * per + add if j is None else j * (UNROLL * per) + (off * per + add)

        ROWS_OUT = 16 * (2 + TC + 1 + 3)
        QUARTER = 16 * SPLIT
        QS_IN = 16 + NSW * QUARTER

        def load_queries(eng, hh, qh, done):
            for c in range(SPLIT):
                src = q_scr[c, qh].rearrange("(d h) n -> d (h n)", h=H)[:, hh * (H // 2) * 512:(hh + 1) * (H // 2) * 512]
                eng.dma_start(qs[KROWS * c:KROWS * (c + 1), 2 * hh + qh, :, :].rearrange("r h n -> r (h n)"),
                              src.unsqueeze(0).to_broadcast([SPLIT, HD, H // 2 * 512])).then_inc(done, 16)

        BIASES_IN = 16 * (4 + 4)
        ROWS_IN = 16 * 3
        MAX_OUT = QUARTER * (NSW - 1) + 16 * (SPLIT + NSW + 2)
        USES = [(NTILE + 1) // 2, NTILE // 2]
        KEYS_OUT = [16 * SPLIT * u for u in USES]
        ROUNDS = (NTILE - 1) // UNROLL - 1
        TAIL = range(ROUNDS * UNROLL + 1, NTILE)

        def buffer_out(eng, done, per, j, off):
            if j is not None:
                eng.wait_ge(done[off % 2], j * (UNROLL // 2 * per) + off // 2 * per)
            elif off >= 2:
                eng.wait_ge(done[off % 2], off // 2 * per)

        @block.sync
        def _(sp):
            ctx_rows = t["ctx_1024"][0]

            def load_ctx(j, off, n=TC):
                sp.dma_start(c_in[off % UNROLL][:, 0:n, 0:D],
                             ctx_rows[bass.ds(at(j, off, TW, 0), n * P), :].rearrange("(c p) d -> p c d", p=P)).then_inc(c_loaded[off % UNROLL], 16)

            load_ctx(None, 0)
            wkv = t["L1_xattn_Wkv"]
            for a, w in enumerate((t["L0_xattn_Wk"], wkv[:, 0:D], t["L3_xattn_Wk"])):
                sp.dma_start(wk_in[:, a, :], w).then_inc(w_in, 16)
            for a, w in enumerate((t["L0_xattn_Wv"], wkv[:, D:2 * D], t["L3_xattn_Wv"])):
                sp.dma_start(wv5[:, a, :], w).then_inc(wv_in, 16)
            for i in range(1, UNROLL):
                load_ctx(None, i)
            sp.wait_ge(first_const, 1)

            def k_step(j, off, ahead=TC):
                b = off % 2
                for c, (done, n) in enumerate(((k_act, 3), (k_part2, 1), (k_part3, 1))):
                    sp.wait_ge(done, at(j, off, n, n))
                    sp.dma_start(ks[bass.ds(at(j, off, TC, 0), TC), :, HD * c:HD * c + HD, :, :].rearrange("c a d h k -> (d h) (c a) k"),
                                 kparts2[b][:, c].rearrange("p c a k -> p (c a) k")).then_inc(k_out[b], 16)
                    if ahead and c == 0:
                        sp.wait_ge(gram_mm, at(j, off, 1, 1))
                        load_ctx(j, off + UNROLL, ahead)
                sp.wait_ge(v_ev, at(j, off, TC, TC))
                sp.dma_start(v_scr[:, bass.ds(at(j, off, TC, 0), TC), :, :].rearrange("p c m v -> p (c m v)"),
                             v_next2[b].rearrange("p c m h v -> p (c m h v)")).then_inc(v_out[b], 16)

            k_step(None, 0)
            with sp.Fori(0, ROUNDS - 1) as j:
                for off in range(1, UNROLL + 1):
                    k_step(j, off)
            for i in range((ROUNDS - 1) * UNROLL + 1, NTILE):
                n = i + UNROLL
                k_step(None, i, 0 if n >= NTILE else TC - 1 if n == NTILE - 1 else TC)

            for a in range(3):
                def load_keys(b, c, hh, done):
                    h0 = hh * (H // 2)
                    parts = ks[bass.ds(c, 1), a, 0:KROWS, h0:h0 + H // 2, :].rearrange("c r h k -> (c r) (h k)")
                    sp.dma_start(kr[b][0:SPLIT * KROWS, :, :].rearrange("r h k -> r (h k)"),
                                 parts.unsqueeze(0).to_broadcast([SPLIT, KROWS, H // 2 * P])).then_inc(done, 16)
                    row = ks[bass.ds(c, 1), a, KROWS:KROWS + 1, h0:h0 + H // 2, :].rearrange("c r h k -> (c r) (h k)")
                    sp.dma_start(kr[b][SROWS - 1:SROWS, :, :].rearrange("r h k -> r (h k)"), row).then_inc(done, 16)

                for b in range(2):
                    sp.wait_ge(k_out[b], KEYS_OUT[b] + (16 * SPLIT if a > 1 else 0))
                sp.wait_ge(rows_out, ROWS_OUT)
                for c in range(TC):
                    load_keys(c, c, 0, kr_in[c])
                if ATT[a] == "L1":
                    for i in range(2):
                        sp.wait_ge(k_act, 3 * NTILE + i + 1)
                        sp.wait_ge(k_part2, NTILE + i + 1)
                        sp.wait_ge(k_part3, NTILE + i + 1)
                        for c in range(SPLIT):
                            sp.dma_start(ks[NC + 4 * i:NC + 4 * i + 4, 1, HD * c:HD * c + HD, :, :].rearrange("c d h k -> (d h) c k"),
                                         xk_part(i, c).rearrange("p (c k) -> p c k", c=4)).then_inc(k_out[i], 16)
                if a:
                    sp.wait_ge(x_ready, 2 * a + (a == 2) * 2)
                else:
                    sp.wait_ge(gram_mm, NTILE)
                sp.dma_start(qs[SPLIT * KROWS:SROWS, :, :, :].rearrange("r q h n -> r (q h n)"), row_scr[:, :]).then_inc(qs_in, 16)

                def store_queries(i):
                    for c in range(SPLIT):
                        if c == 0:
                            sp.wait_ge(q_act, 2 * a + i + 1)
                        if c == 1:
                            sp.wait_ge(q_split, 2 * a + i + 1)
                        sp.dma_start(q_scr[c, i], qparts[:, c, 512 * i:512 * i + 512]).then_inc(q_out, 16)

                store_queries(0)
                sp.wait_ge(bound_ready, a + 1)
                sp.dma_start(bound_row[0:1, :], bound[32 * a:32 * a + H, 0:1]).then_inc(bound_in, 16)
                sp.wait_ge(q_out, 16 * SPLIT * (2 * a + 1))
                load_queries(sp, 0, 0, qs_in)
                store_queries(1)
                sp.wait_ge(flag_ready, a + 1)
                need_max = sp.value_load(flag[0:1, a:a + 1], min_val=0, max_val=1)
                with sp.If(need_max > 0):
                    sp.wait_ge(qs_in, QS_IN * a + 16 + QUARTER)
                    sp.wait_ge(q_out, 2 * 16 * SPLIT * (a + 1))
                    for q in range(1, NSW):
                        load_queries(sp, q // 2, q % 2, mx_out[a])
                    sp.wait_ge(mx_out[a], QUARTER * (NSW - 1))
                    sp.wait_ge(kr_in[0], 32 * (SWEEPS[4 * a].ring[0] + 1))
                    for hh in range(2):
                        q0 = 4 * hh * (NC + (NT if a == 1 else 0))
                        if hh:
                            sp.wait_ge(mx_ps[a], q0)
                        load_keys(0, 0, hh, mx_in[a])
                        with sp.Fori(1, NC) as c:
                            sp.wait_ge(mx_ps[a], q0 + 4 * c)
                            load_keys(0, c, hh, mx_in[a])
                        for c in range(NC, NC + (NT if a == 1 else 0)):
                            sp.wait_ge(mx_ps[a], q0 + 4 * c)
                            load_keys(0, c, hh, mx_in[a])
                    sp.wait_ge(mx_dve[a], 1)
                    n0 = QUARTER * (NSW - 1)
                    for c in range(SPLIT):
                        sp.dma_start(m_scr[c], mparts[:, c, :]).then_inc(mx_out[a], 16)
                    sp.wait_ge(mx_out[a], n0 + 16 * SPLIT)
                    for q in range(NSW):
                        src = m_scr.rearrange("c (h t) k -> c h (t k)", h=H)[:, q // 2 * (H // 2):(q // 2 + 1) * (H // 2), q % 2 * 512:q % 2 * 512 + 512]
                        sp.dma_start(qs[SPLIT * KROWS:SPLIT * KROWS + SPLIT, q, :, :], src).then_inc(mx_out[a], 16)
                    load_keys(0, 0, 0, mx_out[a])
                    sp.wait_ge(mx_out[a], MAX_OUT)
                sp.end_ifs()

                for s in SWEEPS[4 * a:4 * a + 4]:
                    if s.w % NSW == 0 and ATT[a] == "L1":
                        for b in range(2):
                            sp.wait_ge(k_out[b], KEYS_OUT[b] + 16 * SPLIT)
                    for c in range(TC if s.w % NSW else 0):
                        sp.wait_ge(s_ready, s.pairs + (4 * c - 8 if s.aligned else 0))
                        load_keys(c, c, s.hh, kr_in[c])
                    with sp.Fori(1, NTILE) as i:
                        for b in range(TC):
                            sp.wait_ge(s_ready, i * (4 * TC) + (s.pairs + 4 * b - 8))
                            load_keys(b, i * TC + b, s.hh, kr_in[b])
                    for c in range(NC, s.n):
                        sp.wait_ge(s_ready, s.pairs + 4 * c - 8)
                        load_keys(c % TC, c, s.hh, kr_in[c % TC])
                end = SWEEPS[4 * a + 3]
                sp.wait_ge(s_ready, end.pairs + 4 * end.n)

                def load_values():
                    sp.wait_ge(v_copied, end.chunks + end.n)
                    for b in range(2):
                        sp.wait_ge(v_out[b], 16 * USES[b])
                    sp.dma_start(vs[:, 0:NC, :, :].rearrange("p c h v -> p c (h v)"), v_scr[:, :, a, :]).then_inc(v_in, 16)

                between_sp(sp, a, load_values)
            sp.wait_ge(x_ready, 8)
            sp.dma_start(out[0].rearrange("(n p) d -> p n d", p=P), x[:, :, :]).then_inc(x_out, 16)
            sp.wait_ge(x_out, 16)

        @block.gpsimd
        def _(pool):
            g = nc.gpsimd
            chain = Chain(pool, pool_c)
            chain(g.memset(ident[:, :], 0.0))
            for b in range(UNROLL):
                g.memset(c_in[b][:, :, D:D + 1], 1.0)
            g.memset(bqk[:, :, 1:2], 0.0)
            g.memset(b5[:, 1, :], 0.0)
            g.affine_select(out=ident[:, :], in_=ident[:, :], compare_op=ALU.not_equal, fill=1.0,
                            base=0, pattern=[[-1, P]], channel_multiplier=1).then_inc(ident_ready, 1)
            for b in range(2):
                g.memset(v_next2[b][:, :, :, :, HD:VC].rearrange("p c a h o -> p (c a h) o"), 1.0)
            chain(g.memset(head_of[:, :], 0.0))
            for d in range(HD):
                chain(g.affine_select(out=head_of[:, :], in_=head_of[:, :], compare_op=ALU.not_equal, fill=1.0,
                                      base=-H * d, pattern=[[-1, 32]], channel_multiplier=1))
            g.memset(head_of[:, H:32], 0.0).then_inc(first_const, 1)
            g.memset(vs[:, :, :, HD:VC].rearrange("p c h o -> p (c h) o"), 1.0)
            g.memset(mask_u8[:, :], 0)
            chain(g.memset(c_last[:, :], 0.0))
            g.memset(c_last[0:LAST, D:D + 1], 1.0)
            pool.wait_ge(ident_ready, 1)
            chain(g.tensor_copy(ident_b[:, :], ident[:, :]))
            chain(g.memset(stair[:, :], 0.0))
            chain(g.affine_select(out=stair[:, :], in_=stair[:, :], compare_op=ALU.is_ge, fill=-BIG,
                                  base=0, pattern=[[1, P]], channel_multiplier=-1))
            chain(g.memset(upper[:, :], 0.0))
            chain(g.affine_select(out=upper[:, :], in_=upper[:, :], compare_op=ALU.is_ge, fill=-BIG,
                                  base=0, pattern=[[-1, P]], channel_multiplier=1))
            g.memset(ones_row[:, :], 1.0)
            g.memset(zero_one[:, 0, :], 0.0)
            g.memset(zero_one[:, 1, :], 1.0)
            chain(g.memset(valid[:, :], 1.0))
            chain(g.affine_select(out=valid[:, :], in_=valid[:, :], compare_op=ALU.is_ge, fill=0.0,
                                  base=CTX - 1, pattern=[[-1, P]], channel_multiplier=-P))
            chain(g.memset(valid_last[:, :], 0.0))
            chain(g.memset(valid_last[0:LAST, :], 1.0))
            for b in range(TC):
                g.memset(vr[b][:, :, :], 0.0)
            const_pool(g, chain)
            chain(g.memset(kv_mask[:, :], 1.0))
            kvm = kv_mask[:, :].rearrange("p (h d) -> p h d", h=H)
            chain(g.affine_select(out=kvm, in_=kvm, compare_op=ALU.is_ge, fill=0.0,
                                  base=0, pattern=[[-HD, H], [0, HD]], channel_multiplier=1))
            chain(g.affine_select(out=kvm, in_=kvm, compare_op=ALU.is_ge, fill=0.0,
                                  base=HD - 1, pattern=[[HD, H], [0, HD]], channel_multiplier=-1))
            g.memset(run_max[:, :, :], 0.0).then_inc(const_ready, 1)

            def third_parts(i, r1, p2, p3):
                pool.wait_ge(k_part2, i + 1)
                g.tensor_tensor(p3, r1, p2, ALU.subtract).then_inc(k_part3, 1)

            k_restf = k_rest[:, :, :, :].rearrange("p c a k -> p (c a k)")

            def flat_part(b, c):
                return kparts2[b][:, c].rearrange("p c a k -> p (c a k)")

            def k_step(j, off):
                b = off % 2
                buffer_out(pool, k_out, 16 * SPLIT, j, off)
                third_parts(at(j, off, 1, 0), k_restf, flat_part(b, 1), flat_part(b, 2))

            k_step(None, 0)
            with pool.Fori(0, ROUNDS) as j:
                for off in range(1, UNROLL + 1):
                    k_step(j, off)
            for i in TAIL:
                k_step(None, i)

            for a in range(3):
                if ATT[a] == "L1":
                    for i in range(2):
                        if i == 0:
                            for b in range(2):
                                pool.wait_ge(k_out[b], KEYS_OUT[b])
                        cols = slice(512 * i, 512 * i + 512)
                        third_parts(NTILE + i, k_restf[:, cols], flat_part(0, 1)[:, cols], flat_part(0, 2)[:, cols])
                pool.wait_ge(v_final, a + 1)
                if ATT[a] == "L1":
                    pool.wait_ge(xv_ready, 1)
                for s in SWEEPS[4 * a:4 * a + 4]:
                    h0 = s.hh * (H // 2)

                    def copy_values(b, c):
                        g.tensor_copy(vr[b][:, :, 0:VC], vs[:, bass.ds(c, 1), h0:h0 + H // 2, :].rearrange("p o h v -> p (o h) v")).then_inc(v_copied, 1)

                    for c in range(TC):
                        if s.w:
                            pool.wait_ge(pv_done, s.groups + (2 * c - 4 if s.aligned else 0))
                        copy_values(c, c)
                    with pool.Fori(1, NTILE) as i:
                        for b in range(TC):
                            pool.wait_ge(pv_done, i * (2 * TC) + (s.groups + 2 * b - 4))
                            copy_values(b, i * TC + b)
                    for c in range(NC, s.n):
                        pool.wait_ge(pv_done, s.groups + 2 * c - 4)
                        copy_values(c % TC, c)
                between_pool(pool, a)

        @block.scalar
        def _(act):
            sc = nc.scalar
            chain = Chain(act, act_c)
            for a in (0, 2):
                for i, n in ((1, "bk"), (0, "bq")):
                    src = t[f"{ATT[a]}_xattn_{n}"].rearrange("(h d o) -> d h o", h=H, o=1)
                    act.dma_start(bqk[:, i, a:a + 1], src, allow_slow_non_contiguous=True).then_inc(b_in, 16)
            for i, n in ((0, "L0_xattn_bv"), (2, "L3_xattn_bv"), (3, "L2_xattn_bk"), (4, "L2_xattn_bv")):
                act.dma_start(b5[:, i, :], t[n].partition_broadcast(P)).then_inc(b_in, 16)

            def k_step(j, off, first=False, last=False):
                b = off % 2
                buffer_out(act, k_out, 16 * SPLIT, j, off)
                for a in range(3):
                    act.wait_ge(k_ps, at(j, off, 3, a + 1))
                    if a == 0 and not first:
                        act.wait_ge(kn_ps, at(j, off, 1, 0))
                        if j is not None or off > 1:
                            act.wait_ge(k_r1, at(j, off, 1, -1))
                    keys = PS[:, 1 + a, 0:TW].rearrange("p (c k) -> p c k", c=TC)
                    sc.activation(kf2[b][:, :, a, :], keys, ACT.Identity, bias=bqk[:, 1, a:a + 1])
                    sc.activation(kparts2[b][:, 0, :, a, :], keys, ACT.Identity, bias=bqk[:, 1, a:a + 1])
                    sc.activation(ksq[:, a, :], PS[:, 1 + a, 0:TW], ACT.Square, bias=bqk[:, 1, a:a + 1]).then_inc(k_act, 1)
                    if a == 0 and not last:
                        rows(j, off + 1, first)

            def rows(j, off, first=False):
                act.wait_ge(ct_ps, at(j, off, 1, 1))
                if not first:
                    act.wait_ge(v_ps, at(j, off, TC, -TC))
                sc.activation(c_T[off % 2], PS[:, 0, 0:TW], ACT.Copy).then_inc(ct_ready, 1)

            rows(None, 0, True)
            act.wait_ge(b_in, BIASES_IN)
            act.wait_ge(ident_ready, 1)
            k_step(None, 0, first=True)
            act.wait_ge(const_ready, 1)
            mask = t["mask_Bx1xS2_bf1"][0, 0]
            act.dma_start(mask_u8[0:NC - 1, :], mask[0:(NC - 1) * P].rearrange("(c p) -> c p", p=P)).then_inc(rows_in, 16)
            act.dma_start(mask_u8[NC - 1:NC, 0:LAST], mask[(NC - 1) * P:CTX].unsqueeze(0)).then_inc(rows_in, 16)
            act.dma_start(c_last[0:LAST, 0:D], t["ctx_1024"][0][(NC - 1) * P:CTX, :]).then_inc(rows_in, 16)
            act.dma_start(x[:, :, :], t["x"][0].rearrange("(n p) d -> p n d", p=P)).then_inc(x_in, 16)
            act.dma_start(row_scr[0:SPLIT].rearrange("r (p n) -> p r n", p=P), zero_one[:, 0, :].unsqueeze(1).to_broadcast([P, SPLIT, P])).then_inc(rows_out, 16)
            act.dma_start(row_scr[SPLIT].rearrange("(p n) -> p n", p=P), zero_one[:, 1, :]).then_inc(rows_out, 16)

            def attention_weights():
                for a, l in enumerate(ATT):
                    act.dma_start(wq_in[:, a, :], t[f"{l}_xattn_Wq"][:, :]).then_inc(w_late, 16)
                    act.dma_start(wo[:, a, :], t["L1_xattn_Wout" if a == 1 else f"{l}_xattn_Wo"][:, :]).then_inc(w_late, 16)
                    act.dma_start(bo[0:1, a, :], t["L1_xattn_bout" if a == 1 else f"{l}_xattn_bo"].unsqueeze(0)).then_inc(w_late, 16)
                for i, n in enumerate(("L2_xattn_Wk", "L2_xattn_Wv", "L2_xattn_Wq")):
                    act.dma_start(l2w[:, i, :], t[n][:, :]).then_inc(w_late, 16)
                for i, n in enumerate(("g_xattn", "g_ffn")):
                    act.dma_start(gates_raw[:, 4 * i:4 * i + 4], t[n].partition_broadcast(P)).then_inc(w_late, 16)

            def constant_rows():
                for b in range(TC):
                    act.dma_start(kr[b][SPLIT * KROWS:SROWS - 1, :, :], zero_one[0:SPLIT * H // 2, 1, :]).then_inc(rows_out, 16)
                act.dma_start(ks[NC:NC + NT, 1, KROWS, :, :], zero_one[0:NT, 0, :].unsqueeze(1).to_broadcast([NT, H, P])).then_inc(rows_out, 16)
                act.wait_ge(rows_ready, 1)
                for a in range(3):
                    act.dma_start(ks[0:NC, a, KROWS, :, :], mask_rows[0:NC, a // 2, :].unsqueeze(1).to_broadcast([NC, H, P])).then_inc(rows_out, 16)

            with act.Fori(0, ROUNDS) as j:
                for off in range(1, UNROLL + 1):
                    k_step(j, off)
            for i in TAIL:
                k_step(None, i, last=(i == NTILE - 1))
                if i == TAIL[0]:
                    attention_weights()
                if i == TAIL[1]:
                    constant_rows()
                if i == TAIL[2]:
                    late_weights(act)

            for a in range(3):
                ln_act(act, 2 * a + (a == 2) * 2)
                if ATT[a] == "L1":
                    for i in range(2):
                        act.wait_ge(k_ps, 3 * NTILE + i + 1)
                        if i == 0:
                            for b in range(2):
                                act.wait_ge(k_out[b], KEYS_OUT[b])
                        cols = slice(512 * i, 512 * i + 512)
                        flat = [kf[:, :, :, :].rearrange("p c a k -> p (c a k)")[:, cols], kparts[:, 0].rearrange("p c a k -> p (c a k)")[:, cols],
                                ksq[:, :, :].rearrange("p a k -> p (a k)")[:, cols]]
                        sc.activation(flat[0], PS[:, 4 + i, :], ACT.Copy)
                        sc.activation(flat[1], PS[:, 4 + i, :], ACT.Copy)
                        sc.activation(flat[2], PS[:, 4 + i, :], ACT.Square).then_inc(k_act, 1)
                for i in range(2):
                    cols = slice(512 * i, 512 * i + 512)
                    act.wait_ge(q_ps, 2 * a + i + 1)
                    sc.activation(qf[:, cols], PS[:, 2 + i, :], ACT.Identity, bias=bqk[:, 0, a:a + 1])
                    sc.activation(qparts[:, 0, cols], PS[:, 2 + i, :], ACT.Identity, bias=bqk[:, 0, a:a + 1])
                    sc.activation(qsq[:, cols], PS[:, 2 + i, :], ACT.Square, bias=bqk[:, 0, a:a + 1]).then_inc(q_act, 1)
                if a == 0:
                    act.wait_ge(w_late, WEIGHTS_LATE)
                    sc.activation(gates[:, :], gates_raw[:, :], ACT.Tanh).then_inc(wprep_ready, 1)

                for s in SWEEPS[4 * a:4 * a + 4]:
                    def exps(b, c, first=False, q0=0):
                        for p in range(4):
                            act.wait_ge(s_ready, 4 * c + (s.pairs + p + 1))
                            if not (first and s.w == 0 and c < 1):
                                act.wait_ge(pv_done, 2 * c + (s.groups + p // 2 - 1))
                            slot = (b + p) % 3
                            sc.activation(prob[p][:, :, q0:], PS[:, 2 * slot:2 * slot + 2, q0:], ACT.Exp, scale=SCALE).then_inc(p_ready, 1)

                    for c in range(TC):
                        exps(c, c, True)
                        if c == 0 and s.w % NSW < NSW - 1:
                            after = s.w % NSW + 1
                            if after == 1:
                                act.wait_ge(q_out, 2 * 16 * SPLIT * (a + 1))
                            load_queries(act, after // 2, after % 2, qs_in)
                    with act.Fori(1, NTILE) as i:
                        for b in range(TC):
                            exps(b, i * TC + b)
                    for c in range(NC, s.n):
                        exps(c % TC, c, q0=s.seen(c))
                act.wait_ge(atT_ps, a + 1)
                sc.activation(att_T[:, :], PS[:, 0:2, :].rearrange("p b n -> p (b n)"), ACT.Copy).then_inc(atT_ready, 1)
                between_act(act, a)

        @block.tensor
        def _(pe):
            te = nc.tensor
            pe.wait_ge(ident_ready, 1)

            def rows(j, off, last=False):
                b = off % UNROLL
                if j is None:
                    pe.wait_ge(c_loaded[b], 16 * (off // UNROLL + 1))
                else:
                    pe.wait_ge(c_loaded[b], j * 16 + 16 * (off // UNROLL + 1))
                for c in range(TC):
                    src = c_last[:, 0:D] if last and c == TC - 1 else c_in[b][:, c, 0:D]
                    ins = te.transpose(PS[:, 0, c * P:(c + 1) * P], src, ident[:, :])
                ins.then_inc(ct_ps, 1)

            def norms(j, off, first=False):
                pe.wait_ge(k_act, at(j, off, 3, 3))
                if not first:
                    pe.wait_ge(kn_ev, at(j, off, 1, 0))
                for a in range(3):
                    ins = te.matmul(PS[32 * a:32 * a + 32, 7, 0:TW], head_of[:, :], ksq[:, a, :], start=True, stop=True)
                ins.then_inc(kn_ps, 1)

            def k_step(j, off, first=False, last=False, before_last=False):
                b = off % 2
                pe.wait_ge(ct_ready, at(j, off, 1, 1))
                for a in range(3):
                    if not first:
                        pe.wait_ge(k_act, at(j, off, 3, a - 2))
                    te.matmul(PS[:, 1 + a, 0:TW], wk[:, a, :], c_T[b], start=True, stop=True).then_inc(k_ps, 1)
                if not last:
                    rows(j, off + 1, before_last)
                if first:
                    pe.wait_ge(wv_in, 16 * 3)
                else:
                    norms(j, off - 1)
                for c in range(TC):
                    if not (first and c < 2):
                        pe.wait_ge(v_ev, at(j, off, TC, c - 1))
                    te.matmul(PS[:, 4 + (off + c) % 2, 0:3 * D], c_T[b][:, c * P:(c + 1) * P], wv5[:, 0:3, :].rearrange("p a d -> p (a d)"),
                              start=True, stop=True).then_inc(v_ps, 1)
                for c in range(TC):
                    src = c_last[:, :] if last and c == TC - 1 else c_in[off % UNROLL][:, c, :]
                    ins = te.matmul(PS[:, 6, 0:D + 1], src[:, 0:D], src, start=(first and c == 0), stop=True, skip_group_check=True)
                ins.then_inc(gram_mm, 1)

            rows(None, 0)
            pe.wait_ge(wprep_ready, 1)
            k_step(None, 0, first=True)
            pe.wait_ge(first_const, 1)
            with pe.Fori(0, ROUNDS) as j:
                for off in range(1, UNROLL + 1):
                    k_step(j, off)
            pe.wait_ge(rows_in, ROWS_IN)
            for i in TAIL:
                k_step(None, i, last=(i == NTILE - 1), before_last=(i == NTILE - 2))
            norms(None, NTILE - 1)

            pe.wait_ge(wprep_ready, 2)
            pe.wait_ge(k_act, 3 * NTILE)
            pe.wait_ge(v_ev, NTILE * TC)

            for a in range(3):
                k = 2 * a + (a == 2) * 2
                ln_pe(pe, k)
                if ATT[a] == "L1":
                    for i in range(2):
                        pe.wait_ge(ln_xT, 2 * k + i + 1)
                        te.matmul(PS[:, 4 + i, :], wk[:, a, :], xT[:, 512 * i:512 * i + 512], start=True, stop=True).then_inc(k_ps, 1)
                    for n in range(NT):
                        last = te.matmul(PS[:, 6 + n // 4, n % 4 * P:n % 4 * P + P], xT[:, n * P:(n + 1) * P], wv5[:, 1, :], start=True, stop=True)
                        if n % 4 == 3:
                            last.then_inc(v_ps, 1)
                    for i in range(2):
                        pe.wait_ge(k_act, 3 * NTILE + i + 1)
                        te.matmul(PS[0:32, i, :], head_of[:, :], ksq[:, :, :].rearrange("p a k -> p (a k)")[:, 512 * i:512 * i + 512],
                                  start=True, stop=True).then_inc(kn_ps, 1)
                for i in range(2):
                    pe.wait_ge(ln_xT, 2 * k + i + 1)
                    te.matmul(PS[:, 2 + i, :], wq[:, a, :], xT[:, 512 * i:512 * i + 512], start=True, stop=True).then_inc(q_ps, 1)
                if ATT[a] == "L1":
                    pe.wait_ge(kn_ev, NTILE + 2)
                for i in range(2):
                    pe.wait_ge(q_act, 2 * a + i + 1)
                    last = te.matmul(PS[32 * a:32 * a + 32, 4 + i, :], head_of[:, :], qsq[:, 512 * i:512 * i + 512], start=True, stop=True)
                last.then_inc(qn_ps, 1)
                if a == 0:
                    pe.wait_ge(w_late, WEIGHTS_LATE)
                    for i in range(3):
                        last = te.transpose(PS[:, 2, i * D:(i + 1) * D], l2w[:, i, :], ident[:, :])
                    last.then_inc(wprep_ps, 1)
                    pe.wait_ge(rows_ready, 1)
                    te.transpose(PS[:, 0, 0:64], mask_f[0:64, :], ident[0:64, 0:64]).then_inc(wprep_ps, 1)
                    pe.wait_ge(f_in, SMALL_IN)
                    te.transpose(PS[:, 1, 0:96], rows_w[0:96, :], ident[0:96, 0:96]).then_inc(f_cols_ps, 1)
                    pe.wait_ge(wprep_ready, 5)
                    pe.wait_ge(f_cols, 1)
                    pe.wait_ge(gram_sb, 1)
                    pe.wait_ge(kn_ev, NTILE)
                    te.matmul(PS[:, 7, 0:D], gram[:, 0:D], wv5[:, 4, :], start=True, stop=True).then_inc(gram_ps, 1)
                    pe.wait_ge(gram_sb, 2)
                    te.matmul(PS[:, 6, 0:D], wv5[:, 3, :], gram_v[:, :], start=True, stop=False)
                    te.matmul(PS[:, 6, 0:D], sum_bk[:, :], wv5[:, 4, :], start=False, stop=False)
                    te.matmul(PS[:, 6, 0:D], b5[0:1, 3, :], n_bv[0:1, :], start=False, stop=True).then_inc(gram_ps, 1)
                    pe.wait_ge(gram_sb, 3)

                pe.wait_ge(flag_ready, a + 1)
                need_max = pe.value_load(flag[0:1, a:a + 1], min_val=0, max_val=1)
                with pe.If(need_max > 0):
                    def max_scores(c, hh, q0, first=False, xc=None):
                        pe.wait_ge(mx_in[a], 32 * c + (32 * (q0 // 4) + 32))
                        for r in range(4):
                            if not (first and hh == 0 and r < 2):
                                pe.wait_ge(mx_red[a], 4 * c + (q0 + r - 1))
                            for e in range(2):
                                for n in range(0 if xc is None else xc, NT):
                                    o = PS[:, 4 * (r % 2) + 2 * e + n // 4, n % 4 * P:n % 4 * P + P]
                                    h = 2 * r + e
                                    diag = xc == n
                                    last = te.matmul(o, qs[:, 2 * hh + n // 4, h, n % 4 * P:n % 4 * P + P], kr[0][:, h, :], start=True, stop=not diag)
                                    if diag:
                                        last = te.matmul(o, ident_b[:, :], upper[:, :], start=False, stop=True)
                            last.then_inc(mx_ps[a], 1)

                    nx = NT if a == 1 else 0
                    for hh in range(2):
                        q0 = 4 * hh * (NC + nx)
                        max_scores(0, hh, q0, first=True)
                        with pe.Fori(1, NC) as c:
                            max_scores(c, hh, q0)
                        for xc in range(nx):
                            max_scores(NC + xc, hh, q0, xc=xc)
                    pe.wait_ge(mx_red[a], 8 * (NC + nx))
                    pe.wait_ge(mx_run[a], 8 * (NC + nx) - 8)
                    te.transpose(PS[:, 0, 0:P], run_max[:, :, :].rearrange("p h n -> p (h n)"), ident[:, :]).then_inc(mx_tp[a], 1)
                    pe.wait_ge(mx_out[a], MAX_OUT)
                pe.end_ifs()

                for s in SWEEPS[4 * a:4 * a + 4]:
                    pe.wait_ge(qs_in, QS_IN * a + 16 + QUARTER * (s.w % NSW + 1))
                    if s.w:
                        pe.wait_ge(p_ready, s.pairs)

                    def scores(b, c, j, loads, first=False, xc=None):
                        if j == 0:
                            pe.wait_ge(kr_in[b], loads)
                        if not (first and 4 * c + j < 3):
                            pe.wait_ge(p_ready, 4 * c + (s.pairs + j - 2))
                        for e in range(2):
                            h = 2 * j + e
                            q0 = 0 if xc is None else s.seen(NC + xc)
                            o = PS[:, 2 * ((b + j) % 3) + e, q0:]
                            late = xc is not None and xc >= 4 * s.qh
                            last = te.matmul(o, kr[b][:, h, :], qs[:, 2 * s.hh + s.qh, h, q0:], start=True, stop=not late)
                            if late:
                                last = te.matmul(o[:, 0:P], ident_b[:, :], stair[:, :], start=False, stop=True)
                        last.then_inc(s_ready, 1)

                    def values(b, c, g, first=False, q0=0):
                        if g == 0:
                            pe.wait_ge(v_copied, c + (s.chunks + 1))
                        pe.wait_ge(p_ready, 4 * c + (s.pairs + 2 * g + 2))
                        if first and c == 0 and s.w:
                            pe.wait_ge(acc_ev, s.w)
                        for j in range(4):
                            last = te.matmul(PS[32 * j:32 * j + 32, 6 + g, q0:], vr[b][:, 4 * g + j, :], prob[2 * g + j // 2][:, j % 2, q0:],
                                             start=(first and c == 0), stop=True, skip_group_check=True)
                        last.then_inc(pv_done, 1)

                    for c in range(TC):
                        ld = 32 * (s.ring[c] + 1)
                        scores(c, c, 0, ld, True)
                        scores(c, c, 1, ld, True)
                        if c:
                            values(c - 1, c - 1, 1, True)
                        scores(c, c, 2, ld, True)
                        scores(c, c, 3, ld, True)
                        values(c, c, 0, True)
                    with pe.Fori(1, NTILE) as i:
                        for b in range(TC):
                            c = i * TC + b
                            ld = i * 32 + 32 * (s.ring[b] + 1)
                            scores(b, c, 0, ld)
                            scores(b, c, 1, ld)
                            values((b - 1) % TC, i * TC + (b - 1), 1)
                            scores(b, c, 2, ld)
                            scores(b, c, 3, ld)
                            values(b, c, 0)
                    for c in range(NC, s.n):
                        b = c % TC
                        ld = 32 * (s.ring[b] + c // TC + 1)
                        scores(b, c, 0, ld, xc=c - NC)
                        scores(b, c, 1, ld, xc=c - NC)
                        values((b - 1) % TC, c - 1, 1, q0=s.seen(c - 1))
                        scores(b, c, 2, ld, xc=c - NC)
                        scores(b, c, 3, ld, xc=c - NC)
                        values(b, c, 0, q0=s.seen(c))
                    values((s.n - 1) % TC, s.n - 1, 1, q0=s.seen(s.n - 1))

                pe.wait_ge(acc_ev, NSW * (a + 1))
                for n in range(NT):
                    for g in range(4):
                        last = te.transpose(PS[:, n, g * P:(g + 1) * P], accs[:, g, n * P:(n + 1) * P], ident[:, :])
                    last.then_inc(at_ps, 1)
                for n in range(NT):
                    pe.wait_ge(at_rd, NT * a + max(n + 1, 2))
                    last = te.transpose(PS[:, n // 4, n % 4 * P:n % 4 * P + P], att[:, n, :], ident[:, :])
                last.then_inc(atT_ps, 1)
                pe.wait_ge(atT_ready, a + 1)
                for n in range(NT):
                    o = PS[:, 2 + n // 4, n % 4 * P:n % 4 * P + P]
                    te.matmul(o, att_T[:, n * P:(n + 1) * P], wo[:, a, :], start=True, stop=False)
                    last = te.matmul(o, ones_row[0:1, :], bo[0:1, a, :], start=False, stop=True)
                last.then_inc(y_ps, 1)
                between_pe(pe, a)

        @block.vector
        def _(dve):
            v = nc.vector
            chain = Chain(dve, dve_c)
            dve.wait_ge(w_in, 16 * 3)
            for a in range(3):
                last = v.tensor_copy(wk[:, a, :].rearrange("p (d h) -> p d h", d=HD), dh(wk_in[:, a, :]))
            last.then_inc(wprep_ready, 1)
            dve.wait_ge(b_in, BIASES_IN)
            dve.wait_ge(ident_ready, 1)

            def k_step(j, off, first=False):
                b = off % 2
                buffer_out(dve, v_out, 16, j, off)
                for c in range(TC):
                    dve.wait_ge(v_ps, at(j, off, TC, c + 1))
                    bank = 4 + (off + c) % 2
                    for o, m in ((vs[:, bass.ds(at(j, off, TC, c), 1), :, 0:HD].rearrange("p o h d -> p (o h) d"), slice(0, 1)),
                                 (v_next2[b][:, c, :, :, 0:HD].rearrange("p a h d -> p (a h) d"), slice(1, 3))):
                        last = v.tensor_tensor(o, PS[:, bank, m.start * D:m.stop * D].rearrange("p (m d) -> p m d", d=HD),
                                               b5[:, m, :].rearrange("p a (h d) -> p (a h) d", d=HD), ALU.add)
                    last.then_inc(v_ev, 1)
                if not first:
                    longest(j, off - 1)
                dve.wait_ge(k_act, at(j, off, 3, 3))
                if not first:
                    dve.wait_ge(k_part3, at(j, off, 1, 0))
                v.tensor_tensor(k_rest[:, :, :, :], kf2[b], kparts2[b][:, 0], ALU.subtract).then_inc(k_r1, 1)
                buffer_out(dve, k_out, 16 * SPLIT, j, off)
                dve.wait_ge(k_r1, at(j, off, 1, 1))
                v.tensor_copy(kparts2[b][:, 1], k_rest[:, :, :, :]).then_inc(k_part2, 1)

            def longest(j, off):
                dve.wait_ge(kn_ps, at(j, off, 1, 1))
                v.reduce_max(kmax[0:96, bass.ds(at(j, off, 1, 0), 1)], PS[0:96, 7, 0:TW], X_AXIS).then_inc(kn_ev, 1)

            k_step(None, 0, first=True)
            dve.wait_ge(const_ready, 1)
            dve.wait_ge(rows_in, ROWS_IN)
            chain(v.tensor_copy(mask_f[:, :], mask_u8[:, :]))
            v.tensor_scalar(mask_rows[:, 0, :], valid[:, :], -1.0, BIG, ALU.add, ALU.mult)
            v.tensor_scalar(mask_rows[:, 1, :], mask_f[:, :], -1.0, BIG, ALU.add, ALU.mult).then_inc(rows_ready, 1)
            with dve.Fori(0, ROUNDS) as j:
                for off in range(1, UNROLL + 1):
                    k_step(j, off)
            for i in TAIL:
                if i == TAIL[-1]:
                    dve.wait_ge(x_in, 16)
                    norm_stats(chain, x)
                    dve.wait_ge(w_late, WEIGHTS_LATE)
                    for a in range(3):
                        last = v.tensor_copy(wq[:, a, :].rearrange("p (d h) -> p d h", d=HD), dh(wq_in[:, a, :]))
                    last.then_inc(wprep_ready, 1)
                k_step(None, i)
            longest(None, NTILE - 1)

            for a in range(3):
                k = 2 * a + (a == 2) * 2
                if ATT[a] != "L3":
                    if a:
                        dve.wait_ge(v_in, 16 * a)
                    vl = vs[:, NC - 1, :, :]
                    v.tensor_scalar(vl, vl, valid_last[:, 0:1], None, ALU.mult).then_inc(v_final, 1)
                ln_dve(dve, chain, k)
                if ATT[a] == "L1":
                    for i in range(2):
                        cols = slice(512 * i, 512 * i + 512)
                        f = [w.rearrange("p c a k -> p (c a k)")[:, cols] for w in (kf[:, :, :, :], k_rest[:, :, :, :], kparts[:, 0], kparts[:, 1])]
                        dve.wait_ge(k_act, 3 * NTILE + i + 1)
                        if i == 0:
                            dve.wait_ge(k_part3, NTILE)
                            for b in range(2):
                                dve.wait_ge(k_out[b], KEYS_OUT[b])
                        v.tensor_tensor(f[1], f[0], f[2], ALU.subtract).then_inc(k_r1, 1)
                        dve.wait_ge(k_r1, NTILE + i + 1)
                        v.tensor_copy(f[3], f[1]).then_inc(k_part2, 1)
                    for i in range(2):
                        dve.wait_ge(v_ps, NC + i + 1)
                        last = v.tensor_copy(vs[:, NC + 4 * i:NC + 4 * i + 4, :, 0:HD],
                                             PS[:, 6 + i, :].rearrange("p (c h d) -> p c h d", c=4, h=H))
                    last.then_inc(xv_ready, 1)
                    for i in range(2):
                        dve.wait_ge(kn_ps, NTILE + i + 1)
                        v.reduce_max(kmax[0:32, NTILE + i:NTILE + i + 1], PS[0:32, i, :], X_AXIS).then_inc(kn_ev, 1)
                    dve.wait_ge(kn_ev, NTILE + 2)
                    chain(v.tensor_copy(kmax[32:64, NTILE:NTILE + 2], kmax[0:32, NTILE:NTILE + 2]))
                def split(i):
                    cols = slice(512 * i, 512 * i + 512)
                    dve.wait_ge(q_act, 2 * a + i + 1)
                    chain(v.tensor_tensor(qr1[:, cols], qf[:, cols], qparts[:, 0, cols], ALU.subtract))
                    chain(v.tensor_copy(qparts[:, 1, cols], qr1[:, cols]))
                    v.tensor_tensor(qparts[:, 2, cols], qr1[:, cols], qparts[:, 1, cols], ALU.subtract).then_inc(q_split, 1)

                split(0)
                own = slice(32 * a, 32 * a + 32)
                dve.wait_ge(qn_ps, a + 1)
                dve.wait_ge(kn_ev, NTILE)
                v.reduce_max(q_max[own, :], PS[own, 4:6, :].rearrange("p b n -> p (b n)"), X_AXIS)
                chain(v.reduce_max(k_max[own, :], kmax[own, 0:NTILE + (2 if a == 1 else 0)], X_AXIS))
                v.tensor_tensor(bound[own, :], q_max[own, :], k_max[own, :], ALU.mult).then_inc(bound_ready, 1)
                split(1)
                if a == 0:
                    dve.wait_ge(wprep_ps, 1)
                    v.tensor_copy(wv5[:, 3:5, :].rearrange("p a d -> p (a d)"), PS[:, 2, 0:2 * D])
                    v.tensor_copy(l2wq[:, :], PS[:, 2, 2 * D:3 * D]).then_inc(wprep_ready, 1)
                    dve.wait_ge(wprep_ps, 2)
                    v.tensor_copy(mask_T[:, :], PS[:, 0, 0:64]).then_inc(wprep_ready, 1)
                    dve.wait_ge(f_cols_ps, 1)
                    v.tensor_copy(cols_w[:, :], PS[:, 1, 0:96]).then_inc(f_cols, 1)
                    dve.wait_ge(gram_mm, NTILE)
                    chain(v.tensor_copy(gram[:, :], PS[:, 6, 0:D + 1]))
                    v.tensor_scalar(n_bv[:, :], b5[0:1, 4, :], float(CTX), None, ALU.mult)
                    v.tensor_scalar(sum_bk[:, :], b5[:, 3, :], gram[:, D:D + 1], None, ALU.mult).then_inc(gram_sb, 1)
                    dve.wait_ge(gram_ps, 1)
                    v.scalar_tensor_tensor(gram_v[:, :], b5[:, 4, :], gram[:, D:D + 1], PS[:, 7, 0:D], ALU.mult, ALU.add).then_inc(gram_sb, 1)
                    dve.wait_ge(gram_ps, 2)
                    v.tensor_tensor(kv_sum[:, :], PS[:, 6, 0:D], kv_mask[:, :], ALU.mult).then_inc(gram_sb, 1)
                dve.wait_ge(bound_in, 16 * (a + 1))
                chain(v.reduce_max(bound_max[:, :], bound_row[:, :], X_AXIS))
                v.tensor_scalar(flag[0:1, a:a + 1], bound_max[:, :], (SAFE / SCALE) ** 2, None, ALU.is_ge).then_inc(flag_ready, 1)
                dve.wait_ge(flag_ready, a + 1)
                need_max = dve.value_load(flag[0:1, a:a + 1], min_val=0, max_val=1)
                with dve.If(need_max > 0):
                    def reduce_scores(c, hh, q0, first=False, xc=0):
                        for r in range(4):
                            ps = PS[:, 4 * (r % 2):4 * (r % 2) + 4, :].rearrange("p b (n k) -> p (b n) k", k=P).rearrange("p (e n) k -> p e n k", e=2)[:, :, xc:, :]
                            run = run_max[:, hh * 8 + 2 * r:hh * 8 + 2 * r + 2, xc:]
                            new = new_max[:, :].rearrange("p (e n) -> p e n", e=2)[:, :, xc:]
                            dve.wait_ge(mx_ps[a], 4 * c + (q0 + r + 1))
                            if first:
                                v.reduce_max(run, ps, X_AXIS).then_inc(mx_red[a], 1)
                                dve.wait_ge(mx_red[a], 4 * c + (q0 + r + 1))
                            else:
                                v.reduce_max(new, ps, X_AXIS).then_inc(mx_red[a], 1)
                                dve.wait_ge(mx_red[a], 4 * c + (q0 + r + 1))
                                v.tensor_tensor(run, run, new, ALU.max).then_inc(mx_run[a], 1)
                                dve.wait_ge(mx_run[a], 4 * c + (q0 - 4 * hh - 3 + r))

                    nx = NT if a == 1 else 0
                    for hh in range(2):
                        q0 = 4 * hh * (NC + nx)
                        reduce_scores(0, hh, q0, first=True)
                        with dve.Fori(1, NC) as c:
                            reduce_scores(c, hh, q0)
                        for xc in range(nx):
                            reduce_scores(NC + xc, hh, q0, xc=xc)
                    dve.wait_ge(mx_tp[a], 1)
                    n0 = 8 * (NC + nx) - 8
                    for i, (o, i0, i1) in enumerate(((mneg, None, None), (mparts[:, 0], mneg, None), (mr1, mneg, mparts[:, 0]),
                                                     (mparts[:, 1], mr1, None), (mparts[:, 2], mr1, mparts[:, 1]))):
                        if i == 0:
                            ins = v.tensor_scalar(o[:, :], PS[:, 0, 0:P], -1.0, None, ALU.mult)
                        elif i1 is None:
                            ins = v.tensor_copy(o[:, :], i0[:, :])
                        else:
                            ins = v.tensor_tensor(o[:, :], i0[:, :], i1[:, :], ALU.subtract)
                        if i == 4:
                            ins.then_inc(mx_dve[a], 1)
                        else:
                            ins.then_inc(mx_run[a], 1)
                            dve.wait_ge(mx_run[a], n0 + i + 1)
                dve.end_ifs()

                for s in SWEEPS[4 * a:4 * a + 4]:
                    dve.wait_ge(pv_done, s.groups + 2 * s.n)
                    v.tensor_copy(accs[:, 2 * s.hh:2 * s.hh + 2, 512 * s.qh:512 * s.qh + 512], PS[:, 6:8, :]).then_inc(acc_ev, 1)
                for n in range(NT):
                    dve.wait_ge(at_ps, NT * a + n + 1)
                    heads = PS[:, n, :].rearrange("p (h w) -> p h w", w=32)
                    chain(v.reciprocal(rden[:, n, :].unsqueeze(2), heads[:, :, HD:VC]))
                    v.tensor_tensor(att[:, n, :].rearrange("p (h d) -> p h d", h=H), heads[:, :, 0:HD],
                                    rden[:, n, :].unsqueeze(2).to_broadcast([P, H, HD]), ALU.mult).then_inc(at_rd, 1)
                add_to_x(dve, (0, 1, 3)[a], PS[:, 2:4, :].rearrange("p b n -> p (b n)"), y_ps, a + 1, k)
                between_dve(dve, chain, a)


def kernel(**inputs):
    import numpy as _np
    import concourse.bacc as _bacc
    from concourse import mybir as _mybir
    from concourse.bass_utils import run_bass_kernel_spmd as _run

    nc = _bacc.Bacc("TRN2", target_bir_lowering=False, num_devices=1)
    arrays, t = {}, {}
    for name, value in inputs.items():
        a = _np.ascontiguousarray(value)
        arrays[f"in_{name}"] = a
        t[name] = nc.dram_tensor(f"in_{name}", a.shape, _mybir.dt.from_np(a.dtype), kind="ExternalInput").ap()
    out = nc.dram_tensor("out", (1, S, D), F32, kind="ExternalOutput").ap()
    ks = nc.dram_tensor("key_parts", (NC + NT, 3, KROWS + 1, H, P), BF16, kind="Internal").ap()
    v_scr = nc.dram_tensor("values", (P, NC, 2, H * VC), F32, kind="Internal").ap()
    q_scr = nc.dram_tensor("query_parts", (SPLIT, 2, P, S // 2), BF16, kind="Internal").ap()
    m_scr = nc.dram_tensor("maximum_parts", (SPLIT, P, P), BF16, kind="Internal").ap()
    row_scr = nc.dram_tensor("constant_rows", (SPLIT + 1, H * S), BF16, kind="Internal").ap()
    flamingo_decoder(nc, t, out, ks, v_scr, q_scr, m_scr, row_scr)
    r = _run(nc, [arrays], core_ids=[0])
    return r.results[0]["out"]
```
